# Optimizing a Trainium2 kernel written in Bass

```python
import numpy as np
import jax
import jax.numpy as jnp

def _softmax(x, axis=-1):
    return jax.nn.softmax(x, axis=axis)

def _gelu(x):
    return jax.nn.gelu(x, approximate=True)

def _silu(x):
    return jax.nn.silu(x)

def _sigmoid(x):
    return jax.nn.sigmoid(x)

def _layernorm(x, axis=-1, eps=1e-05):
    m = jnp.mean(x, axis=axis, keepdims=True)
    v = jnp.var(x, axis=axis, keepdims=True)
    return (x - m) / jnp.sqrt(v + eps)

def _scatter_add(tgt, idx, src, axis=0):
    return tgt.at[idx].add(src)

def _segment_sum(src, seg, n):
    return jax.ops.segment_sum(src, seg, n)
kernel_name = 'mk_decoder_preln_d2_seqx_r4_42425d'

def setup_inputs(seed: int=0):
    np.random.seed(seed)
    _w = jnp.asarray

    def _rec_inputs():
        import jax
        import jax.numpy as jnp
        _rk = jax.random.key(seed)
        x = 7.22e-05 + 1 * jax.random.normal(jax.random.fold_in(_rk, 1), (16, 256, 256), jnp.float32)
        _lenS = 256 - jax.random.randint(jax.random.fold_in(_rk, 7), (16,), 0, max(1, 256 // 4) + 1, jnp.int32)
        _lenS2 = 120 - jax.random.randint(jax.random.fold_in(_rk, 8), (16,), 0, max(1, 120 // 4) + 1, jnp.int32)
        _ctx_1024P = jax.random.normal(jax.random.fold_in(_rk, 11), (16, 16, 256), jnp.float32)
        _ctx_1024c = jax.random.dirichlet(jax.random.fold_in(_rk, 511), 0.3 * jnp.ones((16,), jnp.float32), (16, 120))
        _ctx_1024t = jnp.einsum('bsk,bkd->bsd', _ctx_1024c, _ctx_1024P)
        _ctx_1024t = _ctx_1024t * jax.lax.rsqrt(jnp.mean(jnp.square(_ctx_1024t)) + 1e-12) * 0.953939
        ctx_1024 = 4.13588e-05 + 0.999923 * (_ctx_1024t + 0.3 * jax.random.normal(jax.random.fold_in(_rk, 611), (16, 120, 256), jnp.float32))
        _validS = jnp.arange(256)[None, :] < _lenS[:, None]
        _validS2 = jnp.arange(120)[None, :] < _lenS2[:, None]
        _causal = jnp.tril(jnp.ones((256, 256), dtype=bool))
        mask_Bx1xSxS2_bk0 = jnp.logical_not(jnp.broadcast_to(_validS2[:, None, None, :], (16, 1, 256, 120)))
        return (x, ctx_1024, mask_Bx1xSxS2_bk0)
    x, ctx_1024, mask_Bx1xSxS2_bk0 = _rec_inputs()

    def _L0_attn_setup():
        import jax, jax.numpy as jnp
        import numpy as np
        from jax import lax
        H = 256
        E = 2
        INNER = H * E
        N = 16
        K = 4
        R = 64
        B, L = (2, 1024)
        key = jax.random.key(seed)
        ks = jax.random.split(key, 12)
        s = 0.02
        inp = {'hidden': jax.random.normal(ks[0], (B, L, H), dtype=jnp.float32), 'ln_w': jnp.ones((H,), jnp.float32), 'ln_b': jnp.zeros((H,), jnp.float32), 'in_w': jax.random.normal(ks[1], (2 * INNER, H), jnp.float32) * s, 'in_b': jnp.zeros((2 * INNER,), jnp.float32), 'conv_w': jax.random.normal(ks[2], (INNER, 1, K), jnp.float32) * s, 'conv_b': jnp.zeros((INNER,), jnp.float32), 'xp_w': jax.random.normal(ks[3], (R + 2 * N, INNER), jnp.float32) * s, 'dtp_w': jax.random.normal(ks[4], (INNER, R), jnp.float32) * s, 'dtp_b': jax.random.normal(ks[5], (INNER,), jnp.float32) * s, 'A_log': jnp.log(jnp.tile(jnp.arange(1, N + 1, dtype=jnp.float32), (INNER, 1))), 'D': jnp.ones((INNER,), jnp.float32), 'out_w': jax.random.normal(ks[6], (H, INNER), jnp.float32) * s, 'out_b': jnp.zeros((H,), jnp.float32)}
        return inp
    _L0_attn_all = _L0_attn_setup()
    _L0_attn_in = {k: v for k, v in _L0_attn_all.items() if k in ('ln_w', 'ln_b', 'in_w', 'in_b', 'conv_w', 'conv_b', 'xp_w', 'dtp_w', 'dtp_b', 'A_log', 'D', 'out_w', 'out_b')}
    del _L0_attn_all

    def _L0_xattn_setup():
        import jax, jax.numpy as jnp
        import numpy as np
        B, S, E, H = (4, 512, 256, 16)
        D = E // H

        def _split_heads(x):
            b, s, e = x.shape
            return x.reshape(b, s, H, D).transpose(0, 2, 1, 3)
        key = jax.random.key(seed)
        ks = jax.random.split(key, 11)
        std = 1.0 / np.sqrt(E)
        inp = {'query': jax.random.normal(ks[0], (B, S, E), jnp.float32), 'key': jax.random.normal(ks[1], (B, S, E), jnp.float32), 'value': jax.random.normal(ks[2], (B, S, E), jnp.float32), 'mask': jnp.broadcast_to(jnp.tril(jnp.ones((S, S), bool)), (B, 1, S, S)), 'wq': jax.random.normal(ks[3], (E, E), jnp.float32) * std, 'bq': jnp.zeros((E,), jnp.float32), 'wk': jax.random.normal(ks[4], (E, E), jnp.float32) * std, 'bk': jnp.zeros((E,), jnp.float32), 'wv': jax.random.normal(ks[5], (E, E), jnp.float32) * std, 'bv': jnp.zeros((E,), jnp.float32), 'wo': jax.random.normal(ks[6], (E, E), jnp.float32) * std, 'bo': jnp.zeros((E,), jnp.float32)}
        return inp
    _L0_xattn_all = _L0_xattn_setup()
    _L0_xattn_in = {k: v for k, v in _L0_xattn_all.items() if k in ('wq', 'bq', 'wk', 'bk', 'wv', 'bv', 'wo', 'bo')}
    del _L0_xattn_all

    def _L0_ffn_setup():
        import jax, jax.numpy as jnp
        import numpy as np
        EPS = 1e-05

        def layernorm(x, w, b):
            mu = jnp.mean(x, axis=-1, keepdims=True)
            var = jnp.mean(jnp.square(x - mu), axis=-1, keepdims=True)
            return (x - mu) * jax.lax.rsqrt(var + EPS) * w + b

        def act_quant_fake(x):
            scale = 127.0 / jnp.clip(jnp.max(jnp.abs(x), axis=-1, keepdims=True), EPS, None)
            return jnp.clip(jnp.round(x * scale), -128.0, 127.0) / scale

        def weight_quant_fake(w):
            scale = 1.0 / jnp.clip(jnp.mean(jnp.abs(w)), EPS, None)
            return jnp.clip(jnp.round(w * scale), -1.0, 1.0) / scale

        def bitlinear(x, w, b):
            dqx = x + jax.lax.stop_gradient(act_quant_fake(x) - x)
            dqw = w + jax.lax.stop_gradient(weight_quant_fake(w) - w)
            return jnp.einsum('btd,hd->bth', dqx, dqw) + b
        key = jax.random.key(seed)
        ks = jax.random.split(key, 5)
        dim, hidden = (256, 1024)
        B, T = (8, 512)
        return {'x': jax.random.normal(ks[0], (B, T, dim), dtype=jnp.float32), 'ln1_w': jnp.ones((dim,), jnp.float32), 'ln1_b': jnp.zeros((dim,), jnp.float32), 'w1': jax.random.normal(ks[1], (hidden, dim), jnp.float32) * (1.0 / np.sqrt(dim)), 'b1': jax.random.normal(ks[2], (hidden,), jnp.float32) * 0.01, 'ln2_w': jnp.ones((hidden,), jnp.float32), 'ln2_b': jnp.zeros((hidden,), jnp.float32), 'w2': jax.random.normal(ks[3], (dim, hidden), jnp.float32) * (1.0 / np.sqrt(hidden)), 'b2': jax.random.normal(ks[4], (dim,), jnp.float32) * 0.01}
    _L0_ffn_all = _L0_ffn_setup()
    _L0_ffn_in = {k: v for k, v in _L0_ffn_all.items() if k in ('ln1_w', 'ln1_b', 'w1', 'b1', 'ln2_w', 'ln2_b', 'w2', 'b2')}
    del _L0_ffn_all

    def _L1_attn_setup():
        import jax, jax.numpy as jnp
        import numpy as np
        NUM_HEADS = 16

        def _heads(t, B, L, nh, hd):
            return t.reshape(B, L, nh, hd).transpose(0, 2, 1, 3)

        def _attention(q, k, v, bias):
            hd = q.shape[-1]
            scores = jnp.einsum('bhqd,bhkd->bhqk', q, k) / jnp.sqrt(jnp.float32(hd))
            if bias is not None:
                scores = scores + bias[None, None]
            attn = jax.nn.softmax(scores, axis=-1)
            return jnp.einsum('bhqk,bhkd->bhqd', attn, v)
        key = jax.random.key(seed)
        ks = jax.random.split(key, 5)
        B, L, H = (4, 256, 256)
        s = 0.02
        return {'x': jax.random.normal(ks[0], (B, L, H), jnp.float32), 'Wq': jax.random.normal(ks[1], (H, H), jnp.float32) * s, 'Wkv_short': jax.random.normal(ks[2], (H, 2 * H), jnp.float32) * s, 'Wkv_long': jax.random.normal(ks[3], (H, 2 * H), jnp.float32) * s, 'Wo': jax.random.normal(ks[4], (H, H), jnp.float32) * s, 'mix_weight': jnp.float32(0.5), 'decay_factor': jnp.float32(0.95)}
    _L1_attn_all = _L1_attn_setup()
    _L1_attn_in = {k: v for k, v in _L1_attn_all.items() if k in ('Wq', 'Wkv_short', 'Wkv_long', 'Wo', 'mix_weight', 'decay_factor')}
    del _L1_attn_all

    def _L1_xattn_setup():
        import jax, jax.numpy as jnp
        import numpy as np
        HIDDEN = 256
        NUM_HEADS = 16
        HEAD_DIM = HIDDEN // NUM_HEADS
        key = jax.random.key(seed)
        ks = jax.random.split(key, 10)
        B, T, S = (2, 512, 512)
        sc = 1.0 / np.sqrt(HIDDEN)
        inp = {'tgt': jax.random.normal(ks[0], (B, T, HIDDEN), jnp.float32), 'src': jax.random.normal(ks[1], (B, S, HIDDEN), jnp.float32), 'Wq': jax.random.normal(ks[2], (NUM_HEADS, HIDDEN, HEAD_DIM), jnp.float32) * sc, 'bq': jnp.zeros((NUM_HEADS, HEAD_DIM), jnp.float32), 'Wk': jax.random.normal(ks[3], (NUM_HEADS, HIDDEN, HEAD_DIM), jnp.float32) * sc, 'bk': jnp.zeros((NUM_HEADS, HEAD_DIM), jnp.float32), 'Wv': jax.random.normal(ks[4], (NUM_HEADS, HIDDEN, HEAD_DIM), jnp.float32) * sc, 'bv': jnp.zeros((NUM_HEADS, HEAD_DIM), jnp.float32), 'Wo': jax.random.normal(ks[5], (HIDDEN, HIDDEN), jnp.float32) * sc, 'bo': jnp.zeros((HIDDEN,), jnp.float32)}
        return inp
    _L1_xattn_all = _L1_xattn_setup()
    _L1_xattn_in = {k: v for k, v in _L1_xattn_all.items() if k in ('Wq', 'bq', 'Wk', 'bk', 'Wv', 'bv', 'Wo', 'bo')}
    del _L1_xattn_all

    def _L1_ffn_setup():
        import jax, jax.numpy as jnp
        import numpy as np
        D = 256
        H = 4
        DF = 1024
        E = 8
        EPS = 1e-05

        def _layer_norm(x, g, b):
            mu = jnp.mean(x, axis=-1, keepdims=True)
            var = jnp.mean(jnp.square(x - mu), axis=-1, keepdims=True)
            return (x - mu) * jax.lax.rsqrt(var + EPS) * g + b

        def _mha(x, Wqkv, bqkv, Wo, bo):
            S, B, _ = x.shape
            hd = D // H
            qkv = x @ Wqkv.T + bqkv
            q, k, v = jnp.split(qkv, 3, axis=-1)
            to_heads = lambda t: t.reshape(S, B, H, hd).transpose(1, 2, 0, 3)
            q, k, v = (to_heads(q), to_heads(k), to_heads(v))
            scores = jnp.einsum('bhqd,bhkd->bhqk', q, k) * (1.0 / np.sqrt(hd))
            att = jax.nn.softmax(scores, axis=-1)
            o = jnp.einsum('bhqk,bhkd->bhqd', att, v)
            o = o.transpose(2, 0, 1, 3).reshape(S, B, D)
            return o @ Wo.T + bo

        def _moe(x, Wg, W1, b1, W2, b2):
            S, B, _ = x.shape
            xf = x.reshape(S * B, D)
            logits = xf @ Wg.T
            idx = jnp.argmax(logits, axis=-1)
            out = jnp.zeros_like(xf)
            for e in range(E):
                m = (idx == e)[:, None].astype(xf.dtype)
                h = jax.nn.relu(xf @ W1[e] + b1[e])
                out = out + m * (h @ W2[e] + b2[e])
            return out.reshape(S, B, D)
        key = jax.random.key(seed)
        ks = jax.random.split(key, 16)
        S, B = (128, 8)
        s = lambda k, shape, fan: jax.random.normal(k, shape, jnp.float32) * (1.0 / np.sqrt(fan))
        return {'x': jax.random.normal(ks[0], (S, B, D), jnp.float32), 'Wqkv': s(ks[1], (3 * D, D), D), 'bqkv': jnp.zeros((3 * D,), jnp.float32), 'Wo': s(ks[2], (D, D), D), 'bo': jnp.zeros((D,), jnp.float32), 'g1': jnp.ones((D,), jnp.float32), 'be1': jnp.zeros((D,), jnp.float32), 'g2': jnp.ones((D,), jnp.float32), 'be2': jnp.zeros((D,), jnp.float32), 'Wg': s(ks[3], (E, D), D), 'W1': s(ks[4], (E, D, DF), D), 'b1': jnp.zeros((E, DF), jnp.float32), 'W2': s(ks[5], (E, DF, D), DF), 'b2': jnp.zeros((E, D), jnp.float32)}
    _L1_ffn_all = _L1_ffn_setup()
    _L1_ffn_in = {k: v for k, v in _L1_ffn_all.items() if k in ('Wqkv', 'bqkv', 'Wo', 'bo', 'g1', 'be1', 'g2', 'be2', 'Wg', 'W1', 'b1', 'W2', 'b2')}
    del _L1_ffn_all
    return {'x': x, 'ctx_1024': ctx_1024, 'mask_Bx1xSxS2_bk0': mask_Bx1xSxS2_bk0, 'L0_attn_ln_w': _L0_attn_in['ln_w'], 'L0_attn_ln_b': _L0_attn_in['ln_b'], 'L0_attn_in_w': _L0_attn_in['in_w'], 'L0_attn_in_b': _L0_attn_in['in_b'], 'L0_attn_conv_w': _L0_attn_in['conv_w'], 'L0_attn_conv_b': _L0_attn_in['conv_b'], 'L0_attn_xp_w': _L0_attn_in['xp_w'], 'L0_attn_dtp_w': _L0_attn_in['dtp_w'], 'L0_attn_dtp_b': _L0_attn_in['dtp_b'], 'L0_attn_A_log': _L0_attn_in['A_log'], 'L0_attn_D': _L0_attn_in['D'], 'L0_attn_out_w': _L0_attn_in['out_w'], 'L0_attn_out_b': _L0_attn_in['out_b'], 'L0_xattn_wq': _L0_xattn_in['wq'], 'L0_xattn_bq': _L0_xattn_in['bq'], 'L0_xattn_wk': _L0_xattn_in['wk'], 'L0_xattn_bk': _L0_xattn_in['bk'], 'L0_xattn_wv': _L0_xattn_in['wv'], 'L0_xattn_bv': _L0_xattn_in['bv'], 'L0_xattn_wo': _L0_xattn_in['wo'], 'L0_xattn_bo': _L0_xattn_in['bo'], 'L0_ffn_ln1_w': _L0_ffn_in['ln1_w'], 'L0_ffn_ln1_b': _L0_ffn_in['ln1_b'], 'L0_ffn_w1': _L0_ffn_in['w1'], 'L0_ffn_b1': _L0_ffn_in['b1'], 'L0_ffn_ln2_w': _L0_ffn_in['ln2_w'], 'L0_ffn_ln2_b': _L0_ffn_in['ln2_b'], 'L0_ffn_w2': _L0_ffn_in['w2'], 'L0_ffn_b2': _L0_ffn_in['b2'], 'L1_attn_Wq': _L1_attn_in['Wq'], 'L1_attn_Wkv_short': _L1_attn_in['Wkv_short'], 'L1_attn_Wkv_long': _L1_attn_in['Wkv_long'], 'L1_attn_Wo': _L1_attn_in['Wo'], 'L1_attn_mix_weight': _L1_attn_in['mix_weight'], 'L1_attn_decay_factor': _L1_attn_in['decay_factor'], 'L1_xattn_Wq': _L1_xattn_in['Wq'], 'L1_xattn_bq': _L1_xattn_in['bq'], 'L1_xattn_Wk': _L1_xattn_in['Wk'], 'L1_xattn_bk': _L1_xattn_in['bk'], 'L1_xattn_Wv': _L1_xattn_in['Wv'], 'L1_xattn_bv': _L1_xattn_in['bv'], 'L1_xattn_Wo': _L1_xattn_in['Wo'], 'L1_xattn_bo': _L1_xattn_in['bo'], 'L1_ffn_Wqkv': _L1_ffn_in['Wqkv'], 'L1_ffn_bqkv': _L1_ffn_in['bqkv'], 'L1_ffn_Wo': _L1_ffn_in['Wo'], 'L1_ffn_bo': _L1_ffn_in['bo'], 'L1_ffn_g1': _L1_ffn_in['g1'], 'L1_ffn_be1': _L1_ffn_in['be1'], 'L1_ffn_g2': _L1_ffn_in['g2'], 'L1_ffn_be2': _L1_ffn_in['be2'], 'L1_ffn_Wg': _L1_ffn_in['Wg'], 'L1_ffn_W1': _L1_ffn_in['W1'], 'L1_ffn_b1': _L1_ffn_in['b1'], 'L1_ffn_W2': _L1_ffn_in['W2'], 'L1_ffn_b2': _L1_ffn_in['b2']}

def reference(x, ctx_1024, mask_Bx1xSxS2_bk0, L0_attn_ln_w, L0_attn_ln_b, L0_attn_in_w, L0_attn_in_b, L0_attn_conv_w, L0_attn_conv_b, L0_attn_xp_w, L0_attn_dtp_w, L0_attn_dtp_b, L0_attn_A_log, L0_attn_D, L0_attn_out_w, L0_attn_out_b, L0_xattn_wq, L0_xattn_bq, L0_xattn_wk, L0_xattn_bk, L0_xattn_wv, L0_xattn_bv, L0_xattn_wo, L0_xattn_bo, L0_ffn_ln1_w, L0_ffn_ln1_b, L0_ffn_w1, L0_ffn_b1, L0_ffn_ln2_w, L0_ffn_ln2_b, L0_ffn_w2, L0_ffn_b2, L1_attn_Wq, L1_attn_Wkv_short, L1_attn_Wkv_long, L1_attn_Wo, L1_attn_mix_weight, L1_attn_decay_factor, L1_xattn_Wq, L1_xattn_bq, L1_xattn_Wk, L1_xattn_bk, L1_xattn_Wv, L1_xattn_bv, L1_xattn_Wo, L1_xattn_bo, L1_ffn_Wqkv, L1_ffn_bqkv, L1_ffn_Wo, L1_ffn_bo, L1_ffn_g1, L1_ffn_be1, L1_ffn_g2, L1_ffn_be2, L1_ffn_Wg, L1_ffn_W1, L1_ffn_b1, L1_ffn_W2, L1_ffn_b2):
    import jax
    import jax.numpy as jnp

    def _L0_attn_ref(hidden, ln_w, ln_b, in_w, in_b, conv_w, conv_b, xp_w, dtp_w, dtp_b, A_log, D, out_w, out_b):
        import jax, jax.numpy as jnp
        import numpy as np
        from jax import lax
        H = 256
        E = 2
        INNER = H * E
        N = 16
        K = 4
        R = 64
        B, L = (2, 1024)
        b_, l_, h_ = hidden.shape
        inner = conv_w.shape[0]
        n = A_log.shape[1]
        r = dtp_w.shape[1]
        k = conv_w.shape[2]
        mu = jnp.mean(hidden, axis=-1, keepdims=True)
        var = jnp.mean((hidden - mu) ** 2, axis=-1, keepdims=True)
        hn = (hidden - mu) / jnp.sqrt(var + 1e-05) * ln_w + ln_b
        proj = hn @ in_w.T + in_b
        x, gate = (proj[..., :inner], proj[..., inner:])
        xc = x.transpose(0, 2, 1)
        xc = lax.conv_general_dilated(xc, conv_w, window_strides=(1,), padding=[(k - 1, 0)], dimension_numbers=('NCH', 'OIH', 'NCH'), feature_group_count=inner) + conv_b[None, :, None]
        x = jax.nn.silu(xc.transpose(0, 2, 1))
        params = x @ xp_w.T
        dt_raw = params[..., :r]
        b_mat = params[..., r:r + n]
        c_mat = params[..., r + n:]
        dt = jax.nn.softplus(dt_raw @ dtp_w.T + dtp_b)
        a = -jnp.exp(A_log)

        def step(state, ins):
            dt_t, x_t, b_t, c_t = ins
            decay = jnp.exp(dt_t[..., None] * a)
            state = decay * state + (dt_t * x_t)[..., None] * b_t[:, None, :]
            y_t = jnp.einsum('bdn,bn->bd', state, c_t) + D * x_t
            return (state, y_t)
        state0 = jnp.zeros((b_, inner, n), dtype=x.dtype)
        xs = (dt.transpose(1, 0, 2), x.transpose(1, 0, 2), b_mat.transpose(1, 0, 2), c_mat.transpose(1, 0, 2))
        _, ys = lax.scan(step, state0, xs)
        y = ys.transpose(1, 0, 2) * jax.nn.silu(gate)
        return hidden + y @ out_w.T + out_b

    def _L0_xattn_ref(query, key, value, mask, wq, bq, wk, bk, wv, bv, wo, bo):
        import jax, jax.numpy as jnp
        import numpy as np
        B, S, E, H = (4, 512, 256, 16)
        D = E // H

        def _split_heads(x):
            b, s, e = x.shape
            return x.reshape(b, s, H, D).transpose(0, 2, 1, 3)
        q = _split_heads(query @ wq + bq)
        k = _split_heads(key @ wk + bk)
        v = _split_heads(value @ wv + bv)
        score = jnp.einsum('bhqd,bhkd->bhqk', q, k)
        score = jnp.where(mask, score, -jnp.inf)
        attn = jax.nn.softmax(score / jnp.sqrt(jnp.float32(D)), axis=-1)
        out = jnp.einsum('bhqk,bhkd->bhqd', attn, v)
        out = out.transpose(0, 2, 1, 3).reshape(query.shape[0], query.shape[1], H * D)
        return out @ wo + bo

    def _L0_ffn_ref(x, ln1_w, ln1_b, w1, b1, ln2_w, ln2_b, w2, b2):
        import jax, jax.numpy as jnp
        import numpy as np
        EPS = 1e-05

        def layernorm(x, w, b):
            mu = jnp.mean(x, axis=-1, keepdims=True)
            var = jnp.mean(jnp.square(x - mu), axis=-1, keepdims=True)
            return (x - mu) * jax.lax.rsqrt(var + EPS) * w + b

        def act_quant_fake(x):
            scale = 127.0 / jnp.clip(jnp.max(jnp.abs(x), axis=-1, keepdims=True), EPS, None)
            return jnp.clip(jnp.round(x * scale), -128.0, 127.0) / scale

        def weight_quant_fake(w):
            scale = 1.0 / jnp.clip(jnp.mean(jnp.abs(w)), EPS, None)
            return jnp.clip(jnp.round(w * scale), -1.0, 1.0) / scale

        def bitlinear(x, w, b):
            dqx = x + jax.lax.stop_gradient(act_quant_fake(x) - x)
            dqw = w + jax.lax.stop_gradient(weight_quant_fake(w) - w)
            return jnp.einsum('btd,hd->bth', dqx, dqw) + b
        h = layernorm(x, ln1_w, ln1_b)
        h = bitlinear(h, w1, b1)
        h = jax.nn.gelu(h, approximate=False)
        h = layernorm(h, ln2_w, ln2_b)
        out = bitlinear(h, w2, b2)
        return out

    def _L1_attn_ref(x, Wq, Wkv_short, Wkv_long, Wo, mix_weight, decay_factor):
        import jax, jax.numpy as jnp
        import numpy as np
        NUM_HEADS = 16

        def _heads(t, B, L, nh, hd):
            return t.reshape(B, L, nh, hd).transpose(0, 2, 1, 3)

        def _attention(q, k, v, bias):
            hd = q.shape[-1]
            scores = jnp.einsum('bhqd,bhkd->bhqk', q, k) / jnp.sqrt(jnp.float32(hd))
            if bias is not None:
                scores = scores + bias[None, None]
            attn = jax.nn.softmax(scores, axis=-1)
            return jnp.einsum('bhqk,bhkd->bhqd', attn, v)
        B, L, H = x.shape
        nh = NUM_HEADS
        hd = H // nh
        q = _heads(x @ Wq, B, L, nh, hd)
        kv_s = x @ Wkv_short
        k_s = _heads(kv_s[..., :H], B, L, nh, hd)
        v_s = _heads(kv_s[..., H:], B, L, nh, hd)
        pos = jnp.arange(L, dtype=jnp.float32)
        decay_bias = -jnp.abs(pos[None, :] - pos[:, None]) * (1.0 - decay_factor)
        out_short = _attention(q, k_s, v_s, decay_bias)
        kv_l = x @ Wkv_long
        k_l = _heads(kv_l[..., :H], B, L, nh, hd)
        v_l = _heads(kv_l[..., H:], B, L, nh, hd)
        out_long = _attention(q, k_l, v_l, None)
        alpha = jax.nn.sigmoid(mix_weight)
        out = alpha * out_short + (1.0 - alpha) * out_long
        out = out.transpose(0, 2, 1, 3).reshape(B, L, H)
        return out @ Wo

    def _L1_xattn_ref(tgt, src, Wq, bq, Wk, bk, Wv, bv, Wo, bo):
        import jax, jax.numpy as jnp
        import numpy as np
        HIDDEN = 256
        NUM_HEADS = 16
        HEAD_DIM = HIDDEN // NUM_HEADS
        q = jnp.einsum('btd,hdk->bhtk', tgt, Wq) + bq[None, :, None, :]
        k = jnp.einsum('bsd,hdk->bhsk', src, Wk) + bk[None, :, None, :]
        v = jnp.einsum('bsd,hdk->bhsk', src, Wv) + bv[None, :, None, :]
        scale = 1.0 / jnp.sqrt(jnp.asarray(HEAD_DIM, q.dtype))
        scores = jnp.einsum('bhtk,bhsk->bhts', q, k) * scale
        weights = jax.nn.softmax(scores, axis=-1)
        out = jnp.einsum('bhts,bhsk->bhtk', weights, v)
        B, H, T, Dh = out.shape
        h = out.transpose(0, 2, 1, 3).reshape(B, T, H * Dh)
        return h @ Wo + bo

    def _L1_ffn_ref(x, Wqkv, bqkv, Wo, bo, g1, be1, g2, be2, Wg, W1, b1, W2, b2):
        import jax, jax.numpy as jnp
        import numpy as np
        D = 256
        H = 4
        DF = 1024
        E = 8
        EPS = 1e-05

        def _layer_norm(x, g, b):
            mu = jnp.mean(x, axis=-1, keepdims=True)
            var = jnp.mean(jnp.square(x - mu), axis=-1, keepdims=True)
            return (x - mu) * jax.lax.rsqrt(var + EPS) * g + b

        def _mha(x, Wqkv, bqkv, Wo, bo):
            S, B, _ = x.shape
            hd = D // H
            qkv = x @ Wqkv.T + bqkv
            q, k, v = jnp.split(qkv, 3, axis=-1)
            to_heads = lambda t: t.reshape(S, B, H, hd).transpose(1, 2, 0, 3)
            q, k, v = (to_heads(q), to_heads(k), to_heads(v))
            scores = jnp.einsum('bhqd,bhkd->bhqk', q, k) * (1.0 / np.sqrt(hd))
            att = jax.nn.softmax(scores, axis=-1)
            o = jnp.einsum('bhqk,bhkd->bhqd', att, v)
            o = o.transpose(2, 0, 1, 3).reshape(S, B, D)
            return o @ Wo.T + bo

        def _moe(x, Wg, W1, b1, W2, b2):
            S, B, _ = x.shape
            xf = x.reshape(S * B, D)
            logits = xf @ Wg.T
            idx = jnp.argmax(logits, axis=-1)
            out = jnp.zeros_like(xf)
            for e in range(E):
                m = (idx == e)[:, None].astype(xf.dtype)
                h = jax.nn.relu(xf @ W1[e] + b1[e])
                out = out + m * (h @ W2[e] + b2[e])
            return out.reshape(S, B, D)
        y = _layer_norm(x + _mha(x, Wqkv, bqkv, Wo, bo), g1, be1)
        z = _layer_norm(y + _moe(y, Wg, W1, b1, W2, b2), g2, be2)
        return z
    x = x + _L0_attn_ref(_layernorm(x, axis=-1), L0_attn_ln_w, L0_attn_ln_b, L0_attn_in_w, L0_attn_in_b, L0_attn_conv_w, L0_attn_conv_b, L0_attn_xp_w, L0_attn_dtp_w, L0_attn_dtp_b, L0_attn_A_log, L0_attn_D, L0_attn_out_w, L0_attn_out_b)
    x = x + _L0_xattn_ref(_layernorm(x, axis=-1), ctx_1024, ctx_1024, mask_Bx1xSxS2_bk0, L0_xattn_wq, L0_xattn_bq, L0_xattn_wk, L0_xattn_bk, L0_xattn_wv, L0_xattn_bv, L0_xattn_wo, L0_xattn_bo)
    x = x + _L0_ffn_ref(_layernorm(x, axis=-1), L0_ffn_ln1_w, L0_ffn_ln1_b, L0_ffn_w1, L0_ffn_b1, L0_ffn_ln2_w, L0_ffn_ln2_b, L0_ffn_w2, L0_ffn_b2)
    x = x + _L1_attn_ref(_layernorm(x, axis=-1), L1_attn_Wq, L1_attn_Wkv_short, L1_attn_Wkv_long, L1_attn_Wo, L1_attn_mix_weight, L1_attn_decay_factor)
    x = x + _L1_xattn_ref(_layernorm(x, axis=-1), ctx_1024, L1_xattn_Wq, L1_xattn_bq, L1_xattn_Wk, L1_xattn_bk, L1_xattn_Wv, L1_xattn_bv, L1_xattn_Wo, L1_xattn_bo)
    x = x + _L1_ffn_ref(_layernorm(x, axis=-1), L1_ffn_Wqkv, L1_ffn_bqkv, L1_ffn_Wo, L1_ffn_bo, L1_ffn_g1, L1_ffn_be1, L1_ffn_g2, L1_ffn_be2, L1_ffn_Wg, L1_ffn_W1, L1_ffn_b1, L1_ffn_W2, L1_ffn_b2)
    return x

_drawn_inputs = setup_inputs


def setup_inputs(seed=0):
    import zlib

    import numpy as np

    out = dict(_drawn_inputs(seed))
    spreads = {'L0_attn_ln_w': (1.0, 0.6),
     'L0_attn_ln_b': (0.0, 0.497),
     'L0_attn_in_b': (0.0, 0.469),
     'L0_attn_conv_b': (0.0, 0.466),
     'L0_attn_D': (1.0, 0.6),
     'L0_attn_out_b': (0.0, 0.397),
     'L0_xattn_bq': (0.0, 0.8),
     'L0_xattn_bk': (0.0, 2.0),
     'L0_xattn_bv': (0.0, 0.367),
     'L0_xattn_bo': (0.0, 0.335),
     'L0_ffn_ln1_w': (1.0, 0.6),
     'L0_ffn_ln1_b': (0.0, 0.458),
     'L0_ffn_ln2_w': (1.0, 0.6),
     'L0_ffn_ln2_b': (0.0, 0.515),
     'L1_xattn_bq': (0.0, 1.531),
     'L1_xattn_bk': (0.0, 2.0),
     'L1_xattn_bv': (0.0, 0.379),
     'L1_xattn_bo': (0.0, 0.407),
     'L1_ffn_bqkv': (0.0, 0.1),
     'L1_ffn_bo': (0.0, 0.1),
     'L1_ffn_g1': (1.0, 0.2),
     'L1_ffn_be1': (0.0, 0.1),
     'L1_ffn_g2': (1.0, 0.566),
     'L1_ffn_be2': (0.0, 0.684),
     'L1_ffn_b1': (0.0, 1.207),
     'L1_ffn_b2': (0.0, 0.304)}
    factors = {'L0_attn_in_w': 3.745,
     'L0_attn_conv_w': 4.61,
     'L0_attn_xp_w': 8.0,
     'L0_attn_dtp_w': 8.0,
     'L0_attn_dtp_b': 8.0,
     'L0_attn_A_log': 8.0,
     'L0_attn_out_w': 3.478,
     'L0_ffn_b1': 18.606,
     'L0_ffn_b2': 22.328,
     'L1_attn_Wq': 28.716,
     'L1_attn_Wkv_short': 9.115,
     'L1_attn_Wkv_long': 13.401}
    for name, (base, spread) in spreads.items():
        noise = np.random.default_rng([zlib.crc32(name.encode()), seed]).standard_normal(out[name].shape)
        drawn = base * np.exp(spread * noise) if base else spread * noise
        out[name] = jnp.asarray(drawn.astype(out[name].dtype))
    for name, factor in factors.items():
        out[name] = (out[name] * factor).astype(out[name].dtype)
    return out
```

```python
from contextlib import ExitStack

import concourse.bass as bass
from concourse import mybir

F32 = mybir.dt.float32
BF16 = mybir.dt.bfloat16
I32 = mybir.dt.int32
U8 = mybir.dt.uint8
ALU = mybir.AluOpType
ACT = mybir.ActivationFunctionType
AX = mybir.AxisListType

P = 128
D = 256
DC = D // P
B, S = 16, 256
NT = B * S // P
EPS = 1e-5
SLOTS = NT + 8


class Stage:

    def __init__(self, nc, name):
        self.nc, self.name, self.ctx, self.sems = nc, name, ExitStack(), []

    def __enter__(self):
        self.ctx.__enter__()
        return self

    def __exit__(self, *a):
        done = self.ctx.__exit__(*a)
        if a[0] is None:
            nums = sorted(s.num for s in self.sems)
            for lo in (n for n in nums if n - 1 not in nums):
                hi = lo
                while hi in nums:
                    hi += 1
                self.nc.all_engine_barrier(sems_to_clear=range(lo, hi))
        return done

    def sb(self, name, shape, dt=F32):
        return self.ctx.enter_context(self.nc.sbuf_tensor(f"{self.name}_{name}", shape, dt))

    def ps(self, name, shape, dt=F32):
        return self.ctx.enter_context(self.nc.psum_tensor(f"{self.name}_ps_{name}", shape, dt))

    def sem(self, name):
        s = self.ctx.enter_context(self.nc.semaphore(f"{self.name}_{name}"))
        self.sems.append(s)
        return s

    def block(self):
        return self.ctx.enter_context(self.nc.Block())


class Chain:

    def __init__(self, eng, sem, per=0, base=0):
        self.eng, self.sem, self.per, self.n, self.i, self.base = eng, sem, per, 0, None, base

    def start(self, i):
        self.i, self.n = i, 0

    def mark(self, ins):
        self.n += 1
        ins.then_inc(self.sem, 1)

    def link(self, ins):
        self.mark(ins)
        at = self.n + self.base
        self.eng.wait_ge(self.sem, at if self.i is None else self.i * self.per + at)

    def stop(self):
        assert self.i is None or self.n == self.per, (self.n, self.per)


def layer_norm_stats(nc, dve, ch, src, tiles, stats, mv, veps, var_ready, nth, pad):
    for t in range(tiles):
        (ch.mark if t < tiles - 1 else ch.link)(nc.vector.bn_stats(stats[:, t, :], src[:, t, :]))
    nc.vector.memset(pad[:, :], 0.0)
    for t in range(tiles):
        (ch.mark if t < tiles - 1 else ch.link)(nc.vector.bn_aggr(mv[:, t, :], stats[:, t, :]))
    nc.vector.tensor_scalar(veps[:, 0:tiles], mv[:, 0:tiles, 1], EPS, None, ALU.add).then_inc(var_ready, 1)
    dve.wait_ge(var_ready, nth)


def rsqrt_guess(nc, act, veps, tiles, logv, guess, var_ready, log_ready, guess_ready, nth):
    act.wait_ge(var_ready, nth)
    nc.scalar.activation(logv[:, 0:tiles], veps[:, 0:tiles], ACT.Ln).then_inc(log_ready, 1)
    act.wait_ge(log_ready, nth)
    nc.scalar.activation(guess[:, 0:tiles], logv[:, 0:tiles], ACT.Exp, scale=-0.5).then_inc(guess_ready, 1)


def rsqrt_refine(nc, dve, link, veps, tiles, guess, tmp, rstd, guess_ready, nth):
    dve.wait_ge(guess_ready, nth)
    link(nc.vector.tensor_tensor(tmp[:, 0:tiles], guess[:, 0:tiles], guess[:, 0:tiles], ALU.mult))
    link(nc.vector.scalar_tensor_tensor(out=tmp[:, 0:tiles], in0=tmp[:, 0:tiles], scalar=-0.5,
                                        in1=veps[:, 0:tiles], op0=ALU.mult, op1=ALU.mult))
    link(nc.vector.scalar_tensor_tensor(out=rstd[:, 0:tiles], in0=tmp[:, 0:tiles], scalar=1.5,
                                        in1=guess[:, 0:tiles], op0=ALU.add, op1=ALU.mult))


def normalize(nc, link, src, dst, tiles, mv, rstd):
    for t in range(tiles):
        link(nc.vector.tensor_scalar(dst[:, t, :], src[:, t, :], mv[:, t, 0:1], rstd[:, t:t + 1],
                                     ALU.subtract, ALU.mult))


def whole(t):
    return t[tuple(slice(None) for _ in t.shape)]


def setup(nc, A, X, ident, identb):
    with Stage(nc, "setup") as st:
        x_loaded, zeroed, made = st.sem("x_loaded"), st.sem("zeroed"), st.sem("made")
        block = st.block()

        @block.sync
        def _(sp):
            sp.dma_start(X[:, :, :], A["x"].rearrange("(n p) d -> p n d", p=P)).then_inc(x_loaded, 16)
            sp.wait_ge(x_loaded, 16)

        @block.gpsimd
        def _(pool):
            nc.gpsimd.memset(ident[:, :], 0.0).then_inc(zeroed, 1)
            nc.gpsimd.memset(identb[:, :], 0.0).then_inc(zeroed, 1)
            pool.wait_ge(zeroed, 2)
            for m in (ident, identb):
                nc.gpsimd.affine_select(out=m[:, :], in_=m[:, :], compare_op=ALU.not_equal, fill=1.0,
                                        base=0, pattern=[[-1, P]], channel_multiplier=1).then_inc(made, 1)
            pool.wait_ge(made, 2)


def mamba(nc, A, X, ident, identb):
    TT = 4
    N = TT * P
    ITER = NT // TT
    BB = N // S
    R, NS = 64, 16
    INNER = 512
    MC = INNER // P
    K = 4
    PAIR = 2
    PAIRS = NS // PAIR
    def spread_row(n):
        q, r = n // 4, n % 4
        return 2 * q + r if r < 2 else NS + 2 * q + r - 2

    RESET = 1.0e20
    with Stage(nc, "mamba") as st:
        sb, ps, sem = st.sb, st.ps, st.sem
        in_w = sb("in_w", [P, DC, 2 * INNER])
        out_w = sb("out_w", [P, MC, D])
        xp_dt = sb("xp_dt", [P, MC, R])
        xp_bc = sb("xp_bc", [P, MC, 96])
        dtp_w = sb("dtp_w", [R, INNER])
        ln_w, ln_b = sb("ln_w", [P, DC]), sb("ln_b", [P, DC])
        in_b = sb("in_b", [P, 2 * MC])
        conv_w, conv_b = sb("conv_w", [P, MC, K]), sb("conv_b", [P, MC])
        dtp_b, Dw = sb("dtp_b", [P, MC]), sb("Dw", [P, MC])
        a_log, neg_a, a = sb("a_log", [P, MC, NS]), sb("neg_a", [P, MC, NS]), sb("a", [P, MC, NS])
        out_b = sb("out_b", [P, D])
        sel = sb("sel", [96, 32, P], BF16)
        eps_t = sb("one", [P, 1])
        xt = sb("xt", [P, TT, D])
        hid = sb("hid", [P, TT, D])
        stats, mv = sb("stats", [P, TT, 6]), sb("mv", [P, TT, 2])
        veps, logv, guess, tmp, rstd = (sb(n, [P, TT]) for n in ("veps", "logv", "guess", "tmp", "rstd"))
        hnT = sb("hnT", [P, DC, N])
        xpad = sb("xpad", [P, MC, BB, K - 1 + S])
        gate = sb("gate", [P, MC, N])
        xc = sb("xc", [P, MC, N])
        dtraw = sb("dtraw", [R, N])
        dt = sb("dt", [P, MC, N])
        dtx = sb("dtx", [P, MC, N])
        hn = dtx[:, 0:MC // 2, :].rearrange("p a (b d) -> p (a b) d", d=D)
        spa = sb("spa", [P, N])
        split2 = sb("split2", [96, N], BF16)
        parts = sb("parts", [96, N], BF16)
        bc = sb("bc", [P, 2 * NS, N])
        decay, u = sb("decay", [P, 2, PAIR, N]), sb("u", [P, 2, PAIR, N])
        h = sb("h", [P, 2, PAIR, N])
        resid = u[0:96, 0, 0, :]
        ps_ring = [ps(f"ring{k}", [P, N]) for k in range(4)]
        ps_y = [ps(f"y{k}", [P, N]) for k in range(2)]

        loaded = sem("loaded")
        sel_zero, sel_ready, a_exp, consts = sem("sel_zero"), sem("sel_ready"), sem("a_exp"), sem("consts")
        step, astep, pstep = sem("dve_step"), sem("act_step"), sem("pool_step")
        var_ready, log_ready, guess_ready = sem("var_ready"), sem("log_ready"), sem("guess_ready")
        hn_ready, turned, hnT_ready = sem("hn_ready"), sem("turned"), sem("hnT_ready")
        proj_ready, proj_taken = sem("proj_ready"), sem("proj_taken")
        conv_ready, xc_ready = sem("conv_ready"), sem("xc_ready")
        bc_ps, parts_ready = sem("bc_ps"), sem("parts_ready")
        dtraw_ps, dtraw_ready = sem("dtraw_ps"), sem("dtraw_ready")
        spread, spread_taken = sem("spread"), sem("spread_taken")
        dt_ps, dt_log, dt_sum = sem("dt_ps"), sem("dt_log"), sem("dt_sum")
        dtx_ready, dt_reset = sem("dtx_ready"), sem("dt_reset")
        decay_ready, u_ready, h_ready, hc_ready = sem("decay_ready"), sem("u_ready"), sem("h_ready"), sem("hc_ready")
        hc_summed = sem("hc_summed")
        yg_ready, out_ready = sem("yg_ready"), sem("out_ready")
        base_ready, x_done = sem("base_ready"), sem("x_done")
        NLOAD = 14
        pad = sb("pad", [P, 1])
        block = st.block()

        @block.sync
        def _(sp):
            for dst, name in ((in_w, "mb_in_w"), (out_w, "mb_out_w"), (xp_dt, "mb_xp_dt"), (xp_bc, "mb_xp_bc"),
                              (dtp_w, "mb_dtp_w"), (ln_w, "mb_ln_w"), (ln_b, "mb_ln_b"), (in_b, "mb_in_b"),
                              (conv_w, "mb_conv_w"), (conv_b, "mb_conv_b"), (dtp_b, "mb_dtp_b"), (Dw, "mb_D"),
                              (a_log, "mb_A_log"), (out_b, "mb_out_b")):
                sp.dma_start(whole(dst), A[name]).then_inc(loaded, 16)
            sp.wait_ge(loaded, 16 * NLOAD)

        @block.gpsimd
        def _(pool):
            nc.gpsimd.memset(sel[:, :, :], 0.0).then_inc(sel_zero, 1)
            for j in range(3):
                pool.wait_ge(sel_zero, j + 1)
                nc.gpsimd.affine_select(out=sel[:, :, :], in_=sel[:, :, :], compare_op=ALU.not_equal, fill=1.0,
                                        base=-32 * j, pattern=[[-1, 32], [0, P]],
                                        channel_multiplier=1).then_inc(sel_zero, 1)
            pool.wait_ge(loaded, 16 * NLOAD)
            with pool.Fori(0, ITER) as i:
                for m in range(MC):
                    pool.wait_ge(dt_sum, i * MC + m + 1)
                    pool.wait_ge(xc_ready, i * MC + m + 1)
                    nc.gpsimd.tensor_tensor(dtx[:, m, :], dt[:, m, :], xc[:, m, :], ALU.mult).then_inc(dtx_ready, 1)
                pool.wait_ge(hn_ready, i + 1)
                nc.gpsimd.tensor_tensor(xt[:, :, :], xt[:, :, :], hid[:, :, :], ALU.add).then_inc(pstep, 1)
                pool.wait_ge(pstep, i + 1)
                nc.gpsimd.tensor_tensor(xt[:, :, :], xt[:, :, :],
                                        out_b[:, :].rearrange("p (a d) -> p a d", a=1).broadcast_to([P, TT, D]),
                                        ALU.add).then_inc(base_ready, 1)
                for m in range(MC):
                    pool.wait_ge(dtx_ready, i * MC + m + 1)
                    for k in range(PAIRS):
                        n = m * PAIRS + k
                        pool.wait_ge(spread_taken, i * 2 * NS + 4 * k + 2)
                        pool.wait_ge(h_ready, i * (MC * PAIRS) + n + 1)
                        nc.gpsimd.tensor_tensor(
                            u[:, n % 2, :, :],
                            dtx[:, m:m + 1, :].broadcast_to([P, PAIR, N]),
                            bc[:, PAIR * k:PAIR * (k + 1), :], ALU.mult).then_inc(u_ready, 1)

        @block.scalar
        def _(act):
            act.wait_ge(loaded, 16 * NLOAD)
            nc.scalar.activation(neg_a[:, :, :], a_log[:, :, :], ACT.Exp).then_inc(a_exp, 1)
            act.wait_ge(consts, 1)
            with act.Fori(0, ITER) as i:
                for r in range(2):
                    rsqrt_guess(nc, act, veps, TT, logv, guess, var_ready, log_ready, guess_ready, i * 2 + r + 1)
                for c in range(DC):
                    act.wait_ge(turned, i * DC + c + 1)
                    nc.scalar.activation(hnT[:, c, :], ps_ring[c][:, :], ACT.Identity,
                                         bias=ln_b[:, c:c + 1], scale=ln_w[:, c:c + 1]).then_inc(hnT_ready, 1)
                for m in range(2 * MC):
                    act.wait_ge(proj_ready, i * 2 * MC + m + 1)
                    src = ps_ring[m % 4]
                    if m < MC:
                        nc.scalar.activation(xpad[:, m, :, K - 1:], src[:, :].rearrange("p (b s) -> p b s", b=BB),
                                             ACT.Identity, bias=in_b[:, m:m + 1]).then_inc(proj_taken, 1)
                    else:
                        nc.scalar.activation(gate[:, m - MC, :], src[:, :], ACT.Silu,
                                             bias=in_b[:, m:m + 1]).then_inc(proj_taken, 1)
                for m in range(MC):
                    act.wait_ge(conv_ready, i * MC + m + 1)
                    nc.scalar.activation(xc[:, m, :], dt[:, m, :], ACT.Silu).then_inc(xc_ready, 1)
                act.wait_ge(dtraw_ps, i + 1)
                nc.scalar.activation(dtraw[:, :], ps_ring[0][0:R, :], ACT.Identity).then_inc(dtraw_ready, 1)
                for m in range(MC):
                    act.wait_ge(dt_ps, i * MC + m + 1)
                    if m:
                        act.wait_ge(dt_sum, i * MC + m)
                    q = ps_ring[2 + m % 2]
                    nc.scalar.activation(spa[:, :], q[:, :], ACT.Abs, bias=dtp_b[:, m:m + 1]).then_inc(astep, 1)
                    nc.scalar.activation(dt[:, m, :], q[:, :], ACT.Relu, bias=dtp_b[:, m:m + 1]).then_inc(astep, 1)
                    act.wait_ge(astep, i * 3 * MC + 3 * m + 2)
                    nc.scalar.activation(spa[:, :], spa[:, :], ACT.Exp, scale=-1.0).then_inc(astep, 1)
                    act.wait_ge(astep, i * 3 * MC + 3 * m + 3)
                    nc.scalar.activation(spa[:, :], spa[:, :], ACT.Ln, bias=1.0).then_inc(dt_log, 1)
                act.wait_ge(dt_reset, i + 1)
                for m in range(MC):
                    for k in range(PAIRS):
                        n = m * PAIRS + k
                        for r in range(4 * k, 4 * k + 4) if m == 0 else ():
                            act.wait_ge(spread, i * 2 * NS + r + 1)
                            nc.scalar.activation(bc[:, spread_row(r), :], ps_ring[r % 4][:, :],
                                                 ACT.Identity).then_inc(spread_taken, 1)
                        act.wait_ge(h_ready, i * (MC * PAIRS) + n + 1)
                        for j in range(PAIR):
                            nc.scalar.activation(decay[:, n % 2, j, :], dt[:, m, :], ACT.Exp,
                                                 scale=a[:, m, PAIR * k + j:PAIR * k + j + 1]).then_inc(decay_ready, 1)

        @block.vector
        def _(dve):
            nc.vector.memset(xpad[:, :, :, 0:K - 1], 0.0)
            dve.wait_ge(a_exp, 1)
            nc.vector.tensor_scalar(a[:, :, :], neg_a[:, :, :], -1.0, None, ALU.mult).then_inc(consts, 1)
            nc.vector.memset(eps_t[:, :], 0.0).then_inc(h_ready, 2)
            dve.wait_ge(loaded, 16 * NLOAD)
            ch = Chain(dve, step, per=1 + 2 * (3 * TT + 3) - 1 + MC * (K - 1) + 4 + MC)
            link = ch.link
            with dve.Fori(0, ITER) as i:
                ch.start(i)
                link(nc.vector.tensor_scalar(xt[:, :, :], X[:, bass.ds(i * TT, TT), :], 1.0, None, ALU.mult))
                src, dst = xt, hid
                for r in range(2):
                    layer_norm_stats(nc, dve, ch, src, TT, stats, mv, veps, var_ready, i * 2 + r + 1, pad)
                    rsqrt_refine(nc, dve, link, veps, TT, guess, tmp, rstd, guess_ready, i * 2 + r + 1)
                    if r == 0:
                        normalize(nc, link, src, dst, TT, mv, rstd)
                        src, dst = hid, hn
                    else:
                        for t in range(TT):
                            ins = nc.vector.tensor_scalar(dst[:, t, :], src[:, t, :], mv[:, t, 0:1], rstd[:, t:t + 1],
                                                          ALU.subtract, ALU.mult)
                            if t < TT - 1:
                                link(ins)
                            else:
                                ins.then_inc(hn_ready, 1)
                for m in range(MC):
                    dve.wait_ge(proj_taken, i * 2 * MC + m + 1)
                    z = dt[:, m, :].rearrange("p (b s) -> p b s", b=BB)
                    link(nc.vector.tensor_scalar(z, xpad[:, m, :, 0:S], conv_w[:, m, 0:1], conv_b[:, m:m + 1],
                                                 ALU.mult, ALU.add))
                    for k in range(1, K):
                        ins = nc.vector.scalar_tensor_tensor(out=z, in0=xpad[:, m, :, k:k + S],
                                                             scalar=conv_w[:, m, k:k + 1], in1=z,
                                                             op0=ALU.mult, op1=ALU.add)
                        if k < K - 1:
                            link(ins)
                        else:
                            ins.then_inc(conv_ready, 1)
                dve.wait_ge(bc_ps, i + 1)
                q = ps_ring[1]
                link(nc.vector.tensor_copy(parts[:, :], q[0:96, :]))
                link(nc.vector.tensor_tensor(resid[:, :], q[0:96, :], parts[:, :], ALU.subtract))
                link(nc.vector.tensor_copy(split2[:, :], resid[:, :]))
                link(nc.vector.tensor_copy(parts[32:64, :], split2[32:64, :]))
                nc.vector.tensor_tensor(parts[64:96, :], resid[64:96, :], split2[64:96, :],
                                        ALU.subtract).then_inc(parts_ready, 1)
                for m in range(MC):
                    dve.wait_ge(dt_log, i * MC + m + 1)
                    nc.vector.tensor_tensor(dt[:, m, :], dt[:, m, :], spa[:, :], ALU.add).then_inc(dt_sum, 1)
                dve.wait_ge(dtx_ready, (i + 1) * MC)
                nc.vector.memset(dt[:, :, 0:N:S], RESET).then_inc(dt_reset, 1)
                for m in range(MC):
                    for k in range(PAIRS):
                        n = m * PAIRS + k
                        nn = i * (MC * PAIRS) + n
                        dve.wait_ge(decay_ready, PAIR * (nn + 1))
                        dve.wait_ge(u_ready, nn + 1)
                        if n >= 2:
                            dve.wait_ge(hc_summed, nn - 1)
                        flat = lambda x: x[:, n % 2, :, :].rearrange("p a b -> p (a b)")
                        nc.vector.tensor_tensor_scan(flat(h), flat(decay), flat(u), 0.0, ALU.mult,
                                                     ALU.add).then_inc(h_ready, 1)
                        dve.wait_ge(h_ready, nn + 3)
                        if m == 0:
                            dve.wait_ge(spread_taken, i * 2 * NS + 4 * k + 4)
                        nc.vector.tensor_tensor(h[:, n % 2, :, :], h[:, n % 2, :, :],
                                                bc[:, NS + PAIR * k:NS + PAIR * (k + 1), :],
                                                ALU.mult).then_inc(hc_ready, 1)
                    dve.wait_ge(hc_summed, i * (MC * PAIRS) + (m + 1) * PAIRS)
                    link(nc.vector.scalar_tensor_tensor(out=xc[:, m, :], in0=xc[:, m, :], scalar=Dw[:, m:m + 1],
                                                        in1=ps_y[m % 2][:, :], op0=ALU.mult, op1=ALU.add))
                    nc.vector.tensor_tensor(xc[:, m, :], xc[:, m, :], gate[:, m, :], ALU.mult).then_inc(yg_ready, 1)
                dve.wait_ge(base_ready, i + 1)
                for p in range(2):
                    dve.wait_ge(out_ready, i * 2 + p + 1)
                    nc.vector.tensor_tensor(X[:, bass.ds(i * TT + 2 * p, 2), :], xt[:, 2 * p:2 * p + 2, :],
                                            ps_ring[p][:, :].rearrange("p (t d) -> p t d", t=2),
                                            ALU.add).then_inc(x_done, 1)
                dve.wait_ge(x_done, (i + 1) * 2)
                ch.stop()

        @block.tensor
        def _(pe):
            def spread_pair(i, k):
                for n in range(4 * k, 4 * k + 4):
                    if n >= 4:
                        pe.wait_ge(spread_taken, i * 2 * NS + n - 3)
                    nc.tensor.matmul(ps_ring[n % 4][:, :], sel[:, spread_row(n), :], parts[:, :],
                                     start=True, stop=True).then_inc(spread, 1)

            pe.wait_ge(loaded, 16 * NLOAD)
            pe.wait_ge(sel_zero, 4)
            with pe.Fori(0, ITER) as i:
                pe.wait_ge(hn_ready, i + 1)
                for c in range(DC):
                    for t in range(TT):
                        mm = nc.tensor.transpose(ps_ring[c][:, t * P:(t + 1) * P], hn[:, t, c * P:(c + 1) * P],
                                                 ident[:, :])
                    mm.then_inc(turned, 1)
                pe.wait_ge(hnT_ready, (i + 1) * DC)
                for m in range(2 * MC):
                    if m >= 4:
                        pe.wait_ge(proj_taken, i * 2 * MC + m - 3)
                    for c in range(DC):
                        mm = nc.tensor.matmul(ps_ring[m % 4][:, :], in_w[:, c, m * P:(m + 1) * P], hnT[:, c, :],
                                              start=(c == 0), stop=(c == DC - 1))
                    mm.then_inc(proj_ready, 1)
                pe.wait_ge(proj_taken, (i + 1) * 2 * MC)
                pe.wait_ge(xc_ready, (i + 1) * MC)
                for m in range(MC):
                    mm = nc.tensor.matmul(ps_ring[0][0:R, :], xp_dt[:, m, :], xc[:, m, :],
                                          start=(m == 0), stop=(m == MC - 1))
                mm.then_inc(dtraw_ps, 1)
                for m in range(MC):
                    mm = nc.tensor.matmul(ps_ring[1][0:96, :], xp_bc[:, m, :], xc[:, m, :],
                                          start=(m == 0), stop=(m == MC - 1))
                mm.then_inc(bc_ps, 1)
                pe.wait_ge(dtraw_ready, i + 1)
                for m in range(MC):
                    if m >= 2:
                        pe.wait_ge(dt_log, i * MC + m - 1)
                    nc.tensor.matmul(ps_ring[2 + m % 2][:, :], dtp_w[:, m * P:(m + 1) * P], dtraw[:, :],
                                     start=True, stop=True).then_inc(dt_ps, 1)
                pe.wait_ge(parts_ready, i + 1)
                pe.wait_ge(dt_log, (i + 1) * MC)
                spread_pair(i, 0)
                spread_pair(i, 1)
                for m in range(MC):
                    for k in range(PAIRS):
                        n = m * PAIRS + k
                        pe.wait_ge(hc_ready, i * (MC * PAIRS) + n + 1)
                        if k == 0 and m >= 2:
                            pe.wait_ge(yg_ready, i * MC + m - 1)
                        for j in range(PAIR):
                            mm = nc.tensor.matmul(ps_y[m % 2][:, :], ident[:, :], h[:, n % 2, j, :],
                                                  start=(k == 0 and j == 0), stop=(k == PAIRS - 1 and j == PAIR - 1))
                        mm.then_inc(hc_summed, 1)
                        if m == 0 and k + 2 < PAIRS:
                            spread_pair(i, k + 2)
                pe.wait_ge(spread_taken, (i + 1) * 2 * NS)
                pe.wait_ge(yg_ready, (i + 1) * MC)
                for p in range(2):
                    for t in range(2):
                        for m in range(MC):
                            mm = nc.tensor.matmul(ps_ring[p][:, t * D:(t + 1) * D],
                                                  xc[:, m, (2 * p + t) * P:(2 * p + t + 1) * P], out_w[:, m, :],
                                                  start=(m == 0), stop=(m == MC - 1))
                    mm.then_inc(out_ready, 1)


def attention(nc, A, X, ident, kind, Y=None):
    LT = 2
    ITER = NT // LT
    HD = 64 if kind == "batch" else 16
    NH = D // HD
    HC = P // HD
    NK = {"self1": 256, "batch": P}.get(kind, 120)
    SETS = 2 if kind in ("self1", "batch") else 1
    UNITS = {"self1": [(0, 0), (0, 1), (1, 0), (1, 1)], "batch": [(0, 0), (1, 1)]}.get(kind, [(0, 0), (1, 0)])
    KC = -(-NK // P)
    KP = min(NK, P)
    GH = 4 // KC
    GU = NH // GH
    U = len(UNITS)
    G = U * GU
    SCALE = HD ** -0.5
    cross = kind.startswith("cross")
    has_bias = kind in ("cross0", "self1", "batch")
    pre = {"cross0": "c0", "cross1": "c1", "self1": "sa", "batch": "ba"}[kind]
    MASKED = 1.0e30

    with Stage(nc, kind) as st:
        sb, ps, sem = st.sb, st.ps, st.sem
        wq, wo = sb("wq", [P, DC, D]), sb("wo", [P, DC, D])
        wk = [sb(f"wk{s}", [P, DC, D]) for s in range(SETS if kind == "self1" else 1)]
        wv = [sb(f"wv{s}", [P, DC, D]) for s in range(SETS if kind == "self1" else 1)]
        loads = [(wq, "wq"), (wo, "wo")] + [(w, f"wk{s}") for s, w in enumerate(wk)] + [(w, f"wv{s}") for s, w in enumerate(wv)]
        if kind != "self1":
            bq, bk, bv, bo = sb("bq", [P, DC]), sb("bk", [P, DC]), sb("bv", [P, D]), sb("bo", [P, D])
            loads += [(bq, "bq"), (bk, "bk"), (bv, "bv"), (bo, "bo")]
        else:
            mix = sb("mix", [P, 2])
            share = sb("share", [P, 2])
            neg_rate = sb("neg_rate", [P, 1])
            small = sb("small", [P, 2])
            loads += [(mix, "mix")]
        if kind == "batch":
            g1, be1 = sb("g1", [P, D]), sb("be1", [P, D])
            mod8 = sb("mod8", [P, 1])
            loads += [(g1, "g1"), (be1, "be1"), (mod8, "mod8")]
        xt, xn = sb("xt", [P, LT, D]), sb("xn", [P, LT, D])
        stats, mv = sb("stats", [P, LT, 6]), sb("mv", [P, LT, 2])
        veps, logv, guess, tmp, rstd = (sb(n, [P, LT]) for n in ("veps", "logv", "guess", "tmp", "rstd"))
        xnT, qT = sb("xnT", [P, DC, LT * P]), sb("qT", [P, DC, LT * P])
        kT = [sb(f"kT{s}", [P, DC, NK]) for s in range(SETS)]
        kz = [sb(f"kz{s}", [P, DC, HC, NK]) for s in range(SETS)]
        V = [sb(f"V{s}", [P, KC, NH, HD + 1]) for s in range(SETS)]
        if cross:
            ctxT = sb("ctxT", [P, 2, DC, NK])
        if kind == "cross0":
            mask8 = sb("mask8", [P, 2, LT, NK], U8)
        if has_bias:
            bias = sb("bias", [P, LT, NK])
            biased = sb("biased", [P, 3, GH, NK])
        top, ntop = sb("top", [P, G * GH]), sb("ntop", [P, G * GH])
        prob = sb("prob", [P, 3, GH, NK])
        pT = sb("pT", [P, 2, 4, P])
        inv = sb("inv", [P, 2, NH])
        ao, aob, aoT = sb("ao", [P, LT, D]), sb("aob", [P, D]), sb("aoT", [P, DC, P])
        ps_s = [ps(f"s{k}", [P, 512]) for k in range(3)]
        ps_t = [ps(f"t{k}", [P, 512]) for k in range(2)]
        ps_o = [ps(f"o{k}", [P, 512]) for k in range(2)]
        ps_w = ps("w", [P, 512])

        loaded, ready0, kzeroed = sem("loaded"), sem("ready0"), sem("kzeroed")
        ctx_loaded = [sem(f"ctx_loaded{k}") for k in range(2)]
        made = sem("made")
        step, pstep = sem("dve_step"), sem("pool_step")
        var_ready, log_ready, guess_ready = sem("var_ready"), sem("log_ready"), sem("guess_ready")
        xn_ready, turned, xnT_ready = sem("xn_ready"), sem("turned"), sem("xnT_ready")
        q_ps, q_ready = sem("q_ps"), sem("q_ready")
        k_ps, kT_ready, kz_ready = sem("k_ps"), sem("kT_ready"), sem("kz_ready")
        v_ps, v_ready = sem("v_ps"), sem("v_ready")
        scored, top_ready, prob_ready = sem("scored"), sem("top_ready"), sem("prob_ready")
        prob_turned = sem("prob_turned")
        pT_even, pT_odd = sem("pT_even"), sem("pT_odd")
        weighed, ao_ready = sem("weighed"), sem("ao_ready")
        ao_turned, aoT_ready, out_ps = sem("ao_turned"), sem("aoT_ready"), sem("out_ps")
        base_ready, x_done = sem("base_ready"), sem("x_done")
        NLOAD = 16 * len(loads)
        NORMS = 2 if kind == "batch" else 1
        NDMA = HC * SETS
        pad = sb("pad", [P, 1])
        block = st.block()

        def tile_ends(u):
            return u == U - 1 or UNITS[u + 1][0] != UNITS[u][0]

        ENDS = [u for u in range(U) if tile_ends(u)]
        STEPS = (1 + NORMS * (2 * LT + 3) + LT - 1 + {"cross0": 1 + G, "cross1": 0, "self1": G // 2, "batch": G + LT + 2}[kind]
                 + {"self1": 2 * 3 + 2 * 3, "batch": LT}.get(kind, LT))

        @block.sync
        def _(sp):
            for dst, name in loads:
                sp.dma_start(whole(dst), A[f"{pre}_{name}"]).then_inc(loaded, 16)
            sp.wait_ge(kzeroed, SETS + 1)
            if cross:
                def fetch(b, k):
                    sp.dma_start(ctxT[:, k, :, :], A["ctxT"][:, :, bass.ds(b * NK, NK)]).then_inc(ctx_loaded[k], 16)
                    if kind == "cross0":
                        sp.dma_start(mask8[:, k, :, :],
                                     A["c0_mask"][:, bass.ds(b * LT, LT), :]).then_inc(ctx_loaded[k], 16)
                fetch(0, 0)
                fetch(1, 1)

                def body(ii, k, i):
                    expand(i)
                    sp.wait_ge(v_ready, (i + 1) * SETS * KC)
                    sp.wait_ge(k_ps, (i + 1) * SETS * DC)

            def expand(i):
                sp.wait_ge(kT_ready, (i + 1) * SETS * DC)
                for s in range(SETS):
                    for h in range(HC):
                        rows = slice(HD * h, HD * h + HD)
                        sp.dma_start(kz[s][rows, :, h, :], kT[s][rows, :, :]).then_inc(kz_ready, 16)

            if cross:
                with sp.Fori(0, ITER // 2 - 1) as ii:
                    for k in range(2):
                        body(ii, k, ii * 2 + k)
                        fetch(ii * 2 + k + 2, k)
                for k in range(2):
                    expand(ITER - 2 + k)
            else:
                with sp.Fori(0, ITER) as i:
                    expand(i)
            sp.wait_ge(loaded, NLOAD)
            sp.wait_ge(kz_ready, 16 * NDMA * ITER)

        @block.gpsimd
        def _(pool):
            for s in range(SETS):
                nc.gpsimd.memset(whole(kz[s]), 0.0).then_inc(kzeroed, 1)
            if kind == "self1":
                nc.gpsimd.iota(bias[:, :, :], [[-P, LT], [1, NK]], base=0, channel_multiplier=-1,
                               allow_small_or_imprecise_dtypes=True).then_inc(kzeroed, 1)
            elif kind == "batch":
                ids = biased[:, 0:1, 0, :].rearrange("p a k -> p (a k)")
                nc.gpsimd.iota(ids.rearrange("p (b q) -> p b q", q=8), [[0, 16], [1, 8]], base=0,
                               channel_multiplier=0, allow_small_or_imprecise_dtypes=True).then_inc(kzeroed, 1)
            else:
                nc.gpsimd.memset(ao[:, 0, 0:1], 0.0).then_inc(kzeroed, 1)
            pool.wait_ge(loaded, NLOAD)
            if kind != "self1":
                with pool.Fori(0, ITER) as i:
                    pool.wait_ge(xn_ready, i + 1)
                    src = xn if kind == "batch" else xt
                    nc.gpsimd.tensor_tensor(xt[:, :, :], src[:, :, :],
                                            bo[:, :].rearrange("p (a d) -> p a d", a=1).broadcast_to([P, LT, D]),
                                            ALU.add).then_inc(base_ready, 1)

        @block.scalar
        def _(act):
            act.wait_ge(loaded, NLOAD)
            if kind == "self1":
                nc.scalar.activation(small[:, 0:1], mix[:, 0:1], ACT.Exp, scale=-1.0).then_inc(ready0, 1)
            with act.Fori(0, ITER) as i:
                rsqrt_guess(nc, act, veps, LT, logv, guess, var_ready, log_ready, guess_ready, i * NORMS + 1)
                act.wait_ge(turned, i + 1)
                nc.scalar.activation(xnT[:, :, :], ps_s[0][:, :].rearrange("p (c n) -> p c n", c=DC),
                                     ACT.Identity).then_inc(xnT_ready, 1)
                for s in range(SETS):
                    src = (ps_s[2], ps_t[0])[s]
                    act.wait_ge(k_ps, i * SETS * DC + DC * (s + 1))
                    for m in range(DC):
                        kw = {} if kind == "self1" else {"bias": bk[:, m:m + 1]}
                        nc.scalar.activation(kT[s][:, m, :], src[:, m * 256:m * 256 + NK], ACT.Identity,
                                             **kw).then_inc(kT_ready, 1)
                for g in range(G + 8):
                    if g < G:
                        act.wait_ge(top_ready, i * G + g + 1)
                        if g >= 3:
                            act.wait_ge(prob_turned, i * G + g - 2)
                        for h in range(GH):
                            src = biased[:, g % 3, h, :] if has_bias and (kind != "self1" or UNITS[g // GU][1] == 0) else ps_s[g % 3][:, h * NK:(h + 1) * NK]
                            ins = nc.scalar.activation(prob[:, g % 3, h, :], src, ACT.Exp,
                                                       bias=ntop[:, g * GH + h:g * GH + h + 1])
                        ins.then_inc(prob_ready, 1)
                    e = g - 2
                    if 0 <= e < G and e % 2:
                        act.wait_ge(prob_turned, i * G + e + 1)
                        if e >= 2:
                            act.wait_ge(weighed, i * G + e - 1)
                        nc.scalar.activation(pT[0:KP, e % 2, :, :],
                                             ps_t[e % 2][0:KP, :].rearrange("p (j n) -> p j n", j=4),
                                             ACT.Identity).then_inc(pT_odd, 1)
                    for n, u in enumerate(ENDS):
                        if g == (u + 1) * GU - 1 + 5:
                            act.wait_ge(ao_turned, i * LT + n + 1)
                            nc.scalar.activation(aoT[:, :, :], ps_w[:, 0:D].rearrange("p (c n) -> p c n", c=DC),
                                                 ACT.Identity).then_inc(aoT_ready, 1)
                if kind == "batch":
                    rsqrt_guess(nc, act, veps, LT, logv, guess, var_ready, log_ready, guess_ready, i * NORMS + 2)

        @block.vector
        def _(dve):
            for s in range(SETS):
                nc.vector.memset(V[s][:, :, :, HD:HD + 1], 1.0).then_inc(made, 1)
            nc.vector.memset(top[:, :], 0.0)
            dve.wait_ge(loaded, NLOAD)
            ch0 = Chain(dve, step)
            if kind == "self1":
                dve.wait_ge(ready0, 1)
                ch0.link(nc.vector.tensor_scalar(small[:, 1:2], small[:, 0:1], 1.0, None, ALU.add))
                ch0.link(nc.vector.reciprocal(share[:, 0:1], small[:, 1:2]))
                ch0.link(nc.vector.tensor_scalar(share[:, 1:2], share[:, 0:1], -1.0, 1.0, ALU.mult, ALU.add))
                ch0.link(nc.vector.tensor_scalar(small[:, 0:1], mix[:, 1:2], -1.0, 1.0, ALU.mult, ALU.add))
                ch0.link(nc.vector.tensor_scalar(neg_rate[:, :], small[:, 0:1], -1.0, None, ALU.mult))
                dve.wait_ge(kzeroed, SETS + 1)
                dist = biased[:, 0:2, 0, :]
                ch0.link(nc.vector.scalar_tensor_tensor(out=dist, in0=bias[:, :, :], scalar=-1.0, in1=bias[:, :, :],
                                                        op0=ALU.mult, op1=ALU.max))
                ch0.link(nc.vector.tensor_scalar(bias[:, :, :], dist, neg_rate[:, 0:1], None, ALU.mult))
            elif kind == "batch":
                dve.wait_ge(kzeroed, SETS + 1)
                ch0.link(nc.vector.tensor_scalar(bias[:, 0, :], biased[:, 0, 0, :], mod8[:, 0:1], None, ALU.is_equal))
                ch0.link(nc.vector.tensor_scalar(bias[:, 0, :], bias[:, 0, :], MASKED, -MASKED, ALU.mult, ALU.add))
                ch0.link(nc.vector.tensor_copy(bias[:, 1, :], bias[:, 0, :]))
            ch = Chain(dve, step, per=STEPS, base=ch0.n)
            link = ch.link

            def body(i, ctx_buffer, ctx_count):
                ch.start(i)
                link(nc.vector.tensor_scalar(xt[:, :, :], X[:, bass.ds(i * LT, LT), :], 1.0, None, ALU.mult))
                norm_front(0, i, xt)
                for t in range(LT):
                    ins = nc.vector.tensor_scalar(xn[:, t, :], xt[:, t, :], mv[:, t, 0:1], rstd[:, t:t + 1],
                                                  ALU.subtract, ALU.mult)
                    if t < LT - 1:
                        link(ins)
                    else:
                        ins.then_inc(xn_ready, 1)
                if kind == "cross0":
                    dve.wait_ge(ctx_loaded[ctx_buffer], ctx_count)
                    link(nc.vector.tensor_scalar(bias[:, :, :], mask8[:, ctx_buffer, :, :], MASKED, -MASKED,
                                                 ALU.mult, ALU.add))
                for s in range(SETS):
                    dve.wait_ge(v_ps, i * SETS * KC + (s + 1) * KC)
                    for k in range(KC):
                        src = (ps_t[1], ps_w)[s][0:KP, k * D:(k + 1) * D].rearrange("p (h e) -> p h e", h=NH)
                        dst = V[s][0:KP, k, :, 0:HD]
                        if kind == "self1":
                            nc.vector.tensor_copy(dst, src).then_inc(v_ready, 1)
                        else:
                            nc.vector.tensor_tensor(dst, src, bv[0:KP, :].rearrange("p (h e) -> p h e", h=NH),
                                                    ALU.add).then_inc(v_ready, 1)
                dve.wait_ge(q_ps, (i + 1) * DC)
                for m in range(DC):
                    src = ps_s[1][:, m * LT * P:(m + 1) * LT * P]
                    if kind == "self1":
                        nc.vector.tensor_scalar(qT[:, m, :], src, SCALE, None, ALU.mult).then_inc(q_ready, 1)
                    else:
                        nc.vector.tensor_scalar(qT[:, m, :], src, bq[:, m:m + 1], SCALE, ALU.add,
                                                ALU.mult).then_inc(q_ready, 1)
                for g in range(G + 8):
                    if g < G:
                        t, s = UNITS[g // GU]
                        dve.wait_ge(scored, i * G + g + 1)
                        if has_bias:
                            if g >= 3:
                                dve.wait_ge(prob_ready, i * G + g - 2)
                            if kind != "self1" or s == 0:
                                nc.vector.memset(pad[:, :], 0.0)
                            if kind != "self1" or s == 0:
                                for h in range(GH):
                                    ins = nc.vector.tensor_tensor_reduce(
                                        out=biased[:, g % 3, h, :], in0=ps_s[g % 3][:, h * NK:(h + 1) * NK],
                                        in1=bias[:, t, :], scale=1.0, scalar=-3.0e38, op0=ALU.add, op1=ALU.max,
                                        accum_out=top[:, g * GH + h:g * GH + h + 1])
                                link(ins)
                                nc.vector.tensor_scalar(ntop[:, g * GH:(g + 1) * GH], top[:, g * GH:(g + 1) * GH],
                                                        -1.0, None, ALU.mult).then_inc(top_ready, 1)
                        if not has_bias or (kind == "self1" and s == 1):
                            nc.vector.tensor_reduce(ntop[:, g * GH:(g + 1) * GH],
                                                    ps_s[g % 3][:, 0:GH * NK].rearrange("p (h k) -> p h k", h=GH),
                                                    AX.X, ALU.max, negate=True).then_inc(top_ready, 1)
                    e = g - 2
                    if 0 <= e < G and e % 2 == 0:
                        dve.wait_ge(prob_turned, i * G + e + 1)
                        if e >= 2:
                            dve.wait_ge(weighed, i * G + e - 1)
                        nc.vector.tensor_copy(pT[0:KP, e % 2, :, :],
                                              ps_t[e % 2][0:KP, :].rearrange("p (j n) -> p j n", j=4)).then_inc(pT_even, 1)
                    for u in range(U):
                        if g == (u + 1) * GU - 1 + 4:
                            normalize_unit(i, u)
                    for n, u in enumerate(ENDS):
                        if g == (u + 1) * GU - 1 + 7:
                            dve.wait_ge(out_ps, i * LT + n + 1)
                            if n == 0 and kind != "self1":
                                dve.wait_ge(base_ready, i + 1)
                            o = ps_w[:, D:2 * D]
                            if kind == "batch":
                                nc.vector.tensor_tensor(xt[:, n, :], xt[:, n, :], o, ALU.add).then_inc(x_done, 1)
                            else:
                                nc.vector.tensor_tensor(X[:, bass.ds(i * LT + n, 1), :],
                                                        xt[:, n:n + 1, :], o.rearrange("p (a d) -> p a d", a=1),
                                                        ALU.add).then_inc(x_done, 1)
                dve.wait_ge(x_done, (i + 1) * LT)
                if kind == "batch":
                    norm_front(1, i, xt)
                    for t in range(LT):
                        link(nc.vector.tensor_scalar(xn[:, t, :], xt[:, t, :], mv[:, t, 0:1], rstd[:, t:t + 1],
                                                     ALU.subtract, ALU.mult))
                    link(nc.vector.tensor_tensor(xn[:, :, :], xn[:, :, :],
                                                 g1[:, :].rearrange("p (a d) -> p a d", a=1).broadcast_to([P, LT, D]), ALU.mult))
                    link(nc.vector.tensor_tensor(Y[:, bass.ds(i * LT, LT), :], xn[:, :, :],
                                                 be1[:, :].rearrange("p (a d) -> p a d", a=1).broadcast_to([P, LT, D]),
                                                 ALU.add))
                ch.stop()

            def norm_front(r, i, src):
                layer_norm_stats(nc, dve, ch, src, LT, stats, mv, veps, var_ready, i * NORMS + r + 1, pad)
                rsqrt_refine(nc, dve, link, veps, LT, guess, tmp, rstd, guess_ready, i * NORMS + r + 1)

            def normalize_unit(i, u):
                t, s = UNITS[u]
                o = ps_o[u % 2][:, 0:NH * (HD + 1)].rearrange("p (h e) -> p h e", h=NH)
                dve.wait_ge(weighed, i * G + (u + 1) * GU)
                link(nc.vector.reciprocal(inv[:, u % 2, :].rearrange("p (h e) -> p h e", e=1), o[:, :, HD:HD + 1]))
                if kind == "self1":
                    link(nc.vector.tensor_scalar(inv[:, u % 2, :], inv[:, u % 2, :], share[:, s:s + 1], None, ALU.mult))
                dst = aob[:, :] if (kind == "self1" and s == 1) else ao[:, t, :]
                ins = nc.vector.tensor_tensor(dst.rearrange("p (h e) -> p h e", h=NH), o[:, :, 0:HD],
                                              inv[:, u % 2, :].rearrange("p (h e) -> p h e", e=1).broadcast_to([P, NH, HD]), ALU.mult)
                if kind == "self1" and s == 1:
                    link(ins)
                    ins = nc.vector.tensor_tensor(ao[:, t, :], ao[:, t, :], aob[:, :], ALU.add)
                if tile_ends(u):
                    ins.then_inc(ao_ready, 1)
                else:
                    link(ins)

            if cross:
                with dve.Fori(0, ITER // 2) as ii:
                    for k in range(2):
                        body(ii * 2 + k, k, (ii + 1) * (32 if kind == "cross0" else 16))
            else:
                with dve.Fori(0, ITER) as i:
                    body(i, 0, 0)

        @block.tensor
        def _(pe):
            pe.wait_ge(loaded, NLOAD)
            pe.wait_ge(made, SETS)

            def body(i, ctx_buffer, ctx_count):
                pe.wait_ge(xn_ready, i + 1)
                for c in range(DC):
                    for t in range(LT):
                        mm = nc.tensor.transpose(ps_s[0][:, (c * LT + t) * P:(c * LT + t + 1) * P],
                                                 xn[:, t, c * P:(c + 1) * P], ident[:, :])
                mm.then_inc(turned, 1)
                if cross:
                    pe.wait_ge(ctx_loaded[ctx_buffer], ctx_count)
                else:
                    pe.wait_ge(xnT_ready, i + 1)
                for s in range(SETS):
                    w = s if kind == "self1" else 0
                    if cross:
                        src = ctxT[:, ctx_buffer, :, :]
                    elif kind == "self1":
                        src = xnT[:, :, :]
                    else:
                        src = xnT[:, :, s * P:(s + 1) * P]
                    for m in range(DC):
                        for c in range(DC):
                            mm = nc.tensor.matmul((ps_s[2], ps_t[0])[s][:, m * 256:m * 256 + NK],
                                                  wk[w][:, c, m * P:(m + 1) * P], src[:, c, :],
                                                  start=(c == 0), stop=(c == DC - 1))
                        mm.then_inc(k_ps, 1)
                if cross:
                    pe.wait_ge(xnT_ready, i + 1)
                for m in range(DC):
                    for c in range(DC):
                        mm = nc.tensor.matmul(ps_s[1][:, m * LT * P:(m + 1) * LT * P], wq[:, c, m * P:(m + 1) * P],
                                              xnT[:, c, :], start=(c == 0), stop=(c == DC - 1))
                    mm.then_inc(q_ps, 1)
                for s in range(SETS):
                    w = s if kind == "self1" else 0
                    src = ctxT[:, ctx_buffer, :, :] if cross else xnT
                    off = s * P if kind == "batch" else 0
                    for k in range(KC):
                        for c in range(DC):
                            mm = nc.tensor.matmul((ps_t[1], ps_w)[s][0:KP, k * D:(k + 1) * D],
                                                  src[:, c, off + k * P:off + k * P + KP], wv[w][:, c, :],
                                                  start=(c == 0), stop=(c == DC - 1))
                        mm.then_inc(v_ps, 1)
                pe.wait_ge(kz_ready, (i + 1) * NDMA * 16)
                pe.wait_ge(q_ready, (i + 1) * DC)
                pe.wait_ge(v_ready, (i + 1) * SETS * KC)
                pe.wait_ge(kT_ready, (i + 1) * SETS * DC)
                for g in range(G + 8):
                    if g < G:
                        t, s = UNITS[g // GU]
                        if g >= 3:
                            pe.wait_ge(prob_ready, i * G + g - 2)
                        h0 = (g % GU) * GH
                        q = lambda c: qT[:, c, t * P:(t + 1) * P]
                        if HC >= GH:
                            c, hh = h0 // HC, h0 % HC
                            mm = nc.tensor.matmul(ps_s[g % 3][:, 0:GH * NK], q(c),
                                                  kz[s][:, c, hh:hh + GH, :].rearrange("p h k -> p (h k)"),
                                                  start=True, stop=True)
                        else:
                            for c in range(DC):
                                mm = nc.tensor.matmul(ps_s[g % 3][:, c * HC * NK:(c + 1) * HC * NK], q(c),
                                                      kz[s][:, c, :, :].rearrange("p h k -> p (h k)"),
                                                      start=True, stop=True)
                        mm.then_inc(scored, 1)
                    e = g - 2
                    if 0 <= e < G:
                        pe.wait_ge(prob_ready, i * G + e + 1)
                        if e >= 2:
                            if e % 2:
                                pe.wait_ge(pT_odd, i * (G // 2) + e // 2)
                            else:
                                pe.wait_ge(pT_even, i * (G // 2) + e // 2)
                        for j in range(4):
                            h, k = j // KC, j % KC
                            mm = nc.tensor.transpose(ps_t[e % 2][0:KP, j * P:(j + 1) * P],
                                                     prob[:, e % 3, h, k * P:k * P + KP], ident[:, :])
                        mm.then_inc(prob_turned, 1)
                    e = g - 3
                    if 0 <= e < G:
                        pe.wait_ge(pT_odd if e % 2 else pT_even, i * (G // 2) + e // 2 + 1)
                        u = e // GU
                        t, s = UNITS[u]
                        if e % GU == 0 and u >= 2:
                            pe.wait_ge(ao_ready, i * LT + 1)
                        for j in range(4):
                            h, k = (e % GU) * GH + j // KC, j % KC
                            mm = nc.tensor.matmul(ps_o[u % 2][:, h * (HD + 1):(h + 1) * (HD + 1)],
                                                  pT[0:KP, e % 2, j, :], V[s][0:KP, k, h, :],
                                                  start=(k == 0), stop=(k == KC - 1))
                        mm.then_inc(weighed, 1)
                    for n, u in enumerate(ENDS):
                        if g == (u + 1) * GU - 1 + 5:
                            pe.wait_ge(ao_ready, i * LT + n + 1)
                            if n:
                                pe.wait_ge(x_done, i * LT + n)
                            for c in range(DC):
                                mm = nc.tensor.transpose(ps_w[:, c * P:(c + 1) * P],
                                                         ao[:, UNITS[u][0], c * P:(c + 1) * P], ident[:, :])
                            mm.then_inc(ao_turned, 1)
                        if g == (u + 1) * GU - 1 + 6:
                            pe.wait_ge(aoT_ready, i * LT + n + 1)
                            for c in range(DC):
                                mm = nc.tensor.matmul(ps_w[:, D:2 * D], aoT[:, c, :], wo[:, c, :],
                                                      start=(c == 0), stop=(c == DC - 1))
                            mm.then_inc(out_ps, 1)

            if cross:
                with pe.Fori(0, ITER // 2) as ii:
                    for k in range(2):
                        body(ii * 2 + k, k, (ii + 1) * (32 if kind == "cross0" else 16))
            else:
                with pe.Fori(0, ITER) as i:
                    body(i, 0, 0)


def bitffn(nc, A, X, identb):
    LT = 2
    ITER = NT // LT
    HID = 1024
    HCH = HID // P
    ROUND = 12582912.0
    with Stage(nc, "bitffn") as st:
        sb, ps, sem = st.sb, st.ps, st.sem
        w1, w2 = sb("w1", [P, DC, HID]), sb("w2", [P, HCH, D])
        w1q, w2q = sb("w1q", [P, DC, HID], BF16), sb("w2q", [P, HCH, D], BF16)
        b1, b2 = sb("b1", [P, HID]), sb("b2", [P, D])
        ln1_w, ln1_b = sb("ln1_w", [P, D]), sb("ln1_b", [P, D])
        ln2_w, ln2_b = sb("ln2_w", [P, HID]), sb("ln2_b", [P, HID])
        loads = [(w1, "w1"), (w2, "w2"), (b1, "b1"), (b2, "b2"), (ln1_w, "ln1_w"), (ln1_b, "ln1_b"),
                 (ln2_w, "ln2_w"), (ln2_b, "ln2_b")]
        ones = sb("ones", [P, P])
        minus_round = sb("minus_round", [P, 1])
        absum, w_mean, w_scale, w_back = (sb(n, [P, 2]) for n in ("absum", "w_mean", "w_scale", "w_back"))
        pad = sb("pad", [P, 1])
        xt, h = sb("xt", [P, LT, D]), sb("h", [P, LT, D])
        stats, stats2, mv = sb("stats", [P, LT, 6]), sb("stats2", [P, LT, 2, 6]), sb("mv", [P, LT, 2])
        veps, logv, guess, tmp, rstd = (sb(n, [P, LT]) for n in ("veps", "logv", "guess", "tmp", "rstd"))
        amax, a_scale, f1, f2 = (sb(n, [P, LT]) for n in ("amax", "a_scale", "f1", "f2"))
        q1, q1T = sb("q1", [P, LT, D], BF16), sb("q1T", [P, DC, LT * P], BF16)
        g = sb("g", [P, LT, HID])
        gn = sb("gn", [P, LT, HID])
        q2, q2T = sb("q2", [P, LT, HID], BF16), sb("q2T", [P, LT, HCH, P], BF16)
        ps_h = [ps(f"h{k}", [P, 512]) for k in range(4)]
        ps_q = ps("q", [P, DC, LT * P], BF16)
        ps_q2 = [ps(f"q2{k}", [P, HCH, P], BF16) for k in range(LT)]
        ps_o = ps("o", [P, LT, D])

        loaded, step, const_ready, summed, w_ready = sem("loaded"), sem("dve_step"), sem("const_ready"), sem("summed"), sem("w_ready")
        var_ready, log_ready, guess_ready = sem("var_ready"), sem("log_ready"), sem("guess_ready")
        base_ready = sem("base_ready")
        xt_free, ln1_ready = sem("xt_free"), sem("ln1_ready")
        q1_sum, q1_ready, q1_turned, q1T_ready = sem("q1_sum"), sem("q1_ready"), sem("q1_turned"), sem("q1T_ready")
        h_ps, h_ready, g_ready = sem("h_ps"), sem("h_ready"), sem("g_ready")
        gn_ready, scaled, q2_sum, q2_ready = sem("gn_ready"), sem("scaled"), sem("q2_sum"), sem("q2_ready")
        q2_turned, q2T_ready, o_ps, x_done = sem("q2_turned"), sem("q2T_ready"), sem("o_ps"), sem("x_done")
        NLOAD = 16 * len(loads)
        NORMS = 3
        block = st.block()

        @block.sync
        def _(sp):
            for dst, name in loads:
                sp.dma_start(whole(dst), A[f"ff_{name}"]).then_inc(loaded, 16)
            sp.wait_ge(loaded, NLOAD)

        @block.gpsimd
        def _(pool):
            nc.gpsimd.memset(ones[:, :], 1.0).then_inc(const_ready, 1)
            nc.gpsimd.memset(minus_round[:, :], -ROUND).then_inc(const_ready, 1)
            pool.wait_ge(loaded, NLOAD)
            with pool.Fori(0, ITER) as i:
                pool.wait_ge(xt_free, i + 1)
                nc.gpsimd.tensor_tensor(xt[:, :, :], xt[:, :, :],
                                        b2[:, :].rearrange("p (a d) -> p a d", a=1).broadcast_to([P, LT, D]),
                                        ALU.add).then_inc(base_ready, 1)
                for t in range(LT):
                    pool.wait_ge(gn_ready, i * LT + t + 1)
                    nc.gpsimd.tensor_tensor(gn[:, t, :], gn[:, t, :], ln2_w[:, :], ALU.mult).then_inc(scaled, 1)

        @block.scalar
        def _(act):
            act.wait_ge(const_ready, 2)
            with act.Fori(0, ITER) as i:
                for r in range(2):
                    rsqrt_guess(nc, act, veps, LT, logv, guess, var_ready, log_ready, guess_ready, i * NORMS + r + 1)
                act.wait_ge(q1_sum, i + 1)
                nc.scalar.activation(q1[:, :, :], h[:, :, :], ACT.Identity, bias=minus_round[:, 0:1]).then_inc(q1_ready, 1)
                act.wait_ge(q1_turned, i + 1)
                nc.scalar.activation(q1T[:, :, :], ps_q[:, :, :], ACT.Identity).then_inc(q1T_ready, 1)
                for t in range(LT):
                    act.wait_ge(h_ready, i * LT + t + 1)
                    nc.scalar.activation(g[:, t, :], g[:, t, :], ACT.Gelu).then_inc(g_ready, 1)
                rsqrt_guess(nc, act, veps, LT, logv, guess, var_ready, log_ready, guess_ready, i * NORMS + 3)
                for t in range(LT):
                    act.wait_ge(q2_sum, i * LT + t + 1)
                    nc.scalar.activation(q2[:, t, :], gn[:, t, :], ACT.Identity, bias=minus_round[:, 0:1]).then_inc(q2_ready, 1)
                    act.wait_ge(q2_turned, i * LT + t + 1)
                    nc.scalar.activation(q2T[:, t, :, :], ps_q2[t][:, :, :], ACT.Identity).then_inc(q2T_ready, 1)

        @block.vector
        def _(dve):
            dve.wait_ge(loaded, NLOAD)
            dve.wait_ge(const_ready, 2)
            ch0 = Chain(dve, step)
            for k, w in enumerate((w1, w2)):
                ch0.link(nc.vector.tensor_reduce(absum[:, k:k + 1], w[:, :, :], AX.XY, ALU.add, apply_absolute_value=True))
            nc.vector.memset(pad[:, :], 0.0).then_inc(summed, 1)
            dve.wait_ge(summed, 2)
            ch0.link(nc.vector.tensor_scalar(w_mean[:, :], ps_o[:, 0, 0:2], 1.0 / (D * HID), EPS, ALU.mult, ALU.max))
            ch0.link(nc.vector.reciprocal(w_scale[:, :], w_mean[:, :]))
            ch0.link(nc.vector.reciprocal(w_back[:, :], w_scale[:, :]))
            for k, (w, q) in enumerate(((w1, w1q), (w2, w2q))):
                ch0.link(nc.vector.tensor_scalar(w[:, :, :], w[:, :, :], w_scale[:, k:k + 1], ROUND, ALU.mult, ALU.add))
                ch0.link(nc.vector.tensor_scalar(w[:, :, :], w[:, :, :], ROUND, -1.0, ALU.subtract, ALU.max))
                nc.vector.tensor_scalar(q[:, :, :], w[:, :, :], 1.0, None, ALU.min).then_inc(w_ready, 1)
            ch = Chain(dve, step, per=42, base=ch0.n)
            link = ch.link

            def quant_scale(src, n, f, w):
                link(nc.vector.tensor_reduce(amax[:, :], src[:, :, :], AX.X, ALU.max, apply_absolute_value=True))
                link(nc.vector.tensor_scalar(amax[:, :], amax[:, :], EPS, None, ALU.max))
                link(nc.vector.reciprocal(a_scale[:, :], amax[:, :]))
                link(nc.vector.tensor_scalar(a_scale[:, :], a_scale[:, :], 127.0, None, ALU.mult))
                link(nc.vector.tensor_scalar(f[:, :], amax[:, :], w_back[:, w:w + 1], 1.0 / 127.0, ALU.mult, ALU.mult))

            with dve.Fori(0, ITER) as i:
                ch.start(i)
                link(nc.vector.tensor_scalar(xt[:, :, :], X[:, bass.ds(i * LT, LT), :], 1.0, None, ALU.mult))
                for r in range(2):
                    src = xt if r == 0 else h
                    layer_norm_stats(nc, dve, ch, src, LT, stats, mv, veps, var_ready, i * NORMS + r + 1, pad)
                    rsqrt_refine(nc, dve, link, veps, LT, guess, tmp, rstd, guess_ready, i * NORMS + r + 1)
                    for t in range(LT):
                        ins = nc.vector.tensor_scalar(h[:, t, :], src[:, t, :], mv[:, t, 0:1], rstd[:, t:t + 1],
                                                      ALU.subtract, ALU.mult)
                        if r == 0 and t == LT - 1:
                            ins.then_inc(xt_free, 1)
                            dve.wait_ge(xt_free, i + 1)
                        else:
                            link(ins)
                for v, op in ((ln1_w, ALU.mult), (ln1_b, ALU.add)):
                    link(nc.vector.tensor_tensor(h[:, :, :], h[:, :, :],
                                                 v[:, :].rearrange("p (a d) -> p a d", a=1).broadcast_to([P, LT, D]), op))
                quant_scale(h, D, f1, 0)
                for t in range(LT):
                    link(nc.vector.tensor_scalar(h[:, t, :], h[:, t, :], a_scale[:, t:t + 1], 127.0, ALU.mult, ALU.min))
                nc.vector.tensor_scalar(h[:, :, :], h[:, :, :], -128.0, ROUND, ALU.max, ALU.add).then_inc(q1_sum, 1)
                for t in range(LT):
                    dve.wait_ge(h_ps, i * LT + t + 1)
                    for k in range(2):
                        ins = nc.vector.scalar_tensor_tensor(out=g[:, t, k * 512:(k + 1) * 512], in0=ps_h[2 * t + k][:, :],
                                                             scalar=f1[:, t:t + 1], in1=b1[:, k * 512:(k + 1) * 512],
                                                             op0=ALU.mult, op1=ALU.add)
                    ins.then_inc(h_ready, 1)
                for t in range(LT):
                    dve.wait_ge(g_ready, i * LT + t + 1)
                    for k in range(2):
                        ins = nc.vector.bn_stats(stats2[:, t, k, :], g[:, t, k * 512:(k + 1) * 512])
                    link(ins)
                nc.vector.memset(pad[:, :], 0.0)
                for t in range(LT):
                    ins = nc.vector.bn_aggr(mv[:, t, :], stats2[:, t, :, :])
                link(ins)
                nc.vector.tensor_scalar(veps[:, :], mv[:, :, 1], EPS, None, ALU.add).then_inc(var_ready, 1)
                dve.wait_ge(var_ready, i * NORMS + 3)
                rsqrt_refine(nc, dve, link, veps, LT, guess, tmp, rstd, guess_ready, i * NORMS + 3)
                for t in range(LT):
                    nc.vector.tensor_scalar(gn[:, t, :], g[:, t, :], mv[:, t, 0:1], rstd[:, t:t + 1],
                                            ALU.subtract, ALU.mult).then_inc(gn_ready, 1)
                for t in range(LT):
                    dve.wait_ge(scaled, i * LT + t + 1)
                    link(nc.vector.tensor_tensor(gn[:, t, :], gn[:, t, :], ln2_b[:, :], ALU.add))
                quant_scale(gn, HID, f2, 1)
                for t in range(LT):
                    link(nc.vector.tensor_scalar(gn[:, t, :], gn[:, t, :], a_scale[:, t:t + 1], 127.0, ALU.mult, ALU.min))
                    nc.vector.tensor_scalar(gn[:, t, :], gn[:, t, :], -128.0, ROUND, ALU.max, ALU.add).then_inc(q2_sum, 1)
                dve.wait_ge(base_ready, i + 1)
                for t in range(LT):
                    dve.wait_ge(o_ps, i * LT + LT)
                    nc.vector.scalar_tensor_tensor(out=X[:, bass.ds(i * LT + t, 1), :], in0=ps_o[:, t:t + 1, :],
                                                   scalar=f2[:, t:t + 1], in1=xt[:, t:t + 1, :],
                                                   op0=ALU.mult, op1=ALU.add).then_inc(x_done, 1)
                dve.wait_ge(x_done, (i + 1) * LT)
                ch.stop()

        @block.tensor
        def _(pe):
            pe.wait_ge(summed, 1)
            nc.tensor.matmul(ps_o[:, 0, 0:2], ones[:, :], absum[:, :], start=True, stop=True).then_inc(summed, 1)
            pe.wait_ge(w_ready, 2)
            with pe.Fori(0, ITER) as i:
                pe.wait_ge(q1_ready, i + 1)
                for c in range(DC):
                    for t in range(LT):
                        mm = nc.tensor.transpose(ps_q[:, c, t * P:(t + 1) * P], q1[:, t, c * P:(c + 1) * P], identb[:, :])
                mm.then_inc(q1_turned, 1)
                pe.wait_ge(q1T_ready, i + 1)
                for t in range(LT):
                    for k in range(2):
                        for c in range(DC):
                            mm = nc.tensor.matmul(ps_h[2 * t + k][:, :], q1T[:, c, t * P:(t + 1) * P],
                                                  w1q[:, c, k * 512:(k + 1) * 512], start=(c == 0), stop=(c == DC - 1))
                    mm.then_inc(h_ps, 1)
                for t in range(LT):
                    pe.wait_ge(q2_ready, i * LT + t + 1)
                    for c in range(HCH):
                        mm = nc.tensor.transpose(ps_q2[t][:, c, :], q2[:, t, c * P:(c + 1) * P], identb[:, :])
                    mm.then_inc(q2_turned, 1)
                for t in range(LT):
                    pe.wait_ge(q2T_ready, i * LT + t + 1)
                    for c in range(HCH):
                        mm = nc.tensor.matmul(ps_o[:, t, :], q2T[:, t, c, :], w2q[:, c, :],
                                              start=(c == 0), stop=(c == HCH - 1))
                    mm.then_inc(o_ps, 1)


def to_positions(nc, X, scratch):
    with Stage(nc, "deal") as st:
        written, read = st.sem("written"), st.sem("read")
        block = st.block()

        @block.sync
        def _(sp):
            sp.dma_start(scratch.rearrange("(n p) d -> p n d", p=P), X[:, :, :]).then_inc(written, 16)
            sp.wait_ge(written, 16)
            for b in range(B):
                sp.dma_start(X[8 * b:8 * b + 8, :, :],
                             scratch[b * S:(b + 1) * S, :].rearrange("(t q) d -> q t d", q=8)).then_inc(read, 16)
            sp.wait_ge(read, 16 * B)


def route(nc, A, ident, Y, ysort, pos, expert):
    LT, E = 4, 8
    ITER = NT // LT
    ROUND = 12582912.0
    with Stage(nc, "route") as st:
        sb, ps, sem = st.sb, st.ps, st.sem
        wg = sb("wg", [P, DC, E])
        yb, yT = sb("yb", [P, LT, D]), sb("yT", [P, DC, LT * P])
        logits = sb("logits", [P, NT, E])
        best = sb("best", [P, NT])
        chosen, rank = sb("chosen", [P, NT, E]), sb("rank", [P, NT, E])
        zeros = sb("zeros", [P, SLOTS // 2, D])
        before, ones = sb("before", [P, P]), sb("ones", [P, P])
        descend = sb("descend", [P, E])
        keep = sb("keep", [P, E, NT])
        slot = sb("slot", [P, SLOTS])
        count, upto = sb("count", [P, E, NT]), sb("upto", [P, E, NT])
        tiles, end, base = sb("tiles", [P, E]), sb("end", [P, E]), sb("base", [P, E])
        ended = sb("ended", [P, SLOTS, E - 1])
        posf, expertf = sb("posf", [P, NT]), sb("expertf", [P, SLOTS])
        ps_t = [ps(f"t{k}", [P, LT * P]) for k in range(DC)]
        ps_l = ps("l", [P, LT, E])
        ps_rank, ps_count = ps("rank", [P, NT, E]), ps("count", [P, NT, E])

        loaded, zeroed, cleared, const_ready = sem("loaded"), sem("zeroed"), sem("cleared"), sem("const_ready")
        yb_ready, turned, yT_ready = sem("yb_ready"), sem("turned"), sem("yT_ready")
        logits_ps, logits_ready = sem("logits_ps"), sem("logits_ready")
        step, chosen_ready, counted, pos_ready, scattered = (
            sem("dve_step"), sem("chosen_ready"), sem("counted"), sem("pos_ready"), sem("scattered"))
        block = st.block()

        @block.sync
        def _(sp):
            sp.dma_start(wg[:, :, :], A["moe_wg"]).then_inc(loaded, 16)
            sp.wait_ge(zeroed, 1)
            for k in range(2):
                sp.dma_start(ysort.rearrange("(s p) d -> p s d", p=P)[:, k * (SLOTS // 2):(k + 1) * (SLOTS // 2), :],
                             zeros[:, :, :]).then_inc(cleared, 16)
            sp.wait_ge(loaded, 16)
            sp.wait_ge(cleared, 32)

        @block.gpsimd
        def _(pool):
            nc.gpsimd.memset(zeros[:, :, :], 0.0).then_inc(zeroed, 1)
            nc.gpsimd.memset(before[:, :], 1.0).then_inc(zeroed, 1)
            nc.gpsimd.memset(ones[:, :], 1.0).then_inc(zeroed, 1)
            nc.gpsimd.memset(keep[:, :, :], 1.0).then_inc(zeroed, 1)
            pool.wait_ge(zeroed, 4)
            nc.gpsimd.affine_select(out=before[:, :], in_=before[:, :], compare_op=ALU.is_ge, fill=0.0,
                                    base=-1, pattern=[[1, P]], channel_multiplier=-1).then_inc(const_ready, 1)
            nc.gpsimd.affine_select(out=keep[:, :, :], in_=keep[:, :, :], compare_op=ALU.is_ge, fill=0.0,
                                    base=-1, pattern=[[0, E], [1, NT]], channel_multiplier=0).then_inc(const_ready, 1)
            nc.gpsimd.iota(slot[:, :], [[1, SLOTS]], base=0, channel_multiplier=0,
                           allow_small_or_imprecise_dtypes=True).then_inc(const_ready, 1)
            nc.gpsimd.iota(descend[:, :], [[-1, E]], base=E, channel_multiplier=0,
                           allow_small_or_imprecise_dtypes=True).then_inc(const_ready, 1)
            pool.wait_ge(cleared, 32)
            pool.wait_ge(pos_ready, 1)
            for t in range(NT):
                nc.gpsimd.indirect_dma_start(
                    ysort, bass.IndirectOffsetOnAxis(ap=pos[:, t:t + 1], axis=0), Y[:, t, :], None).then_inc(scattered, 16)
            pool.wait_ge(scattered, 16 * NT)

        @block.scalar
        def _(act):
            with act.Fori(0, ITER) as i:
                for c in range(DC):
                    act.wait_ge(turned, i * DC + c + 1)
                    nc.scalar.activation(yT[:, c, :], ps_t[c][:, :], ACT.Identity).then_inc(yT_ready, 1)

        @block.tensor
        def _(pe):
            pe.wait_ge(loaded, 16)
            with pe.Fori(0, ITER) as i:
                pe.wait_ge(yb_ready, i + 1)
                for c in range(DC):
                    for t in range(LT):
                        mm = nc.tensor.transpose(ps_t[c][:, t * P:(t + 1) * P], yb[:, t, c * P:(c + 1) * P], ident[:, :])
                    mm.then_inc(turned, 1)
                pe.wait_ge(yT_ready, (i + 1) * DC)
                for t in range(LT):
                    for c in range(DC):
                        mm = nc.tensor.matmul(ps_l[:, t, :], yT[:, c, t * P:(t + 1) * P], wg[:, c, :],
                                              start=(c == 0), stop=(c == DC - 1))
                mm.then_inc(logits_ps, 1)
            pe.wait_ge(chosen_ready, 1)
            pe.wait_ge(const_ready, 4)
            flat = lambda v: v[:, :, :].rearrange("p t e -> p (t e)")
            nc.tensor.matmul(flat(ps_rank), before[:, :], flat(chosen), start=True, stop=True).then_inc(counted, 1)
            nc.tensor.matmul(flat(ps_count), ones[:, :], flat(chosen), start=True, stop=True).then_inc(counted, 1)

        @block.vector
        def _(dve):
            with dve.Fori(0, ITER) as i:
                nc.vector.tensor_scalar(yb[:, :, :], Y[:, bass.ds(i * LT, LT), :], 1.0, None, ALU.mult).then_inc(yb_ready, 1)
                dve.wait_ge(logits_ps, i + 1)
                nc.vector.tensor_scalar(logits[:, bass.ds(i * LT, LT), :], ps_l[:, :, :], 1.0, None,
                                        ALU.mult).then_inc(logits_ready, 1)
                dve.wait_ge(logits_ready, i + 1)
            dve.wait_ge(const_ready, 4)
            link = Chain(dve, step).link
            over_e = lambda v: v[:, :].rearrange("p (t e) -> p t e", e=1).broadcast_to([P, NT, E])
            by_e = lambda v, n: v.rearrange("p (a e) -> p a e", a=1).broadcast_to([P, n, v.shape[-1]])
            tile_major = lambda v: v[:, :, :].rearrange("p e t -> p t e")
            link(nc.vector.tensor_reduce(best[:, :], logits[:, :, :], AX.X, ALU.max))
            link(nc.vector.tensor_tensor(chosen[:, :, :], logits[:, :, :], over_e(best), ALU.is_equal))
            link(nc.vector.tensor_tensor(rank[:, :, :], chosen[:, :, :], by_e(descend[:, :], NT), ALU.mult))
            link(nc.vector.tensor_reduce(best[:, :], rank[:, :, :], AX.X, ALU.max))
            nc.vector.tensor_tensor(chosen[:, :, :], rank[:, :, :], over_e(best), ALU.is_equal).then_inc(chosen_ready, 1)
            dve.wait_ge(counted, 2)
            link(nc.vector.tensor_copy(tile_major(count), ps_count[:, :, :]))
            link(nc.vector.tensor_tensor_scan(upto[:, :, :].rearrange("p e t -> p (e t)"),
                                              keep[:, :, :].rearrange("p e t -> p (e t)"),
                                              count[:, :, :].rearrange("p e t -> p (e t)"), 0.0, ALU.mult, ALU.add))
            link(nc.vector.tensor_scalar(tiles[:, :], upto[:, :, NT - 1], 1.0 / P, (P - 1) / (2.0 * P), ALU.mult, ALU.add))
            link(nc.vector.tensor_scalar(tiles[:, :], tiles[:, :], ROUND, None, ALU.add))
            link(nc.vector.tensor_scalar(tiles[:, :], tiles[:, :], ROUND, None, ALU.subtract))
            link(nc.vector.tensor_tensor_scan(end[:, :], ones[:, 0:E], tiles[:, :], 0.0, ALU.mult, ALU.add))
            link(nc.vector.tensor_tensor(base[:, :], end[:, :], tiles[:, :], ALU.subtract))
            link(nc.vector.tensor_scalar(base[:, :], base[:, :], float(P), None, ALU.mult))
            link(nc.vector.tensor_tensor(upto[:, :, :], upto[:, :, :], count[:, :, :], ALU.subtract))
            link(nc.vector.tensor_tensor(rank[:, :, :], ps_rank[:, :, :], tile_major(upto), ALU.add))
            link(nc.vector.tensor_tensor(rank[:, :, :], rank[:, :, :], by_e(base[:, :], NT), ALU.add))
            link(nc.vector.tensor_tensor(rank[:, :, :], rank[:, :, :], chosen[:, :, :], ALU.mult))
            link(nc.vector.tensor_reduce(posf[:, :], rank[:, :, :], AX.X, ALU.add))
            nc.vector.tensor_copy(pos[:, :], posf[:, :]).then_inc(pos_ready, 1)
            link(nc.vector.tensor_tensor(ended[:, :, :],
                                         slot[:, :].rearrange("p (s e) -> p s e", e=1).broadcast_to([P, SLOTS, E - 1]),
                                         by_e(end[:, 0:E - 1], SLOTS), ALU.is_ge))
            link(nc.vector.tensor_reduce(expertf[:, :], ended[:, :, :], AX.X, ALU.add))
            link(nc.vector.tensor_copy(expert[:, :], expertf[:, :]))


def moe(nc, A, X, ident, ysort, zsort, pos, expert):
    E, DF = 8, 1024
    FC, HALF = DF // P, DF // 2
    with Stage(nc, "experts") as st:
        sb, ps, sem = st.sb, st.ps, st.sem
        w1, w2 = sb("w1", [P, E, DC, DF]), sb("w2", [P, E, FC, D])
        b1, b2 = sb("b1", [P, E, FC]), sb("b2", [P, E, D])
        b1_slot = sb("b1_slot", [P, 1, FC])
        g2, be2 = sb("g2", [P, D]), sb("be2", [P, D])
        y, yT = sb("y", [P, 2, D]), sb("yT", [P, D])
        h, hT = sb("h", [P, DF]), sb("hT", [P, DF])
        base, z = sb("base", [P, 2, D]), sb("z", [P, D])
        zout = sb("zout", [P, 2, D])
        stats, mv = sb("stats", [P, 1, 6]), sb("mv", [P, 1, 2])
        veps, logv, guess, tmp, rstd, pad = (sb(n, [P, 1]) for n in ("veps", "logv", "guess", "tmp", "rstd", "pad"))
        ps_h = [ps(f"h{k}", [P, HALF]) for k in range(2)]
        ps_hT = [ps(f"hT{k}", [P, HALF]) for k in range(2)]
        ps_y, ps_z = ps("y", [P, D]), ps("z", [P, D])

        loaded = sem("loaded")
        y_loaded = [sem(f"y_loaded{k}") for k in range(2)]
        y_turned, yT_ready, base_ready = sem("y_turned"), sem("yT_ready"), sem("base_ready")
        h_ps, h_ready, h_turned, hT_ready = sem("h_ps"), sem("h_ready"), sem("h_turned"), sem("hT_ready")
        z_ps, step = sem("z_ps"), sem("dve_step")
        var_ready, log_ready, guess_ready = sem("var_ready"), sem("log_ready"), sem("guess_ready")
        normed, scaled, zout_ready = sem("normed"), sem("scaled"), sem("zout_ready")
        stored = [sem(f"stored{k}") for k in range(2)]
        gathered, x_done = sem("gathered"), sem("x_done")
        GB = 2
        loads = [(w1, "w1"), (w2, "w2"), (b1, "b1"), (b2, "b2"), (g2, "g2"), (be2, "be2")]
        NLOAD = 16 * len(loads)
        block = st.block()

        def slots(eng, body):
            with eng.Fori(0, SLOTS // 2) as jj:
                for k in range(2):
                    body(jj * 2 + k, k, jj)

        @block.sync
        def _(sp):
            for dst, name in loads:
                sp.dma_start(whole(dst), A[f"moe_{name}"]).then_inc(loaded, 16)
            sp.wait_ge(loaded, NLOAD)
            for k in range(2):
                sp.dma_start(y[:, k, :], ysort[k * P:(k + 1) * P, :]).then_inc(y_loaded[k], 16)

            def body(j, k, fetch):
                if fetch:
                    sp.wait_ge(y_turned, j + 1)
                    sp.wait_ge(base_ready, j + 1)
                    sp.dma_start(y[:, k, :], ysort[bass.ds(j * P + 2 * P, P), :]).then_inc(y_loaded[k], 16)
                sp.wait_ge(zout_ready, j + 1)
                sp.dma_start(zsort[bass.ds(j * P, P), :], zout[:, k, :]).then_inc(stored[k], 16)

            with sp.Fori(0, SLOTS // 2 - 1) as jj:
                for k in range(2):
                    body(jj * 2 + k, k, True)
            for k in range(2):
                body(SLOTS - 2 + k, k, False)
            for k in range(2):
                sp.wait_ge(stored[k], 16 * (SLOTS // 2))

        @block.gpsimd
        def _(pool):
            pool.wait_ge(loaded, NLOAD)

            def scale(j):
                pool.wait_ge(normed, j + 1)
                nc.gpsimd.tensor_tensor(z[:, :], z[:, :], g2[:, :], ALU.mult).then_inc(scaled, 1)
                pool.wait_ge(scaled, j + 1)

            def body(j, k, jj):
                e = pool.value_load(expert[0:1, bass.ds(j, 1)], min_val=0, max_val=E - 1)
                pool.wait_ge(y_loaded[k], (jj + 1) * 16)
                nc.gpsimd.tensor_tensor(base[:, k, :].rearrange("p (a d) -> p a d", a=1),
                                        y[:, k, :].rearrange("p (a d) -> p a d", a=1),
                                        b2[:, bass.ds(e, 1), :], ALU.add).then_inc(base_ready, 1)
                scale(j)
                pool.wait_ge(stored[k], jj * 16)
                nc.gpsimd.tensor_tensor(zout[:, k, :], z[:, :], be2[:, :], ALU.add).then_inc(zout_ready, 1)

            with pool.Fori(0, SLOTS // 2) as jj:
                for k in range(2):
                    j = jj * 2 + k
                    body(j, k, jj)
            for k in range(2):
                pool.wait_ge(stored[k], 16 * (SLOTS // 2))
            for t in range(NT):
                if t >= GB:
                    pool.wait_ge(x_done, t - GB + 1)
                nc.gpsimd.indirect_dma_start(
                    base[:, t % GB, :], None, zsort,
                    bass.IndirectOffsetOnAxis(ap=pos[:, t:t + 1], axis=0)).then_inc(gathered, 16)
                pool.wait_ge(gathered, 16 * (t + 1))

        @block.scalar
        def _(act):
            def turn(j):
                act.wait_ge(y_turned, j + 1)
                nc.scalar.activation(yT[:, :], ps_y[:, :], ACT.Identity).then_inc(yT_ready, 1)

            def relu(j):
                for k in range(2):
                    act.wait_ge(h_turned, j * 2 + k + 1)
                    for c in range(k * FC // 2, (k + 1) * FC // 2):
                        ins = nc.scalar.activation(hT[:, c * P:(c + 1) * P], ps_hT[k][:, c * P - k * HALF:(c + 1) * P - k * HALF],
                                                   ACT.Relu, bias=b1_slot[:, 0, c:c + 1])
                    ins.then_inc(hT_ready, 1)

            def root(j):
                rsqrt_guess(nc, act, veps, 1, logv, guess, var_ready, log_ready, guess_ready, j + 1)

            turn(0)
            turn(1)
            relu(0)
            with act.Fori(1, SLOTS - 1) as j:
                root(j - 1)
                turn(j + 1)
                relu(j)
            root(SLOTS - 2)
            relu(SLOTS - 1)
            root(SLOTS - 1)

        @block.vector
        def _(dve):
            dve.wait_ge(loaded, NLOAD)

            def hidden(j):
                e = dve.value_load(expert[0:1, bass.ds(j, 1)], min_val=0, max_val=E - 1)
                if type(j) is not int or j:
                    dve.wait_ge(hT_ready, j * 2)
                nc.vector.tensor_scalar(b1_slot[:, :, :], b1[:, bass.ds(e, 1), :], 1.0, None, ALU.mult)
                for k in range(2):
                    dve.wait_ge(h_ps, j * 2 + k + 1)
                    nc.vector.tensor_copy(h[:, k * HALF:(k + 1) * HALF], ps_h[k][:, :]).then_inc(h_ready, 1)

            ch = Chain(dve, step, per=6)

            def finish(j, k):
                ch.start(j)
                dve.wait_ge(z_ps, j + 1)
                dve.wait_ge(base_ready, j + 1)
                if type(j) is not int or j:
                    dve.wait_ge(zout_ready, j)
                ch.link(nc.vector.tensor_tensor(z[:, :], ps_z[:, :], base[:, k, :], ALU.add))
                layer_norm_stats(nc, dve, ch, z[:, :].rearrange("p (a d) -> p a d", a=1), 1, stats, mv, veps,
                                 var_ready, j + 1, pad)
                rsqrt_refine(nc, dve, ch.link, veps, 1, guess, tmp, rstd, guess_ready, j + 1)
                nc.vector.tensor_scalar(z[:, :], z[:, :], mv[:, 0, 0:1], rstd[:, 0:1],
                                        ALU.subtract, ALU.mult).then_inc(normed, 1)
                ch.stop()

            hidden(0)
            with dve.Fori(0, SLOTS // 2 - 1) as jj:
                for k in range(2):
                    hidden(jj * 2 + k + 1)
                    finish(jj * 2 + k, k)
            hidden(SLOTS - 1)
            finish(SLOTS - 2, 0)
            finish(SLOTS - 1, 1)
            for t in range(NT):
                dve.wait_ge(gathered, 16 * (t + 1))
                nc.vector.tensor_tensor(X[:, t, :], X[:, t, :], base[:, t % GB, :], ALU.add).then_inc(x_done, 1)
            dve.wait_ge(x_done, NT)

        @block.tensor
        def _(pe):
            pe.wait_ge(loaded, NLOAD)

            def turn_y(j, k, n):
                pe.wait_ge(y_loaded[k], n * 16)
                if type(j) is not int or j:
                    pe.wait_ge(yT_ready, j)
                for c in range(DC):
                    mm = nc.tensor.transpose(ps_y[:, c * P:(c + 1) * P], y[:, k, c * P:(c + 1) * P], ident[:, :])
                mm.then_inc(y_turned, 1)

            def up(j):
                e = pe.value_load(expert[0:1, bass.ds(j, 1)], min_val=0, max_val=E - 1)
                pe.wait_ge(yT_ready, j + 1)
                for k in range(2):
                    if type(j) is not int or j:
                        pe.wait_ge(h_ready, j * 2 - 1 + k)
                    for c in range(DC):
                        mm = nc.tensor.matmul(ps_h[k][:, :], yT[:, c * P:(c + 1) * P],
                                              w1[:, bass.ds(e, 1), c, k * HALF:(k + 1) * HALF].rearrange("p a d -> p (a d)"),
                                              start=(c == 0), stop=(c == DC - 1))
                    mm.then_inc(h_ps, 1)

            def turn_h(j):
                for k in range(2):
                    pe.wait_ge(h_ready, j * 2 + k + 1)
                    if type(j) is not int or j:
                        pe.wait_ge(hT_ready, j * 2 - 1 + k)
                    for c in range(4):
                        mm = nc.tensor.transpose(ps_hT[k][:, c * P:(c + 1) * P],
                                                 h[:, k * HALF + c * P:k * HALF + (c + 1) * P], ident[:, :])
                    mm.then_inc(h_turned, 1)

            def down(j):
                e = pe.value_load(expert[0:1, bass.ds(j, 1)], min_val=0, max_val=E - 1)
                for k in range(2):
                    pe.wait_ge(hT_ready, j * 2 + k + 1)
                if type(j) is not int or j:
                    pe.wait_ge(var_ready, j)
                for c in range(FC):
                    mm = nc.tensor.matmul(ps_z[:, :], hT[:, c * P:(c + 1) * P],
                                          w2[:, bass.ds(e, 1), c, :].rearrange("p a d -> p (a d)"),
                                          start=(c == 0), stop=(c == FC - 1))
                mm.then_inc(z_ps, 1)

            turn_y(0, 0, 1)
            up(0)
            turn_y(1, 1, 1)
            turn_h(0)
            with pe.Fori(0, SLOTS // 2 - 1) as jj:
                for k in range(2):
                    j = jj * 2 + k + 1
                    up(j)
                    down(j - 1)
                    turn_y(j + 1, k, jj + 2)
                    turn_h(j)
            up(SLOTS - 1)
            down(SLOTS - 2)
            turn_h(SLOTS - 1)
            down(SLOTS - 1)


def store(nc, X, out, dealt):
    with Stage(nc, "store") as st:
        stored = st.sem("stored")
        block = st.block()

        @block.sync
        def _(sp):
            if dealt:
                for b in range(B):
                    sp.dma_start(out[b * S:(b + 1) * S, :].rearrange("(t q) d -> q t d", q=8),
                                 X[8 * b:8 * b + 8, :, :]).then_inc(stored, 16)
                sp.wait_ge(stored, 16 * B)
            else:
                sp.dma_start(out.rearrange("(n p) d -> p n d", p=P), X[:, :, :]).then_inc(stored, 16)
                sp.wait_ge(stored, 16)


STAGES = ("mamba", "cross0", "bitffn", "self1", "cross1", "moe")


def program(nc, A, out, stages=STAGES):
    with ExitStack() as ctx:
        X = ctx.enter_context(nc.sbuf_tensor("X", [P, NT, D], F32))
        ident = ctx.enter_context(nc.sbuf_tensor("ident", [P, P], F32))
        identb = ctx.enter_context(nc.sbuf_tensor("identb", [P, P], BF16))
        setup(nc, A, X, ident, identb)
        for kind in stages:
            if kind == "mamba":
                mamba(nc, A, X, ident, identb)
            elif kind == "bitffn":
                bitffn(nc, A, X, identb)
            elif kind == "moe":
                scratch = nc.dram_tensor("scratch", (B * S, D), F32).ap()
                ysort = nc.dram_tensor("ysort", (SLOTS * P, D), F32).ap()
                zsort = nc.dram_tensor("zsort", (SLOTS * P, D), F32).ap()
                to_positions(nc, X, scratch)
                pos = ctx.enter_context(nc.sbuf_tensor("pos", [P, NT], I32))
                expert = ctx.enter_context(nc.sbuf_tensor("expert", [P, SLOTS], I32))
                with nc.sbuf_tensor("Y", [P, NT, D], F32) as Y:
                    attention(nc, A, X, ident, "batch", Y)
                    route(nc, A, ident, Y, ysort, pos, expert)
                moe(nc, A, X, ident, ysort, zsort, pos, expert)
            else:
                attention(nc, A, X, ident, kind)
        store(nc, X, out, "moe" in stages)


def layout(inputs):
    import numpy as np

    a = {k: np.asarray(v) for k, v in inputs.items()}

    def rows(w):
        return np.ascontiguousarray(w.reshape(-1, P, w.shape[-1]).transpose(1, 0, 2))

    def cols(v):
        return np.ascontiguousarray(v.reshape(-1, P).T)

    def spread(v):
        return np.ascontiguousarray(np.broadcast_to(v.reshape(1, -1), (P, v.size)))

    def heads_last(w):
        return w.transpose(1, 0, 2).reshape(D, -1)

    o = {"x": a["x"].reshape(B * S, D)}
    w = {k[8:]: v for k, v in a.items() if k.startswith("L0_attn_")}
    xp = w["xp_w"].T
    o |= {
        "mb_in_w": rows(w["in_w"].T), "mb_out_w": rows(w["out_w"].T), "mb_xp_dt": rows(xp[:, :64]),
        "mb_xp_bc": rows(np.concatenate([xp[:, 64:]] * 3, axis=1)), "mb_dtp_w": np.ascontiguousarray(w["dtp_w"].T),
        "mb_ln_w": cols(w["ln_w"]), "mb_ln_b": cols(w["ln_b"]), "mb_in_b": cols(w["in_b"]),
        "mb_conv_w": rows(w["conv_w"][:, 0, :]), "mb_conv_b": cols(w["conv_b"]), "mb_dtp_b": cols(w["dtp_b"]),
        "mb_D": cols(w["D"]), "mb_A_log": rows(w["A_log"]), "mb_out_b": spread(w["out_b"]),
    }
    o["ctxT"] = rows(a["ctx_1024"].reshape(-1, D).T)
    o["c0_mask"] = np.ascontiguousarray(
        a["mask_Bx1xSxS2_bk0"].reshape(NT, P, -1).transpose(1, 0, 2))
    for pre, name, fix in (("c0", "L0_xattn", lambda m: m), ("c1", "L1_xattn", heads_last)):
        for k in "qkv":
            o[f"{pre}_w{k}" + ("" if k == "q" else "0")] = rows(fix(a[f"{name}_{'w' if pre == 'c0' else 'W'}{k}"]))
            v = a[f"{name}_b{k}"].reshape(-1)
            o[f"{pre}_b{k}"] = spread(v) if k == "v" else cols(v)
        o[f"{pre}_wo"] = rows(a[f"{name}_{'w' if pre == 'c0' else 'W'}o"])
        o[f"{pre}_bo"] = spread(a[f"{name}_bo"])
    o |= {"sa_wq": rows(a["L1_attn_Wq"]), "sa_wo": rows(a["L1_attn_Wo"])}
    for s, name in enumerate(("L1_attn_Wkv_short", "L1_attn_Wkv_long")):
        o |= {f"sa_wk{s}": rows(a[name][:, :D]), f"sa_wv{s}": rows(a[name][:, D:])}
    o["sa_mix"] = spread(np.stack([a["L1_attn_mix_weight"], a["L1_attn_decay_factor"]]))
    f = {k[7:]: v for k, v in a.items() if k.startswith("L0_ffn_")}
    o |= {"ff_w1": rows(f["w1"].T), "ff_w2": rows(f["w2"].T)}
    o |= {f"ff_{k}": spread(f[k]) for k in ("b1", "b2", "ln1_w", "ln1_b", "ln2_w", "ln2_b")}
    wqkv = a["L1_ffn_Wqkv"].T
    for k, name in enumerate(("wq", "wk0", "wv0")):
        o[f"ba_{name}"] = rows(wqkv[:, k * D:(k + 1) * D])
    bqkv = a["L1_ffn_bqkv"]
    o |= {"ba_bq": cols(bqkv[:D]), "ba_bk": cols(bqkv[D:2 * D]), "ba_bv": spread(bqkv[2 * D:]),
          "ba_wo": rows(a["L1_ffn_Wo"].T), "ba_bo": spread(a["L1_ffn_bo"]),
          "ba_g1": spread(a["L1_ffn_g1"]), "ba_be1": spread(a["L1_ffn_be1"]),
          "ba_mod8": (np.arange(P) % 8).astype(np.float32).reshape(P, 1)}
    m = {k[7:]: v for k, v in a.items() if k.startswith("L1_ffn_")}
    E = m["Wg"].shape[0]

    def per_expert(w):
        return np.ascontiguousarray(w.reshape(E, -1, P, w.shape[-1]).transpose(2, 0, 1, 3))

    def spread_all(v):
        return np.ascontiguousarray(np.broadcast_to(v[None], (P,) + v.shape))

    o |= {"moe_wg": rows(m["Wg"].T), "moe_w1": per_expert(m["W1"]), "moe_w2": per_expert(m["W2"]),
          "moe_b1": np.ascontiguousarray(m["b1"].reshape(E, -1, P).transpose(2, 0, 1)), "moe_b2": spread_all(m["b2"]),
          "moe_g2": spread(m["g2"]), "moe_be2": spread(m["be2"])}
    return o


def kernel(**inputs):
    import concourse.bacc as _bacc
    from concourse.bass_utils import run_bass_kernel_spmd as _run

    nc = _bacc.Bacc("TRN2", target_bir_lowering=False, num_devices=1)
    arrays, A = {}, {}
    for name, v in layout(inputs).items():
        arrays[f"in_{name}_dram"] = v
        A[name] = nc.dram_tensor(f"in_{name}_dram", v.shape, mybir.dt.from_np(v.dtype), kind="ExternalInput").ap()
    out = nc.dram_tensor("out_0_dram", (B * S, D), F32, kind="ExternalOutput").ap()
    program(nc, A, out)
    r = _run(nc, [arrays], core_ids=[0])
    return r.results[0]["out_0_dram"].reshape(B, S, D)
```

```python
from contextlib import ExitStack

import concourse.bass as bass
from concourse import mybir

F32 = mybir.dt.float32
BF16 = mybir.dt.bfloat16
I32 = mybir.dt.int32
U8 = mybir.dt.uint8
ALU = mybir.AluOpType
ACT = mybir.ActivationFunctionType
AX = mybir.AxisListType

P = 128
D = 256
DC = D // P
B, S = 16, 256
NT = B * S // P
EPS = 1e-5
SLOTS = NT + 7


class Stage:

    used = []

    def __init__(self, nc, name):
        self.nc, self.name, self.ctx = nc, name, ExitStack()

    def __enter__(self):
        self.ctx.__enter__()
        return self

    def __exit__(self, *a):
        return self.ctx.__exit__(*a)

    def sb(self, name, shape, dt=F32):
        return self.ctx.enter_context(self.nc.sbuf_tensor(f"{self.name}_{name}", shape, dt))

    def ps(self, name, shape, dt=F32):
        return self.ctx.enter_context(self.nc.psum_tensor(f"{self.name}_ps_{name}", shape, dt))

    def sem(self, name):
        s = self.ctx.enter_context(self.nc.semaphore(f"{self.name}_{name}"))
        self.used.append(s.num)
        return s

    def block(self):
        return self.ctx.enter_context(self.nc.Block())


def clear_semaphores(nc):
    nums = sorted(Stage.used)
    for lo in (n for n in nums if n - 1 not in nums):
        hi = lo
        while hi in nums:
            hi += 1
        nc.all_engine_barrier(sems_to_clear=range(lo, hi))
    Stage.used.clear()


class Chain:

    def __init__(self, eng, sem, per=0, base=0):
        self.eng, self.sem, self.per, self.n, self.i, self.base = eng, sem, per, 0, None, base

    def start(self, i):
        self.i, self.n = i, 0

    def mark(self, ins):
        self.n += 1
        ins.then_inc(self.sem, 1)

    def link(self, ins):
        self.mark(ins)
        at = self.n + self.base
        self.eng.wait_ge(self.sem, at if self.i is None else self.i * self.per + at)

    def stop(self):
        assert self.i is None or self.n == self.per, (self.n, self.per)


def layer_norm_stats(nc, ch, src, tiles, stats, mv, pad):
    for t in range(tiles):
        (ch.mark if t < tiles - 1 else ch.link)(nc.vector.bn_stats(stats[:, t, :], src[:, t, :]))
    nc.vector.memset(pad[:, :], 0.0)
    for t in range(tiles):
        (ch.mark if t < tiles - 1 else ch.link)(nc.vector.bn_aggr(mv[:, t, :], stats[:, t, :]))


ROOT_STEPS = 12


def inverse_root(nc, link, mv, tiles, veps, guess, tmp, rstd):
    bits = lambda v: v[:, 0:tiles].bitcast(I32)
    link(nc.vector.tensor_scalar(veps[:, 0:tiles], mv[:, 0:tiles, 1], EPS, None, ALU.add))
    link(nc.vector.tensor_scalar(bits(tmp), bits(veps), 1, None, ALU.arith_shift_right))
    link(nc.vector.tensor_scalar(bits(guess), bits(tmp), -1.0, float(0x5F3759DF), ALU.mult, ALU.add))
    for k in range(3):
        link(nc.vector.tensor_tensor(tmp[:, 0:tiles], guess[:, 0:tiles], guess[:, 0:tiles], ALU.mult))
        link(nc.vector.scalar_tensor_tensor(out=tmp[:, 0:tiles], in0=tmp[:, 0:tiles], scalar=-0.5,
                                            in1=veps[:, 0:tiles], op0=ALU.mult, op1=ALU.mult))
        link(nc.vector.scalar_tensor_tensor(out=(rstd if k == 2 else guess)[:, 0:tiles], in0=tmp[:, 0:tiles],
                                            scalar=1.5, in1=guess[:, 0:tiles], op0=ALU.add, op1=ALU.mult))


def normalize(nc, link, src, dst, tiles, mv, rstd):
    for t in range(tiles):
        link(nc.vector.tensor_scalar(dst[:, t, :], src[:, t, :], mv[:, t, 0:1], rstd[:, t:t + 1],
                                     ALU.subtract, ALU.mult))


def whole(t):
    return t[tuple(slice(None) for _ in t.shape)]


def setup(nc, A, X, ident, identb):
    with Stage(nc, "setup") as st:
        x_loaded, zeroed, made = st.sem("x_loaded"), st.sem("zeroed"), st.sem("made")
        block = st.block()

        @block.sync
        def _(sp):
            sp.dma_start(X[:, :, :], A["x"].rearrange("(n p) d -> p n d", p=P)).then_inc(x_loaded, 16)
            sp.wait_ge(x_loaded, 16)

        @block.gpsimd
        def _(pool):
            nc.gpsimd.memset(ident[:, :], 0.0).then_inc(zeroed, 1)
            nc.gpsimd.memset(identb[:, :], 0.0).then_inc(zeroed, 1)
            pool.wait_ge(zeroed, 2)
            for m in (ident, identb):
                nc.gpsimd.affine_select(out=m[:, :], in_=m[:, :], compare_op=ALU.not_equal, fill=1.0,
                                        base=0, pattern=[[-1, P]], channel_multiplier=1).then_inc(made, 1)
            pool.wait_ge(made, 2)


def mamba(nc, A, X, ident, identb):
    TT = 4
    N = TT * P
    ITER = NT // TT
    BB = N // S
    R, NS = 64, 16
    INNER = 512
    MC = INNER // P
    K = 4
    PAIR = 2
    PAIRS = NS // PAIR
    def spread_row(n):
        q, r = n // 4, n % 4
        return 2 * q + r if r < 2 else NS + 2 * q + r - 2

    RESET = 1.0e20
    with Stage(nc, "mamba") as st:
        sb, ps, sem = st.sb, st.ps, st.sem
        in_w = sb("in_w", [P, DC, 2 * INNER])
        out_w = sb("out_w", [P, MC, D])
        xp_dt = sb("xp_dt", [P, MC, R])
        xp_bc = sb("xp_bc", [P, MC, 96])
        dtp_w = sb("dtp_w", [R, INNER])
        ln_w, ln_b = sb("ln_w", [P, DC]), sb("ln_b", [P, DC])
        in_b = sb("in_b", [P, 2 * MC])
        conv_w, conv_b = sb("conv_w", [P, MC, K]), sb("conv_b", [P, MC])
        dtp_b, Dw = sb("dtp_b", [P, MC]), sb("Dw", [P, MC])
        a_log, neg_a, a = sb("a_log", [P, MC, NS]), sb("neg_a", [P, MC, NS]), sb("a", [P, MC, NS])
        out_b = sb("out_b", [P, D])
        sel = sb("sel", [96, 32, P], BF16)
        eps_t = sb("one", [P, 1])
        xt = sb("xt", [P, TT, D])
        hid = sb("hid", [P, TT, D])
        stats, mv = sb("stats", [P, TT, 6]), sb("mv", [P, TT, 2])
        veps, guess, tmp, rstd = (sb(n, [P, TT]) for n in ("veps", "guess", "tmp", "rstd"))
        hnT = sb("hnT", [P, DC, N])
        xpad = sb("xpad", [P, MC, BB, K - 1 + S])
        gate = sb("gate", [P, MC, N])
        xc = sb("xc", [P, MC, N])
        dtraw = sb("dtraw", [R, N])
        dt = sb("dt", [P, MC, N])
        dtx = sb("dtx", [P, MC, N])
        hn = dtx[:, 0:MC // 2, :].rearrange("p a (b d) -> p (a b) d", d=D)
        spa = sb("spa", [P, N])
        split2 = sb("split2", [96, N], BF16)
        parts = sb("parts", [96, N], BF16)
        bc = sb("bc", [P, 2 * NS, N])
        decay, u = sb("decay", [P, 2, PAIR, N]), sb("u", [P, 2, PAIR, N])
        h = sb("h", [P, 2, PAIR, N])
        resid = u[0:96, 0, 0, :]
        ps_ring = [ps(f"ring{k}", [P, N]) for k in range(4)]
        ps_y = [ps(f"y{k}", [P, N]) for k in range(2)]

        loaded = sem("loaded")
        sel_zero, sel_ready, a_exp, consts = sem("sel_zero"), sem("sel_ready"), sem("a_exp"), sem("consts")
        step, astep, pstep = sem("dve_step"), sem("act_step"), sem("pool_step")
        hn_ready, turned, hnT_ready = sem("hn_ready"), sem("turned"), sem("hnT_ready")
        proj_ready, proj_taken = sem("proj_ready"), sem("proj_taken")
        conv_ready, xc_ready = sem("conv_ready"), sem("xc_ready")
        bc_ps, parts_ready = sem("bc_ps"), sem("parts_ready")
        dtraw_ps, dtraw_ready = sem("dtraw_ps"), sem("dtraw_ready")
        spread, spread_taken = sem("spread"), sem("spread_taken")
        dt_ps, dt_log, dt_sum = sem("dt_ps"), sem("dt_log"), sem("dt_sum")
        dtx_ready, dt_reset = sem("dtx_ready"), sem("dt_reset")
        decay_ready, u_ready, h_ready, hc_ready = sem("decay_ready"), sem("u_ready"), sem("h_ready"), sem("hc_ready")
        hc_summed = sem("hc_summed")
        yg_ready, out_ready = sem("yg_ready"), sem("out_ready")
        base_ready, x_done = sem("base_ready"), sem("x_done")
        NLOAD = 14
        pad = sb("pad", [P, 1])
        block = st.block()

        @block.sync
        def _(sp):
            for dst, name in ((in_w, "mb_in_w"), (out_w, "mb_out_w"), (xp_dt, "mb_xp_dt"), (xp_bc, "mb_xp_bc"),
                              (dtp_w, "mb_dtp_w"), (ln_w, "mb_ln_w"), (ln_b, "mb_ln_b"), (in_b, "mb_in_b"),
                              (conv_w, "mb_conv_w"), (conv_b, "mb_conv_b"), (dtp_b, "mb_dtp_b"), (Dw, "mb_D"),
                              (a_log, "mb_A_log"), (out_b, "mb_out_b")):
                sp.dma_start(whole(dst), A[name]).then_inc(loaded, 16)
            sp.wait_ge(loaded, 16 * NLOAD)

        @block.gpsimd
        def _(pool):
            nc.gpsimd.memset(sel[:, :, :], 0.0).then_inc(sel_zero, 1)
            for j in range(3):
                pool.wait_ge(sel_zero, j + 1)
                nc.gpsimd.affine_select(out=sel[:, :, :], in_=sel[:, :, :], compare_op=ALU.not_equal, fill=1.0,
                                        base=-32 * j, pattern=[[-1, 32], [0, P]],
                                        channel_multiplier=1).then_inc(sel_zero, 1)
            pool.wait_ge(loaded, 16 * NLOAD)
            with pool.Fori(0, ITER) as i:
                for m in range(MC):
                    pool.wait_ge(dt_sum, i * MC + m + 1)
                    pool.wait_ge(xc_ready, i * MC + m + 1)
                    nc.gpsimd.tensor_tensor(dtx[:, m, :], dt[:, m, :], xc[:, m, :], ALU.mult).then_inc(dtx_ready, 1)
                pool.wait_ge(hn_ready, i + 1)
                nc.gpsimd.tensor_tensor(xt[:, :, :], xt[:, :, :], hid[:, :, :], ALU.add).then_inc(pstep, 1)
                pool.wait_ge(pstep, i + 1)
                nc.gpsimd.tensor_tensor(xt[:, :, :], xt[:, :, :],
                                        out_b[:, :].rearrange("p (a d) -> p a d", a=1).broadcast_to([P, TT, D]),
                                        ALU.add).then_inc(base_ready, 1)
                for m in range(MC):
                    pool.wait_ge(dtx_ready, i * MC + m + 1)
                    for k in range(PAIRS):
                        n = m * PAIRS + k
                        pool.wait_ge(spread_taken, i * 2 * NS + 4 * k + 2)
                        pool.wait_ge(h_ready, i * (MC * PAIRS) + n + 1)
                        nc.gpsimd.tensor_tensor(
                            u[:, n % 2, :, :],
                            dtx[:, m:m + 1, :].broadcast_to([P, PAIR, N]),
                            bc[:, PAIR * k:PAIR * (k + 1), :], ALU.mult).then_inc(u_ready, 1)

        @block.scalar
        def _(act):
            act.wait_ge(loaded, 16 * NLOAD)
            nc.scalar.activation(neg_a[:, :, :], a_log[:, :, :], ACT.Exp).then_inc(a_exp, 1)
            act.wait_ge(consts, 1)
            with act.Fori(0, ITER) as i:
                for c in range(DC):
                    act.wait_ge(turned, i * DC + c + 1)
                    nc.scalar.activation(hnT[:, c, :], ps_ring[c][:, :], ACT.Identity,
                                         bias=ln_b[:, c:c + 1], scale=ln_w[:, c:c + 1]).then_inc(hnT_ready, 1)
                for m in range(2 * MC):
                    act.wait_ge(proj_ready, i * 2 * MC + m + 1)
                    src = ps_ring[m % 4]
                    if m < MC:
                        nc.scalar.activation(xpad[:, m, :, K - 1:], src[:, :].rearrange("p (b s) -> p b s", b=BB),
                                             ACT.Identity, bias=in_b[:, m:m + 1]).then_inc(proj_taken, 1)
                    else:
                        nc.scalar.activation(gate[:, m - MC, :], src[:, :], ACT.Silu,
                                             bias=in_b[:, m:m + 1]).then_inc(proj_taken, 1)
                for m in range(MC):
                    act.wait_ge(conv_ready, i * MC + m + 1)
                    nc.scalar.activation(xc[:, m, :], dt[:, m, :], ACT.Silu).then_inc(xc_ready, 1)
                act.wait_ge(dtraw_ps, i + 1)
                nc.scalar.activation(dtraw[:, :], ps_ring[0][0:R, :], ACT.Identity).then_inc(dtraw_ready, 1)
                for m in range(MC):
                    act.wait_ge(dt_ps, i * MC + m + 1)
                    if m:
                        act.wait_ge(dt_sum, i * MC + m)
                    q = ps_ring[2 + m % 2]
                    nc.scalar.activation(spa[:, :], q[:, :], ACT.Abs, bias=dtp_b[:, m:m + 1]).then_inc(astep, 1)
                    nc.scalar.activation(dt[:, m, :], q[:, :], ACT.Relu, bias=dtp_b[:, m:m + 1]).then_inc(astep, 1)
                    act.wait_ge(astep, i * 3 * MC + 3 * m + 2)
                    nc.scalar.activation(spa[:, :], spa[:, :], ACT.Exp, scale=-1.0).then_inc(astep, 1)
                    act.wait_ge(astep, i * 3 * MC + 3 * m + 3)
                    nc.scalar.activation(spa[:, :], spa[:, :], ACT.Ln, bias=1.0).then_inc(dt_log, 1)
                act.wait_ge(dt_reset, i + 1)
                for m in range(MC):
                    for k in range(PAIRS):
                        n = m * PAIRS + k
                        for r in range(4 * k, 4 * k + 4) if m == 0 else ():
                            act.wait_ge(spread, i * 2 * NS + r + 1)
                            nc.scalar.activation(bc[:, spread_row(r), :], ps_ring[r % 4][:, :],
                                                 ACT.Identity).then_inc(spread_taken, 1)
                        act.wait_ge(h_ready, i * (MC * PAIRS) + n + 1)
                        for j in range(PAIR):
                            nc.scalar.activation(decay[:, n % 2, j, :], dt[:, m, :], ACT.Exp,
                                                 scale=a[:, m, PAIR * k + j:PAIR * k + j + 1]).then_inc(decay_ready, 1)

        @block.vector
        def _(dve):
            nc.vector.memset(xpad[:, :, :, 0:K - 1], 0.0)
            dve.wait_ge(a_exp, 1)
            nc.vector.tensor_scalar(a[:, :, :], neg_a[:, :, :], -1.0, None, ALU.mult).then_inc(consts, 1)
            nc.vector.memset(eps_t[:, :], 0.0).then_inc(h_ready, 2)
            dve.wait_ge(loaded, 16 * NLOAD)
            ch = Chain(dve, step, per=1 + 2 * (3 * TT + ROOT_STEPS) - 1 + MC * (K - 1) + 4 + MC)
            link = ch.link
            with dve.Fori(0, ITER) as i:
                ch.start(i)
                link(nc.vector.tensor_scalar(xt[:, :, :], X[:, bass.ds(i * TT, TT), :], 1.0, None, ALU.mult))
                src, dst = xt, hid
                for r in range(2):
                    layer_norm_stats(nc, ch, src, TT, stats, mv, pad)
                    inverse_root(nc, link, mv, TT, veps, guess, tmp, rstd)
                    if r == 0:
                        normalize(nc, link, src, dst, TT, mv, rstd)
                        src, dst = hid, hn
                    else:
                        for t in range(TT):
                            ins = nc.vector.tensor_scalar(dst[:, t, :], src[:, t, :], mv[:, t, 0:1], rstd[:, t:t + 1],
                                                          ALU.subtract, ALU.mult)
                            if t < TT - 1:
                                link(ins)
                            else:
                                ins.then_inc(hn_ready, 1)
                for m in range(MC):
                    dve.wait_ge(proj_taken, i * 2 * MC + m + 1)
                    z = dt[:, m, :].rearrange("p (b s) -> p b s", b=BB)
                    link(nc.vector.tensor_scalar(z, xpad[:, m, :, 0:S], conv_w[:, m, 0:1], conv_b[:, m:m + 1],
                                                 ALU.mult, ALU.add))
                    for k in range(1, K):
                        ins = nc.vector.scalar_tensor_tensor(out=z, in0=xpad[:, m, :, k:k + S],
                                                             scalar=conv_w[:, m, k:k + 1], in1=z,
                                                             op0=ALU.mult, op1=ALU.add)
                        if k < K - 1:
                            link(ins)
                        else:
                            ins.then_inc(conv_ready, 1)
                dve.wait_ge(bc_ps, i + 1)
                q = ps_ring[1]
                link(nc.vector.tensor_copy(parts[:, :], q[0:96, :]))
                link(nc.vector.tensor_tensor(resid[:, :], q[0:96, :], parts[:, :], ALU.subtract))
                link(nc.vector.tensor_copy(split2[:, :], resid[:, :]))
                link(nc.vector.tensor_copy(parts[32:64, :], split2[32:64, :]))
                nc.vector.tensor_tensor(parts[64:96, :], resid[64:96, :], split2[64:96, :],
                                        ALU.subtract).then_inc(parts_ready, 1)
                for m in range(MC):
                    dve.wait_ge(dt_log, i * MC + m + 1)
                    nc.vector.tensor_tensor(dt[:, m, :], dt[:, m, :], spa[:, :], ALU.add).then_inc(dt_sum, 1)
                dve.wait_ge(dtx_ready, (i + 1) * MC)
                nc.vector.memset(dt[:, :, 0:N:S], RESET).then_inc(dt_reset, 1)
                for m in range(MC):
                    for k in range(PAIRS):
                        n = m * PAIRS + k
                        nn = i * (MC * PAIRS) + n
                        dve.wait_ge(decay_ready, PAIR * (nn + 1))
                        dve.wait_ge(u_ready, nn + 1)
                        if n >= 2:
                            dve.wait_ge(hc_summed, nn - 1)
                        flat = lambda x: x[:, n % 2, :, :].rearrange("p a b -> p (a b)")
                        nc.vector.tensor_tensor_scan(flat(h), flat(decay), flat(u), 0.0, ALU.mult,
                                                     ALU.add).then_inc(h_ready, 1)
                        dve.wait_ge(h_ready, nn + 3)
                        if m == 0:
                            dve.wait_ge(spread_taken, i * 2 * NS + 4 * k + 4)
                        nc.vector.tensor_tensor(h[:, n % 2, :, :], h[:, n % 2, :, :],
                                                bc[:, NS + PAIR * k:NS + PAIR * (k + 1), :],
                                                ALU.mult).then_inc(hc_ready, 1)
                    dve.wait_ge(hc_summed, i * (MC * PAIRS) + (m + 1) * PAIRS)
                    link(nc.vector.scalar_tensor_tensor(out=xc[:, m, :], in0=xc[:, m, :], scalar=Dw[:, m:m + 1],
                                                        in1=ps_y[m % 2][:, :], op0=ALU.mult, op1=ALU.add))
                    nc.vector.tensor_tensor(xc[:, m, :], xc[:, m, :], gate[:, m, :], ALU.mult).then_inc(yg_ready, 1)
                dve.wait_ge(base_ready, i + 1)
                for p in range(2):
                    dve.wait_ge(out_ready, i * 2 + p + 1)
                    nc.vector.tensor_tensor(X[:, bass.ds(i * TT + 2 * p, 2), :], xt[:, 2 * p:2 * p + 2, :],
                                            ps_ring[p][:, :].rearrange("p (t d) -> p t d", t=2),
                                            ALU.add).then_inc(x_done, 1)
                dve.wait_ge(x_done, (i + 1) * 2)
                ch.stop()

        @block.tensor
        def _(pe):
            def spread_pair(i, k):
                for n in range(4 * k, 4 * k + 4):
                    if n >= 4:
                        pe.wait_ge(spread_taken, i * 2 * NS + n - 3)
                    nc.tensor.matmul(ps_ring[n % 4][:, :], sel[:, spread_row(n), :], parts[:, :],
                                     start=True, stop=True).then_inc(spread, 1)

            pe.wait_ge(loaded, 16 * NLOAD)
            pe.wait_ge(sel_zero, 4)
            with pe.Fori(0, ITER) as i:
                pe.wait_ge(hn_ready, i + 1)
                for c in range(DC):
                    for t in range(TT):
                        mm = nc.tensor.transpose(ps_ring[c][:, t * P:(t + 1) * P], hn[:, t, c * P:(c + 1) * P],
                                                 ident[:, :])
                    mm.then_inc(turned, 1)
                pe.wait_ge(hnT_ready, (i + 1) * DC)
                for m in range(2 * MC):
                    if m >= 4:
                        pe.wait_ge(proj_taken, i * 2 * MC + m - 3)
                    for c in range(DC):
                        mm = nc.tensor.matmul(ps_ring[m % 4][:, :], in_w[:, c, m * P:(m + 1) * P], hnT[:, c, :],
                                              start=(c == 0), stop=(c == DC - 1))
                    mm.then_inc(proj_ready, 1)
                pe.wait_ge(proj_taken, (i + 1) * 2 * MC)
                pe.wait_ge(xc_ready, (i + 1) * MC)
                for m in range(MC):
                    mm = nc.tensor.matmul(ps_ring[0][0:R, :], xp_dt[:, m, :], xc[:, m, :],
                                          start=(m == 0), stop=(m == MC - 1))
                mm.then_inc(dtraw_ps, 1)
                for m in range(MC):
                    mm = nc.tensor.matmul(ps_ring[1][0:96, :], xp_bc[:, m, :], xc[:, m, :],
                                          start=(m == 0), stop=(m == MC - 1))
                mm.then_inc(bc_ps, 1)
                pe.wait_ge(dtraw_ready, i + 1)
                for m in range(MC):
                    if m >= 2:
                        pe.wait_ge(dt_log, i * MC + m - 1)
                    nc.tensor.matmul(ps_ring[2 + m % 2][:, :], dtp_w[:, m * P:(m + 1) * P], dtraw[:, :],
                                     start=True, stop=True).then_inc(dt_ps, 1)
                pe.wait_ge(parts_ready, i + 1)
                pe.wait_ge(dt_log, (i + 1) * MC)
                spread_pair(i, 0)
                spread_pair(i, 1)
                for m in range(MC):
                    for k in range(PAIRS):
                        n = m * PAIRS + k
                        pe.wait_ge(hc_ready, i * (MC * PAIRS) + n + 1)
                        if k == 0 and m >= 2:
                            pe.wait_ge(yg_ready, i * MC + m - 1)
                        for j in range(PAIR):
                            mm = nc.tensor.matmul(ps_y[m % 2][:, :], ident[:, :], h[:, n % 2, j, :],
                                                  start=(k == 0 and j == 0), stop=(k == PAIRS - 1 and j == PAIR - 1))
                        mm.then_inc(hc_summed, 1)
                        if m == 0 and k + 2 < PAIRS:
                            spread_pair(i, k + 2)
                pe.wait_ge(spread_taken, (i + 1) * 2 * NS)
                pe.wait_ge(yg_ready, (i + 1) * MC)
                for p in range(2):
                    for t in range(2):
                        for m in range(MC):
                            mm = nc.tensor.matmul(ps_ring[p][:, t * D:(t + 1) * D],
                                                  xc[:, m, (2 * p + t) * P:(2 * p + t + 1) * P], out_w[:, m, :],
                                                  start=(m == 0), stop=(m == MC - 1))
                    mm.then_inc(out_ready, 1)


def attention(nc, A, X, ident, kind, Y=None):
    LT = 2
    ITER = NT // LT
    HD = 64 if kind == "batch" else 16
    NH = D // HD
    HC = P // HD
    NK = {"self1": 256, "batch": P}.get(kind, 120)
    SETS = 2 if kind in ("self1", "batch") else 1
    UNITS = {"self1": [(0, 0), (0, 1), (1, 0), (1, 1)], "batch": [(0, 0), (1, 1)]}.get(kind, [(0, 0), (1, 0)])
    KC = -(-NK // P)
    KP = min(NK, P)
    GH = 4 // KC
    GU = NH // GH
    U = len(UNITS)
    G = U * GU
    SCALE = HD ** -0.5
    cross = kind.startswith("cross")
    has_bias = kind in ("cross0", "self1", "batch")
    pre = {"cross0": "c0", "cross1": "c1", "self1": "sa", "batch": "ba"}[kind]
    MASKED = 1.0e30
    LAGT, LAGW = 3, 4
    NP = LAGT + 1
    NB = 4 if kind == "batch" else 2

    with Stage(nc, kind) as st:
        sb, ps, sem = st.sb, st.ps, st.sem
        wq, wo = sb("wq", [P, DC, D]), sb("wo", [P, DC, D])
        wk = [sb(f"wk{s}", [P, DC, D]) for s in range(SETS if kind == "self1" else 1)]
        wv = [sb(f"wv{s}", [P, DC, D]) for s in range(SETS if kind == "self1" else 1)]
        loads = [(wq, "wq"), (wo, "wo")] + [(w, f"wk{s}") for s, w in enumerate(wk)] + [(w, f"wv{s}") for s, w in enumerate(wv)]
        if kind != "self1":
            bq, bk, bv, bo = sb("bq", [P, DC]), sb("bk", [P, DC]), sb("bv", [P, D]), sb("bo", [P, D])
            loads += [(bq, "bq"), (bk, "bk"), (bv, "bv"), (bo, "bo")]
        else:
            mix = sb("mix", [P, 2])
            share = sb("share", [P, 2])
            neg_rate = sb("neg_rate", [P, 1])
            small = sb("small", [P, 2])
            loads += [(mix, "mix")]
        if kind == "batch":
            g1, be1 = sb("g1", [P, D]), sb("be1", [P, D])
            mod8 = sb("mod8", [P, 1])
            loads += [(g1, "g1"), (be1, "be1"), (mod8, "mod8")]
        xt, xn = sb("xt", [P, LT, D]), sb("xn", [P, LT, D])
        stats, mv = sb("stats", [P, LT, 6]), sb("mv", [P, LT, 2])
        veps, guess, tmp, rstd = (sb(n, [P, LT]) for n in ("veps", "guess", "tmp", "rstd"))
        xnT, qT = sb("xnT", [P, DC, LT * P]), [sb(f"qT{k}", [P, DC, LT * P]) for k in range(NB)]
        kT = [sb(f"kT{s}", [P, DC, NK]) for s in range(SETS)]
        kz = [[sb(f"kz{s}{k}", [P, DC, HC, NK]) for k in range(NB)] for s in range(SETS)]
        V = [[sb(f"V{s}{k}", [P, KC, NH, HD + 1]) for k in range(NB)] for s in range(SETS)]
        if cross:
            ctxT = sb("ctxT", [P, 2, DC, NK])
        if kind == "cross0":
            mask8 = sb("mask8", [P, 2, LT, NK], U8)
        if has_bias:
            biases = [sb(f"bias{k}", [P, LT, NK]) for k in range(2 if kind == "cross0" else 1)]
            bias = biases[0]
            biased = sb("biased", [P, 3, GH, NK])
        top, ntop = sb("top", [P, G * GH]), sb("ntop", [P, G * GH])
        prob = sb("prob", [P, NP, GH, NK])
        pT = sb("pT", [P, 2, 4, P])
        inv = sb("inv", [P, 2, NH])
        ao, aob, aoT = sb("ao", [P, LT, D]), sb("aob", [P, D]), sb("aoT", [P, DC, P])
        if kind == "batch":
            total = sb("total", [P, 1, D])
            stats2, mv2 = sb("stats2", [P, 1, 6]), sb("mv2", [P, 1, 2])
            veps2, guess2, tmp2, rstd2, pad2 = (sb(n, [P, 1]) for n in ("veps2", "guess2", "tmp2", "rstd2", "pad2"))
        ps_s = [ps(f"s{k}", [P, 512]) for k in range(2)]
        ps_t = [ps(f"t{k}", [P, 512]) for k in range(2)]
        ps_o = [ps(f"o{k}", [P, 512]) for k in range(2)]
        ps_w = ps("w", [P, 512])
        ps_f = ps("f", [P, 512])

        loaded, ready0, kzeroed = sem("loaded"), sem("ready0"), sem("kzeroed")
        ctx_loaded = [sem(f"ctx_loaded{k}") for k in range(2)]
        made = sem("made")
        step, fstep, ustep, tstep = sem("dve_step"), sem("dve_front_step"), sem("dve_unit_step"), sem("dve_tail_step")
        y_done = sem("y_done")
        xn_ready, turned, xnT_ready = sem("xn_ready"), sem("turned"), sem("xnT_ready")
        q_ps, q_ready = sem("q_ps"), sem("q_ready")
        k_ps, kT_ready, kz_ready = sem("k_ps"), sem("kT_ready"), sem("kz_ready")
        v_ps, v_ready = sem("v_ps"), sem("v_ready")
        scored, top_ready, prob_ready = sem("scored"), sem("top_ready"), sem("prob_ready")
        prob_turned = sem("prob_turned")
        pT_even, pT_odd = sem("pT_even"), sem("pT_odd")
        bias_ready = sem("bias_ready")
        sums_read = sem("sums_read")
        weighed, ao_ready = sem("weighed"), sem("ao_ready")
        ao_turned, aoT_ready, out_ps = sem("ao_turned"), sem("aoT_ready"), sem("out_ps")
        base_ready, x_done = sem("base_ready"), sem("x_done")
        NLOAD = 16 * len(loads)
        NDMA = HC * SETS
        pad = sb("pad", [P, 1])
        block = st.block()

        def tile_ends(u):
            return u == U - 1 or UNITS[u + 1][0] != UNITS[u][0]

        ENDS = [u for u in range(U) if tile_ends(u)]
        FRONT_STEPS = 1 + 2 * LT + ROOT_STEPS + LT - 1
        SCORE_STEPS = {"cross0": G, "cross1": 0, "self1": G // 2, "batch": G}[kind]
        UNIT_STEPS = 2 if kind == "self1" else 1
        TAIL_STEPS = LT * (2 + ROOT_STEPS + 2) if kind == "batch" else 0
        at = lambda x: int(x * G)
        F_NORM = 0
        F_TURN = at(0.25)
        F_KEYS = [at(0.0 if cross else 0.35 + 0.1 * s) for s in range(SETS)]
        F_QUERIES = at(0.55)
        F_VALUES = [at(0.65 + 0.1 * s) for s in range(SETS)]
        E_UNIT = [(u + 1) * GU - 1 + LAGW for u in range(U)]
        E_TILE = [(u + 1) * GU - 1 + LAGW for u in ENDS]
        LATE = max(E_TILE) + 4
        DEPTH = LATE // G + 1
        FIRST = -(-DEPTH // NB) * NB
        LOOPS = (ITER - 1 - FIRST) // NB

        def after(eng, sem, value):
            if type(value) is not int or value > 0:
                eng.wait_ge(sem, value)

        def context_count(i, k):
            per = 32 if kind == "cross0" else 16
            if type(i) is int:
                return (i // 2 + 1) * per
            return (i - k) * (per // 2) + per

        DEPTHS = range(DEPTH, -1, -1) if kind == "batch" else range(DEPTH + 1)
        E_ADD = 2 if kind == "batch" else 3

        def run(eng, front, group, tail):
            def body(j, jk, here):
                for g in range(G):
                    if here < ITER:
                        group(j, jk, g)
                    if here < ITER - 1:
                        front(j + 1, (jk + 1) % NB, g)
                    for d in DEPTHS:
                        if 0 <= here - d < ITER:
                            tail(j - d, (jk - d) % NB, d * G + g)

            for g in range(G):
                front(0, 0, g)
            for j in range(FIRST):
                body(j, j % NB, j)
            with eng.Fori(0, LOOPS) as jj:
                for k in range(NB):
                    body(jj * NB + FIRST + k, k, FIRST + k)
            for j in range(FIRST + LOOPS * NB, ITER + DEPTH):
                body(j, j % NB, j)

        @block.sync
        def _(sp):
            for dst, name in loads:
                sp.dma_start(whole(dst), A[f"{pre}_{name}"]).then_inc(loaded, 16)
            sp.wait_ge(kzeroed, NB * SETS + 1)

            def fetch(b, k):
                sp.dma_start(ctxT[:, k, :, :], A["ctxT"][:, :, bass.ds(b * NK, NK)]).then_inc(ctx_loaded[k], 16)
                if kind == "cross0":
                    sp.dma_start(mask8[:, k, :, :],
                                 A["c0_mask"][:, bass.ds(b * LT, LT), :]).then_inc(ctx_loaded[k], 16)

            def body(i, k, first=False, more=True):
                sp.wait_ge(kT_ready, (i + 1) * SETS * DC)
                if not first:
                    sp.wait_ge(scored, (i - NB + 1) * G)
                for s in range(SETS):
                    for h in range(HC):
                        rows = slice(HD * h, HD * h + HD)
                        sp.dma_start(kz[s][k][rows, :, h, :], kT[s][rows, :, :]).then_inc(kz_ready, 16)
                if cross and more:
                    sp.wait_ge(v_ps, (i + 1) * SETS * KC)
                    sp.wait_ge(k_ps, (i + 1) * SETS * DC)
                    if kind == "cross0":
                        sp.wait_ge(bias_ready, i + 1)
                    fetch(i + 2, k)

            if cross:
                fetch(0, 0)
                fetch(1, 1)
            for i in range(NB):
                body(i, i, first=True)
            with sp.Fori(0, ITER // NB - 2) as ii:
                for k in range(NB):
                    body(ii * NB + NB + k, k)
            for k in range(NB):
                body(ITER - NB + k, k, more=False)
            sp.wait_ge(loaded, NLOAD)
            sp.wait_ge(kz_ready, 16 * NDMA * ITER)

        @block.gpsimd
        def _(pool):
            for s in range(SETS):
                for k in range(NB):
                    nc.gpsimd.memset(whole(kz[s][k]), 0.0).then_inc(kzeroed, 1)
            if kind == "self1":
                nc.gpsimd.iota(bias[:, :, :], [[-P, LT], [1, NK]], base=0, channel_multiplier=-1,
                               allow_small_or_imprecise_dtypes=True).then_inc(kzeroed, 1)
            elif kind == "batch":
                ids = biased[:, 0:1, 0, :].rearrange("p a k -> p (a k)")
                nc.gpsimd.iota(ids.rearrange("p (b q) -> p b q", q=8), [[0, 16], [1, 8]], base=0,
                               channel_multiplier=0, allow_small_or_imprecise_dtypes=True).then_inc(kzeroed, 1)
            else:
                nc.gpsimd.memset(ao[:, 0, 0:1], 0.0).then_inc(kzeroed, 1)
            pool.wait_ge(loaded, NLOAD)
            if kind != "self1":
                with pool.Fori(0, ITER) as i:
                    pool.wait_ge(xn_ready, i + 1)
                    there = (Y if kind == "batch" else X)[:, bass.ds(i * LT, LT), :]
                    nc.gpsimd.tensor_tensor(there, xn[:, :, :] if kind == "batch" else there,
                                            bo[:, :].rearrange("p (a d) -> p a d", a=1).broadcast_to([P, LT, D]),
                                            ALU.add).then_inc(base_ready, 1)

        @block.scalar
        def _(act):
            act.wait_ge(loaded, NLOAD)
            if kind == "self1":
                nc.scalar.activation(small[:, 0:1], mix[:, 0:1], ACT.Exp, scale=-1.0).then_inc(ready0, 1)

            def front(i, k, g):
                if g == F_TURN:
                    act.wait_ge(turned, i + 1)
                    after(act, v_ps, i * SETS * KC)
                    nc.scalar.activation(xnT[:, :, :], ps_f[:, :].rearrange("p (c n) -> p c n", c=DC),
                                         ACT.Identity).then_inc(xnT_ready, 1)
                for s in range(SETS):
                    if g == F_KEYS[s]:
                        act.wait_ge(k_ps, i * SETS * DC + DC * (s + 1))
                        after(act, kz_ready, i * NDMA * 16)
                        for m in range(DC):
                            kw = {} if kind == "self1" else {"bias": bk[:, m:m + 1]}
                            nc.scalar.activation(kT[s][:, m, :], ps_f[:, m * 256:m * 256 + NK], ACT.Identity,
                                                 **kw).then_inc(kT_ready, 1)

            def group(i, k, g):
                act.wait_ge(top_ready, i * G + g + 1)
                after(act, prob_turned, i * G + g - NP + 1)
                for h in range(GH):
                    src = (biased[:, g % 2, h, :] if has_bias and (kind != "self1" or UNITS[g // GU][1] == 0)
                           else ps_s[g % 2][:, h * NK:(h + 1) * NK])
                    ins = nc.scalar.activation(prob[:, (k * G + g) % NP, h, :], src, ACT.Exp,
                                               bias=ntop[:, g * GH + h:g * GH + h + 1])
                ins.then_inc(prob_ready, 1)

            def tail(i, k, t):
                e = t - LAGT
                if 0 <= e < G and e % 2:
                    act.wait_ge(prob_turned, i * G + e + 1)
                    after(act, weighed, i * G + e - 1)
                    nc.scalar.activation(pT[0:KP, e % 2, :, :],
                                         ps_t[e % 2][0:KP, :].rearrange("p (j n) -> p j n", j=4),
                                         ACT.Identity).then_inc(pT_odd, 1)
                for n, at_end in enumerate(E_TILE):
                    if t == at_end + 1:
                        act.wait_ge(ao_turned, i * LT + n + 1)
                        nc.scalar.activation(aoT[:, :, :], ps_w[:, 0:D].rearrange("p (c n) -> p c n", c=DC),
                                             ACT.Identity).then_inc(aoT_ready, 1)

            run(act, front, group, tail)

        @block.vector
        def _(dve):
            for s in range(SETS):
                for k in range(NB):
                    nc.vector.memset(V[s][k][:, :, :, HD:HD + 1], 1.0).then_inc(made, 1)
            nc.vector.memset(top[:, :], 0.0)
            dve.wait_ge(loaded, NLOAD)
            ch0 = Chain(dve, step)
            if kind == "self1":
                dve.wait_ge(ready0, 1)
                ch0.link(nc.vector.tensor_scalar(small[:, 1:2], small[:, 0:1], 1.0, None, ALU.add))
                ch0.link(nc.vector.reciprocal(share[:, 0:1], small[:, 1:2]))
                ch0.link(nc.vector.tensor_scalar(share[:, 1:2], share[:, 0:1], -1.0, 1.0, ALU.mult, ALU.add))
                ch0.link(nc.vector.tensor_scalar(small[:, 0:1], mix[:, 1:2], -1.0, 1.0, ALU.mult, ALU.add))
                ch0.link(nc.vector.tensor_scalar(neg_rate[:, :], small[:, 0:1], -1.0, None, ALU.mult))
                dve.wait_ge(kzeroed, NB * SETS + 1)
                dist = biased[:, 0:2, 0, :]
                ch0.link(nc.vector.scalar_tensor_tensor(out=dist, in0=bias[:, :, :], scalar=-1.0, in1=bias[:, :, :],
                                                        op0=ALU.mult, op1=ALU.max))
                ch0.link(nc.vector.tensor_scalar(bias[:, :, :], dist, neg_rate[:, 0:1], None, ALU.mult))
            elif kind == "batch":
                dve.wait_ge(kzeroed, NB * SETS + 1)
                ch0.link(nc.vector.tensor_scalar(bias[:, 0, :], biased[:, 0, 0, :], mod8[:, 0:1], None, ALU.is_equal))
                ch0.link(nc.vector.tensor_scalar(bias[:, 0, :], bias[:, 0, :], MASKED, -MASKED, ALU.mult, ALU.add))
                ch0.link(nc.vector.tensor_copy(bias[:, 1, :], bias[:, 0, :]))
            fch = Chain(dve, fstep, per=FRONT_STEPS)
            sch = Chain(dve, step, per=SCORE_STEPS, base=ch0.n)
            uch = Chain(dve, ustep, per=U * UNIT_STEPS)
            tch = Chain(dve, tstep, per=TAIL_STEPS)

            def front(i, k, g):
                if g == 0:
                    fch.start(i)
                if g == F_NORM:
                    fch.link(nc.vector.tensor_scalar(xt[:, :, :], X[:, bass.ds(i * LT, LT), :], 1.0, None, ALU.mult))
                    layer_norm_stats(nc, fch, xt, LT, stats, mv, pad)
                    inverse_root(nc, fch.link, mv, LT, veps, guess, tmp, rstd)
                    after(dve, turned, i)
                    if kind != "self1":
                        after(dve, base_ready, i)
                    for t in range(LT):
                        ins = nc.vector.tensor_scalar(xn[:, t, :], xt[:, t, :], mv[:, t, 0:1], rstd[:, t:t + 1],
                                                      ALU.subtract, ALU.mult)
                        if t < LT - 1:
                            fch.link(ins)
                        else:
                            ins.then_inc(xn_ready, 1)
                if g == F_TURN and kind == "cross0":
                    dve.wait_ge(ctx_loaded[k], context_count(i, k))
                    nc.vector.tensor_scalar(biases[k][:, :, :], mask8[:, k, :, :], MASKED, -MASKED,
                                            ALU.mult, ALU.add).then_inc(bias_ready, 1)
                if g == F_QUERIES:
                    dve.wait_ge(q_ps, (i + 1) * DC)
                    for m in range(DC):
                        src = ps_f[:, m * LT * P:(m + 1) * LT * P]
                        if kind == "self1":
                            nc.vector.tensor_scalar(qT[k][:, m, :], src, SCALE, None, ALU.mult).then_inc(q_ready, 1)
                        else:
                            nc.vector.tensor_scalar(qT[k][:, m, :], src, bq[:, m:m + 1], SCALE, ALU.add,
                                                    ALU.mult).then_inc(q_ready, 1)
                for s in range(SETS):
                    if g == F_VALUES[s]:
                        dve.wait_ge(v_ps, i * SETS * KC + (s + 1) * KC)
                        after(dve, weighed, (i - NB + 1) * G)
                        for c in range(KC):
                            src = ps_f[0:KP, c * D:(c + 1) * D].rearrange("p (h e) -> p h e", h=NH)
                            dst = V[s][k][0:KP, c, :, 0:HD]
                            if kind == "self1":
                                nc.vector.tensor_copy(dst, src).then_inc(v_ready, 1)
                            else:
                                nc.vector.tensor_tensor(dst, src, bv[0:KP, :].rearrange("p (h e) -> p h e", h=NH),
                                                        ALU.add).then_inc(v_ready, 1)
                if g == G - 1:
                    fch.stop()

            def group(i, k, g):
                if g == 0:
                    sch.start(i)
                t, s = UNITS[g // GU]
                dve.wait_ge(scored, i * G + g + 1)
                if has_bias and (kind != "self1" or s == 0):
                    after(dve, prob_ready, i * G + g - 1)
                    if g == 0 and kind == "cross0":
                        dve.wait_ge(bias_ready, i + 1)
                    nc.vector.memset(pad[:, :], 0.0)
                    for h in range(GH):
                        ins = nc.vector.tensor_tensor_reduce(
                            out=biased[:, g % 2, h, :], in0=ps_s[g % 2][:, h * NK:(h + 1) * NK],
                            in1=biases[k if kind == "cross0" else 0][:, t, :], scale=1.0, scalar=-3.0e38,
                            op0=ALU.add, op1=ALU.max, accum_out=top[:, g * GH + h:g * GH + h + 1])
                    sch.link(ins)
                    nc.vector.tensor_scalar(ntop[:, g * GH:(g + 1) * GH], top[:, g * GH:(g + 1) * GH],
                                            -1.0, None, ALU.mult).then_inc(top_ready, 1)
                else:
                    nc.vector.tensor_reduce(ntop[:, g * GH:(g + 1) * GH],
                                            ps_s[g % 2][:, 0:GH * NK].rearrange("p (h k) -> p h k", h=GH),
                                            AX.X, ALU.max, negate=True).then_inc(top_ready, 1)
                if g == G - 1:
                    sch.stop()

            def tail(i, k, t):
                e = t - LAGT
                if 0 <= e < G and e % 2 == 0:
                    dve.wait_ge(prob_turned, i * G + e + 1)
                    after(dve, weighed, i * G + e - 1)
                    nc.vector.tensor_copy(pT[0:KP, e % 2, :, :],
                                          ps_t[e % 2][0:KP, :].rearrange("p (j n) -> p j n", j=4)).then_inc(pT_even, 1)
                for n, at_end in enumerate(E_TILE):
                    if t == at_end + E_ADD:
                        dve.wait_ge(out_ps, i * LT + n + 1)
                        if n == 0 and kind != "self1":
                            dve.wait_ge(base_ready, i + 1)
                        if kind == "batch":
                            after(dve, y_done, i * LT + n)
                        R = (Y if kind == "batch" else X)[:, bass.ds(i * LT + n, 1), :]
                        o = ps_w[:, D:2 * D].rearrange("p (a d) -> p a d", a=1)
                        nc.vector.tensor_tensor(total[:, :, :] if kind == "batch" else R, R, o, ALU.add).then_inc(x_done, 1)
                        if kind == "batch":
                            dve.wait_ge(x_done, i * LT + n + 1)
                            tch.start(i)
                            tch.n = n * (TAIL_STEPS // LT)
                            layer_norm_stats(nc, tch, total, 1, stats2, mv2, pad2)
                            inverse_root(nc, tch.link, mv2, 1, veps2, guess2, tmp2, rstd2)
                            tch.link(nc.vector.tensor_scalar(total[:, 0, :], total[:, 0, :], mv2[:, 0, 0:1], rstd2[:, 0:1],
                                                             ALU.subtract, ALU.mult))
                            g1b = g1[:, :].rearrange("p (a d) -> p a d", a=1)
                            tch.link(nc.vector.tensor_tensor(total[:, :, :], total[:, :, :], g1b, ALU.mult))
                            nc.vector.tensor_tensor(R, total[:, :, :], be1[:, :].rearrange("p (a d) -> p a d", a=1),
                                                    ALU.add).then_inc(y_done, 1)
                for u in range(U):
                    if t == E_UNIT[u]:
                        normalize_unit(i, u)

            def normalize_unit(i, u):
                t, s = UNITS[u]
                o = ps_o[u % 2][:, 0:NH * (HD + 1)].rearrange("p (h e) -> p h e", h=NH)
                dve.wait_ge(weighed, i * G + (u + 1) * GU)
                uch.start(i)
                uch.n = u * UNIT_STEPS
                uch.link(nc.vector.reciprocal(inv[:, u % 2, :].rearrange("p (h e) -> p h e", e=1), o[:, :, HD:HD + 1]))
                if kind == "self1":
                    uch.link(nc.vector.tensor_scalar(inv[:, u % 2, :], inv[:, u % 2, :], share[:, s:s + 1], None, ALU.mult))
                second = kind == "self1" and s == 1
                dst = aob[:, :] if second else ao[:, t, :]
                nc.vector.tensor_tensor(dst.rearrange("p (h e) -> p h e", h=NH), o[:, :, 0:HD],
                                        inv[:, u % 2, :].rearrange("p (h e) -> p h e", e=1).broadcast_to([P, NH, HD]),
                                        ALU.mult).then_inc(sums_read, 1)
                if second:
                    dve.wait_ge(sums_read, i * U + u + 1)
                    nc.vector.tensor_tensor(ao[:, t, :], ao[:, t, :], aob[:, :], ALU.add).then_inc(ao_ready, 1)

            run(dve, front, group, tail)
            dve.wait_ge(x_done, ITER * LT)
            if kind == "batch":
                dve.wait_ge(y_done, ITER * LT)

        @block.tensor
        def _(pe):
            pe.wait_ge(loaded, NLOAD)
            pe.wait_ge(made, NB * SETS)

            def front(i, k, g):
                values_read = lambda: after(pe, v_ready, i * SETS * KC)
                for s in range(SETS):
                    if g == F_KEYS[s] and cross:
                        values_read()
                        pe.wait_ge(ctx_loaded[k], context_count(i, k))
                        keys(k, s)
                if g == F_TURN:
                    pe.wait_ge(xn_ready, i + 1)
                    if cross:
                        pe.wait_ge(kT_ready, (i + 1) * SETS * DC)
                    else:
                        values_read()
                    for c in range(DC):
                        for t in range(LT):
                            mm = nc.tensor.transpose(ps_f[:, (c * LT + t) * P:(c * LT + t + 1) * P],
                                                     xn[:, t, c * P:(c + 1) * P], ident[:, :])
                    mm.then_inc(turned, 1)
                for s in range(SETS):
                    if g == F_KEYS[s] and not cross:
                        if s == 0:
                            pe.wait_ge(xnT_ready, i + 1)
                        else:
                            pe.wait_ge(kT_ready, i * SETS * DC + s * DC)
                        keys(k, s)
                if g == F_QUERIES:
                    if cross:
                        pe.wait_ge(xnT_ready, i + 1)
                    else:
                        pe.wait_ge(kT_ready, (i + 1) * SETS * DC)
                    for m in range(DC):
                        for c in range(DC):
                            mm = nc.tensor.matmul(ps_f[:, m * LT * P:(m + 1) * LT * P], wq[:, c, m * P:(m + 1) * P],
                                                  xnT[:, c, :], start=(c == 0), stop=(c == DC - 1))
                        mm.then_inc(q_ps, 1)
                for s in range(SETS):
                    if g == F_VALUES[s]:
                        if s == 0:
                            pe.wait_ge(q_ready, (i + 1) * DC)
                        else:
                            pe.wait_ge(v_ready, i * SETS * KC + s * KC)
                        src = ctxT[:, k, :, :] if cross else xnT
                        off = s * P if kind == "batch" else 0
                        for n in range(KC):
                            for c in range(DC):
                                mm = nc.tensor.matmul(ps_f[0:KP, n * D:(n + 1) * D],
                                                      src[:, c, off + n * P:off + n * P + KP],
                                                      wv[s if kind == "self1" else 0][:, c, :],
                                                      start=(c == 0), stop=(c == DC - 1))
                            mm.then_inc(v_ps, 1)

            def keys(k, s):
                src = ctxT[:, k, :, :] if cross else xnT[:, :, :] if kind == "self1" else xnT[:, :, s * P:(s + 1) * P]
                for m in range(DC):
                    for c in range(DC):
                        mm = nc.tensor.matmul(ps_f[:, m * 256:m * 256 + NK],
                                              wk[s if kind == "self1" else 0][:, c, m * P:(m + 1) * P], src[:, c, :],
                                              start=(c == 0), stop=(c == DC - 1))
                    mm.then_inc(k_ps, 1)

            def group(i, k, g):
                if g == 0:
                    pe.wait_ge(kz_ready, (i + 1) * NDMA * 16)
                    pe.wait_ge(q_ready, (i + 1) * DC)
                    pe.wait_ge(v_ready, (i + 1) * SETS * KC)
                t, s = UNITS[g // GU]
                by_vector = has_bias and (kind != "self1" or UNITS[(g - 2) % G // GU][1] == 0)
                after(pe, top_ready if by_vector else prob_ready, i * G + g - 1)
                h0 = (g % GU) * GH
                q = lambda c: qT[k][:, c, t * P:(t + 1) * P]
                if HC >= GH:
                    c, hh = h0 // HC, h0 % HC
                    mm = nc.tensor.matmul(ps_s[g % 2][:, 0:GH * NK], q(c),
                                          kz[s][k][:, c, hh:hh + GH, :].rearrange("p h k -> p (h k)"),
                                          start=True, stop=True)
                else:
                    for c in range(DC):
                        mm = nc.tensor.matmul(ps_s[g % 2][:, c * HC * NK:(c + 1) * HC * NK], q(c),
                                              kz[s][k][:, c, :, :].rearrange("p h k -> p (h k)"),
                                              start=True, stop=True)
                mm.then_inc(scored, 1)

            def tail(i, k, t):
                e = t - LAGT
                if 0 <= e < G:
                    pe.wait_ge(prob_ready, i * G + e + 1)
                    after(pe, pT_odd if e % 2 else pT_even, i * (G // 2) + e // 2)
                    for j in range(4):
                        h, c = j // KC, j % KC
                        mm = nc.tensor.transpose(ps_t[e % 2][0:KP, j * P:(j + 1) * P],
                                                 prob[:, (k * G + e) % NP, h, c * P:c * P + KP], ident[:, :])
                    mm.then_inc(prob_turned, 1)
                e = t - LAGW
                if 0 <= e < G:
                    pe.wait_ge(pT_odd if e % 2 else pT_even, i * (G // 2) + e // 2 + 1)
                    u = e // GU
                    _, s = UNITS[u]
                    if e % GU == 0:
                        after(pe, sums_read, i * U + u - 1)
                    for j in range(4):
                        h, c = (e % GU) * GH + j // KC, j % KC
                        mm = nc.tensor.matmul(ps_o[u % 2][:, h * (HD + 1):(h + 1) * (HD + 1)],
                                              pT[0:KP, e % 2, j, :], V[s][k][0:KP, c, h, :],
                                              start=(c == 0), stop=(c == KC - 1))
                    mm.then_inc(weighed, 1)
                for n, at_end in enumerate(E_TILE):
                    if t == at_end + 1:
                        if kind == "self1":
                            pe.wait_ge(ao_ready, i * LT + n + 1)
                        else:
                            pe.wait_ge(sums_read, i * U + ENDS[n] + 1)
                        after(pe, x_done, i * LT + n)
                        for c in range(DC):
                            mm = nc.tensor.transpose(ps_w[:, c * P:(c + 1) * P],
                                                     ao[:, UNITS[ENDS[n]][0], c * P:(c + 1) * P], ident[:, :])
                        mm.then_inc(ao_turned, 1)
                    if t == at_end + 2:
                        pe.wait_ge(aoT_ready, i * LT + n + 1)
                        for c in range(DC):
                            mm = nc.tensor.matmul(ps_w[:, D:2 * D], aoT[:, c, :], wo[:, c, :],
                                                  start=(c == 0), stop=(c == DC - 1))
                        mm.then_inc(out_ps, 1)

            run(pe, front, group, tail)


def bitffn(nc, A, X, identb):
    LT = 2
    ITER = NT // LT
    HID = 1024
    HCH = HID // P
    ROUND = 12582912.0
    with Stage(nc, "bitffn") as st:
        sb, ps, sem = st.sb, st.ps, st.sem
        w1, w2 = sb("w1", [P, DC, HID]), sb("w2", [P, HCH, D])
        w1q, w2q = sb("w1q", [P, DC, HID], BF16), sb("w2q", [P, HCH, D], BF16)
        b1, b2 = sb("b1", [P, HID]), sb("b2", [P, D])
        ln1_w, ln1_b = sb("ln1_w", [P, D]), sb("ln1_b", [P, D])
        ln2_w, ln2_b = sb("ln2_w", [P, HID]), sb("ln2_b", [P, HID])
        loads = [(w1, "w1"), (w2, "w2"), (b1, "b1"), (b2, "b2"), (ln1_w, "ln1_w"), (ln1_b, "ln1_b"),
                 (ln2_w, "ln2_w"), (ln2_b, "ln2_b")]
        ones = sb("ones", [P, P])
        minus_round = sb("minus_round", [P, 1])
        absum, w_mean, w_scale, w_back = (sb(n, [P, 2]) for n in ("absum", "w_mean", "w_scale", "w_back"))
        pad = sb("pad", [P, 1])
        xt, h = sb("xt", [P, LT, D]), sb("h", [P, LT, D])
        stats, stats2, mv = sb("stats", [P, LT, 6]), sb("stats2", [P, LT, 2, 6]), sb("mv", [P, LT, 2])
        veps, guess, tmp, rstd = (sb(n, [P, LT]) for n in ("veps", "guess", "tmp", "rstd"))
        amax, a_scale, f1, f2 = (sb(n, [P, LT]) for n in ("amax", "a_scale", "f1", "f2"))
        q1, q1T = sb("q1", [P, LT, D], BF16), sb("q1T", [P, DC, LT * P], BF16)
        g = sb("g", [P, LT, HID])
        gn = sb("gn", [P, LT, HID])
        q2, q2T = sb("q2", [P, LT, HID], BF16), sb("q2T", [P, LT, HCH, P], BF16)
        ps_h = [ps(f"h{k}", [P, 512]) for k in range(4)]
        ps_q = ps("q", [P, DC, LT * P], BF16)
        ps_q2 = [ps(f"q2{k}", [P, HCH, P], BF16) for k in range(LT)]
        ps_o = ps("o", [P, LT, D])

        loaded, step, const_ready, summed, w_ready = sem("loaded"), sem("dve_step"), sem("const_ready"), sem("summed"), sem("w_ready")
        base_ready = sem("base_ready")
        xt_free, ln1_ready = sem("xt_free"), sem("ln1_ready")
        q1_sum, q1_ready, q1_turned, q1T_ready = sem("q1_sum"), sem("q1_ready"), sem("q1_turned"), sem("q1T_ready")
        h_ps, h_ready, g_ready = sem("h_ps"), sem("h_ready"), sem("g_ready")
        gn_ready, scaled, q2_sum, q2_ready = sem("gn_ready"), sem("scaled"), sem("q2_sum"), sem("q2_ready")
        q2_turned, q2T_ready, o_ps, x_done = sem("q2_turned"), sem("q2T_ready"), sem("o_ps"), sem("x_done")
        NLOAD = 16 * len(loads)
        NORMS = 3
        block = st.block()

        @block.sync
        def _(sp):
            for dst, name in loads:
                sp.dma_start(whole(dst), A[f"ff_{name}"]).then_inc(loaded, 16)
            sp.wait_ge(loaded, NLOAD)

        @block.gpsimd
        def _(pool):
            nc.gpsimd.memset(ones[:, :], 1.0).then_inc(const_ready, 1)
            nc.gpsimd.memset(minus_round[:, :], -ROUND).then_inc(const_ready, 1)
            pool.wait_ge(loaded, NLOAD)
            with pool.Fori(0, ITER) as i:
                pool.wait_ge(xt_free, i + 1)
                nc.gpsimd.tensor_tensor(xt[:, :, :], xt[:, :, :],
                                        b2[:, :].rearrange("p (a d) -> p a d", a=1).broadcast_to([P, LT, D]),
                                        ALU.add).then_inc(base_ready, 1)
                for t in range(LT):
                    pool.wait_ge(gn_ready, i * LT + t + 1)
                    nc.gpsimd.tensor_tensor(gn[:, t, :], gn[:, t, :], ln2_w[:, :], ALU.mult).then_inc(scaled, 1)

        @block.scalar
        def _(act):
            act.wait_ge(const_ready, 2)
            with act.Fori(0, ITER) as i:
                act.wait_ge(q1_sum, i + 1)
                nc.scalar.activation(q1[:, :, :], h[:, :, :], ACT.Identity, bias=minus_round[:, 0:1]).then_inc(q1_ready, 1)
                act.wait_ge(q1_turned, i + 1)
                nc.scalar.activation(q1T[:, :, :], ps_q[:, :, :], ACT.Identity).then_inc(q1T_ready, 1)
                for t in range(LT):
                    act.wait_ge(h_ready, i * LT + t + 1)
                    nc.scalar.activation(g[:, t, :], g[:, t, :], ACT.Gelu).then_inc(g_ready, 1)
                for t in range(LT):
                    act.wait_ge(q2_sum, i * LT + t + 1)
                    nc.scalar.activation(q2[:, t, :], gn[:, t, :], ACT.Identity, bias=minus_round[:, 0:1]).then_inc(q2_ready, 1)
                    act.wait_ge(q2_turned, i * LT + t + 1)
                    nc.scalar.activation(q2T[:, t, :, :], ps_q2[t][:, :, :], ACT.Identity).then_inc(q2T_ready, 1)

        @block.vector
        def _(dve):
            dve.wait_ge(loaded, NLOAD)
            dve.wait_ge(const_ready, 2)
            ch0 = Chain(dve, step)
            for k, w in enumerate((w1, w2)):
                ch0.link(nc.vector.tensor_reduce(absum[:, k:k + 1], w[:, :, :], AX.XY, ALU.add, apply_absolute_value=True))
            nc.vector.memset(pad[:, :], 0.0).then_inc(summed, 1)
            dve.wait_ge(summed, 2)
            ch0.link(nc.vector.tensor_scalar(w_mean[:, :], ps_o[:, 0, 0:2], 1.0 / (D * HID), EPS, ALU.mult, ALU.max))
            ch0.link(nc.vector.reciprocal(w_scale[:, :], w_mean[:, :]))
            ch0.link(nc.vector.reciprocal(w_back[:, :], w_scale[:, :]))
            for k, (w, q) in enumerate(((w1, w1q), (w2, w2q))):
                ch0.link(nc.vector.tensor_scalar(w[:, :, :], w[:, :, :], w_scale[:, k:k + 1], ROUND, ALU.mult, ALU.add))
                ch0.link(nc.vector.tensor_scalar(w[:, :, :], w[:, :, :], ROUND, -1.0, ALU.subtract, ALU.max))
                nc.vector.tensor_scalar(q[:, :, :], w[:, :, :], 1.0, None, ALU.min).then_inc(w_ready, 1)
            ch = Chain(dve, step, per=33 + ROOT_STEPS * NORMS, base=ch0.n)
            link = ch.link

            def quant_scale(src, n, f, w):
                link(nc.vector.tensor_reduce(amax[:, :], src[:, :, :], AX.X, ALU.max, apply_absolute_value=True))
                link(nc.vector.tensor_scalar(amax[:, :], amax[:, :], EPS, None, ALU.max))
                link(nc.vector.reciprocal(a_scale[:, :], amax[:, :]))
                link(nc.vector.tensor_scalar(a_scale[:, :], a_scale[:, :], 127.0, None, ALU.mult))
                link(nc.vector.tensor_scalar(f[:, :], amax[:, :], w_back[:, w:w + 1], 1.0 / 127.0, ALU.mult, ALU.mult))

            with dve.Fori(0, ITER) as i:
                ch.start(i)
                link(nc.vector.tensor_scalar(xt[:, :, :], X[:, bass.ds(i * LT, LT), :], 1.0, None, ALU.mult))
                for r in range(2):
                    src = xt if r == 0 else h
                    layer_norm_stats(nc, ch, src, LT, stats, mv, pad)
                    inverse_root(nc, link, mv, LT, veps, guess, tmp, rstd)
                    for t in range(LT):
                        ins = nc.vector.tensor_scalar(h[:, t, :], src[:, t, :], mv[:, t, 0:1], rstd[:, t:t + 1],
                                                      ALU.subtract, ALU.mult)
                        if r == 0 and t == LT - 1:
                            ins.then_inc(xt_free, 1)
                            dve.wait_ge(xt_free, i + 1)
                        else:
                            link(ins)
                for v, op in ((ln1_w, ALU.mult), (ln1_b, ALU.add)):
                    link(nc.vector.tensor_tensor(h[:, :, :], h[:, :, :],
                                                 v[:, :].rearrange("p (a d) -> p a d", a=1).broadcast_to([P, LT, D]), op))
                quant_scale(h, D, f1, 0)
                for t in range(LT):
                    link(nc.vector.tensor_scalar(h[:, t, :], h[:, t, :], a_scale[:, t:t + 1], 127.0, ALU.mult, ALU.min))
                nc.vector.tensor_scalar(h[:, :, :], h[:, :, :], -128.0, ROUND, ALU.max, ALU.add).then_inc(q1_sum, 1)
                for t in range(LT):
                    dve.wait_ge(h_ps, i * LT + t + 1)
                    for k in range(2):
                        ins = nc.vector.scalar_tensor_tensor(out=g[:, t, k * 512:(k + 1) * 512], in0=ps_h[2 * t + k][:, :],
                                                             scalar=f1[:, t:t + 1], in1=b1[:, k * 512:(k + 1) * 512],
                                                             op0=ALU.mult, op1=ALU.add)
                    ins.then_inc(h_ready, 1)
                for t in range(LT):
                    dve.wait_ge(g_ready, i * LT + t + 1)
                    for k in range(2):
                        ins = nc.vector.bn_stats(stats2[:, t, k, :], g[:, t, k * 512:(k + 1) * 512])
                    link(ins)
                nc.vector.memset(pad[:, :], 0.0)
                for t in range(LT):
                    ins = nc.vector.bn_aggr(mv[:, t, :], stats2[:, t, :, :])
                link(ins)
                inverse_root(nc, link, mv, LT, veps, guess, tmp, rstd)
                for t in range(LT):
                    nc.vector.tensor_scalar(gn[:, t, :], g[:, t, :], mv[:, t, 0:1], rstd[:, t:t + 1],
                                            ALU.subtract, ALU.mult).then_inc(gn_ready, 1)
                for t in range(LT):
                    dve.wait_ge(scaled, i * LT + t + 1)
                    link(nc.vector.tensor_tensor(gn[:, t, :], gn[:, t, :], ln2_b[:, :], ALU.add))
                quant_scale(gn, HID, f2, 1)
                for t in range(LT):
                    link(nc.vector.tensor_scalar(gn[:, t, :], gn[:, t, :], a_scale[:, t:t + 1], 127.0, ALU.mult, ALU.min))
                    nc.vector.tensor_scalar(gn[:, t, :], gn[:, t, :], -128.0, ROUND, ALU.max, ALU.add).then_inc(q2_sum, 1)
                dve.wait_ge(base_ready, i + 1)
                for t in range(LT):
                    dve.wait_ge(o_ps, i * LT + LT)
                    nc.vector.scalar_tensor_tensor(out=X[:, bass.ds(i * LT + t, 1), :], in0=ps_o[:, t:t + 1, :],
                                                   scalar=f2[:, t:t + 1], in1=xt[:, t:t + 1, :],
                                                   op0=ALU.mult, op1=ALU.add).then_inc(x_done, 1)
                dve.wait_ge(x_done, (i + 1) * LT)
                ch.stop()

        @block.tensor
        def _(pe):
            pe.wait_ge(summed, 1)
            nc.tensor.matmul(ps_o[:, 0, 0:2], ones[:, :], absum[:, :], start=True, stop=True).then_inc(summed, 1)
            pe.wait_ge(w_ready, 2)
            with pe.Fori(0, ITER) as i:
                pe.wait_ge(q1_ready, i + 1)
                for c in range(DC):
                    for t in range(LT):
                        mm = nc.tensor.transpose(ps_q[:, c, t * P:(t + 1) * P], q1[:, t, c * P:(c + 1) * P], identb[:, :])
                mm.then_inc(q1_turned, 1)
                pe.wait_ge(q1T_ready, i + 1)
                for t in range(LT):
                    for k in range(2):
                        for c in range(DC):
                            mm = nc.tensor.matmul(ps_h[2 * t + k][:, :], q1T[:, c, t * P:(t + 1) * P],
                                                  w1q[:, c, k * 512:(k + 1) * 512], start=(c == 0), stop=(c == DC - 1))
                    mm.then_inc(h_ps, 1)
                for t in range(LT):
                    pe.wait_ge(q2_ready, i * LT + t + 1)
                    for c in range(HCH):
                        mm = nc.tensor.transpose(ps_q2[t][:, c, :], q2[:, t, c * P:(c + 1) * P], identb[:, :])
                    mm.then_inc(q2_turned, 1)
                for t in range(LT):
                    pe.wait_ge(q2T_ready, i * LT + t + 1)
                    for c in range(HCH):
                        mm = nc.tensor.matmul(ps_o[:, t, :], q2T[:, t, c, :], w2q[:, c, :],
                                              start=(c == 0), stop=(c == HCH - 1))
                    mm.then_inc(o_ps, 1)


def to_positions(nc, X, scratch):
    with Stage(nc, "deal") as st:
        written, read = st.sem("written"), st.sem("read")
        block = st.block()

        @block.sync
        def _(sp):
            sp.dma_start(scratch.rearrange("(n p) d -> p n d", p=P), X[:, :, :]).then_inc(written, 16)
            sp.wait_ge(written, 16)
            for b in range(B):
                sp.dma_start(X[8 * b:8 * b + 8, :, :],
                             scratch[b * S:(b + 1) * S, :].rearrange("(t q) d -> q t d", q=8)).then_inc(read, 16)
            sp.wait_ge(read, 16 * B)


def route(nc, A, ident, Y, ysort, pos, expert):
    LT, E = 4, 8
    ITER = NT // LT
    ROUND = 12582912.0
    with Stage(nc, "route") as st:
        sb, ps, sem = st.sb, st.ps, st.sem
        wg = sb("wg", [P, DC, E])
        yb, yT = sb("yb", [P, LT, D]), sb("yT", [P, DC, LT * P])
        logits = sb("logits", [P, NT, E])
        best = sb("best", [P, NT])
        chosen, rank = sb("chosen", [P, NT, E]), sb("rank", [P, NT, E])
        zeros = sb("zeros", [P, SLOTS // 3, D])
        before, ones = sb("before", [P, P]), sb("ones", [P, P])
        descend = sb("descend", [P, E])
        keep = sb("keep", [P, E, NT])
        slot = sb("slot", [P, SLOTS])
        count, upto = sb("count", [P, E, NT]), sb("upto", [P, E, NT])
        tiles, end, base = sb("tiles", [P, E]), sb("end", [P, E]), sb("base", [P, E])
        ended = sb("ended", [P, SLOTS, E - 1])
        posf, expertf = sb("posf", [P, NT]), sb("expertf", [P, SLOTS])
        ps_t = [ps(f"t{k}", [P, LT * P]) for k in range(DC)]
        ps_l = ps("l", [P, LT, E])
        ps_rank, ps_count = ps("rank", [P, NT, E]), ps("count", [P, NT, E])

        loaded, zeroed, cleared, const_ready = sem("loaded"), sem("zeroed"), sem("cleared"), sem("const_ready")
        yb_ready, turned, yT_ready = sem("yb_ready"), sem("turned"), sem("yT_ready")
        logits_ps, logits_ready = sem("logits_ps"), sem("logits_ready")
        step, chosen_ready, counted, pos_ready, scattered = (
            sem("dve_step"), sem("chosen_ready"), sem("counted"), sem("pos_ready"), sem("scattered"))
        block = st.block()

        @block.sync
        def _(sp):
            sp.dma_start(wg[:, :, :], A["moe_wg"]).then_inc(loaded, 16)
            sp.wait_ge(zeroed, 1)
            for k in range(3):
                sp.dma_start(ysort.rearrange("(s p) d -> p s d", p=P)[:, k * (SLOTS // 3):(k + 1) * (SLOTS // 3), :],
                             zeros[:, :, :]).then_inc(cleared, 16)
            sp.wait_ge(loaded, 16)
            sp.wait_ge(cleared, 48)

        @block.gpsimd
        def _(pool):
            nc.gpsimd.memset(zeros[:, :, :], 0.0).then_inc(zeroed, 1)
            nc.gpsimd.memset(before[:, :], 1.0).then_inc(zeroed, 1)
            nc.gpsimd.memset(ones[:, :], 1.0).then_inc(zeroed, 1)
            nc.gpsimd.memset(keep[:, :, :], 1.0).then_inc(zeroed, 1)
            pool.wait_ge(zeroed, 4)
            nc.gpsimd.affine_select(out=before[:, :], in_=before[:, :], compare_op=ALU.is_ge, fill=0.0,
                                    base=-1, pattern=[[1, P]], channel_multiplier=-1).then_inc(const_ready, 1)
            nc.gpsimd.affine_select(out=keep[:, :, :], in_=keep[:, :, :], compare_op=ALU.is_ge, fill=0.0,
                                    base=-1, pattern=[[0, E], [1, NT]], channel_multiplier=0).then_inc(const_ready, 1)
            nc.gpsimd.iota(slot[:, :], [[1, SLOTS]], base=0, channel_multiplier=0,
                           allow_small_or_imprecise_dtypes=True).then_inc(const_ready, 1)
            nc.gpsimd.iota(descend[:, :], [[-1, E]], base=E, channel_multiplier=0,
                           allow_small_or_imprecise_dtypes=True).then_inc(const_ready, 1)
            pool.wait_ge(cleared, 48)
            pool.wait_ge(pos_ready, 1)
            for t in range(NT):
                nc.gpsimd.indirect_dma_start(
                    ysort, bass.IndirectOffsetOnAxis(ap=pos[:, t:t + 1], axis=0), Y[:, t, :], None).then_inc(scattered, 16)
            pool.wait_ge(scattered, 16 * NT)

        @block.scalar
        def _(act):
            with act.Fori(0, ITER) as i:
                for c in range(DC):
                    act.wait_ge(turned, i * DC + c + 1)
                    nc.scalar.activation(yT[:, c, :], ps_t[c][:, :], ACT.Identity).then_inc(yT_ready, 1)

        @block.tensor
        def _(pe):
            pe.wait_ge(loaded, 16)
            with pe.Fori(0, ITER) as i:
                pe.wait_ge(yb_ready, i + 1)
                for c in range(DC):
                    for t in range(LT):
                        mm = nc.tensor.transpose(ps_t[c][:, t * P:(t + 1) * P], yb[:, t, c * P:(c + 1) * P], ident[:, :])
                    mm.then_inc(turned, 1)
                pe.wait_ge(yT_ready, (i + 1) * DC)
                for t in range(LT):
                    for c in range(DC):
                        mm = nc.tensor.matmul(ps_l[:, t, :], yT[:, c, t * P:(t + 1) * P], wg[:, c, :],
                                              start=(c == 0), stop=(c == DC - 1))
                mm.then_inc(logits_ps, 1)
            pe.wait_ge(chosen_ready, 1)
            pe.wait_ge(const_ready, 4)
            flat = lambda v: v[:, :, :].rearrange("p t e -> p (t e)")
            nc.tensor.matmul(flat(ps_rank), before[:, :], flat(chosen), start=True, stop=True).then_inc(counted, 1)
            nc.tensor.matmul(flat(ps_count), ones[:, :], flat(chosen), start=True, stop=True).then_inc(counted, 1)

        @block.vector
        def _(dve):
            with dve.Fori(0, ITER) as i:
                nc.vector.tensor_scalar(yb[:, :, :], Y[:, bass.ds(i * LT, LT), :], 1.0, None, ALU.mult).then_inc(yb_ready, 1)
                dve.wait_ge(logits_ps, i + 1)
                nc.vector.tensor_scalar(logits[:, bass.ds(i * LT, LT), :], ps_l[:, :, :], 1.0, None,
                                        ALU.mult).then_inc(logits_ready, 1)
                dve.wait_ge(logits_ready, i + 1)
            dve.wait_ge(const_ready, 4)
            link = Chain(dve, step).link
            over_e = lambda v: v[:, :].rearrange("p (t e) -> p t e", e=1).broadcast_to([P, NT, E])
            by_e = lambda v, n: v.rearrange("p (a e) -> p a e", a=1).broadcast_to([P, n, v.shape[-1]])
            tile_major = lambda v: v[:, :, :].rearrange("p e t -> p t e")
            link(nc.vector.tensor_reduce(best[:, :], logits[:, :, :], AX.X, ALU.max))
            link(nc.vector.tensor_tensor(chosen[:, :, :], logits[:, :, :], over_e(best), ALU.is_equal))
            link(nc.vector.tensor_tensor(rank[:, :, :], chosen[:, :, :], by_e(descend[:, :], NT), ALU.mult))
            link(nc.vector.tensor_reduce(best[:, :], rank[:, :, :], AX.X, ALU.max))
            nc.vector.tensor_tensor(chosen[:, :, :], rank[:, :, :], over_e(best), ALU.is_equal).then_inc(chosen_ready, 1)
            dve.wait_ge(counted, 2)
            link(nc.vector.tensor_copy(tile_major(count), ps_count[:, :, :]))
            link(nc.vector.tensor_tensor_scan(upto[:, :, :].rearrange("p e t -> p (e t)"),
                                              keep[:, :, :].rearrange("p e t -> p (e t)"),
                                              count[:, :, :].rearrange("p e t -> p (e t)"), 0.0, ALU.mult, ALU.add))
            link(nc.vector.tensor_scalar(tiles[:, :], upto[:, :, NT - 1], 1.0 / P, (P - 1) / (2.0 * P), ALU.mult, ALU.add))
            link(nc.vector.tensor_scalar(tiles[:, :], tiles[:, :], ROUND, None, ALU.add))
            link(nc.vector.tensor_scalar(tiles[:, :], tiles[:, :], ROUND, None, ALU.subtract))
            link(nc.vector.tensor_tensor_scan(end[:, :], ones[:, 0:E], tiles[:, :], 0.0, ALU.mult, ALU.add))
            link(nc.vector.tensor_tensor(base[:, :], end[:, :], tiles[:, :], ALU.subtract))
            link(nc.vector.tensor_scalar(base[:, :], base[:, :], float(P), None, ALU.mult))
            link(nc.vector.tensor_tensor(upto[:, :, :], upto[:, :, :], count[:, :, :], ALU.subtract))
            link(nc.vector.tensor_tensor(rank[:, :, :], ps_rank[:, :, :], tile_major(upto), ALU.add))
            link(nc.vector.tensor_tensor(rank[:, :, :], rank[:, :, :], by_e(base[:, :], NT), ALU.add))
            link(nc.vector.tensor_tensor(rank[:, :, :], rank[:, :, :], chosen[:, :, :], ALU.mult))
            link(nc.vector.tensor_reduce(posf[:, :], rank[:, :, :], AX.X, ALU.add))
            nc.vector.tensor_copy(pos[:, :], posf[:, :]).then_inc(pos_ready, 1)
            link(nc.vector.tensor_tensor(ended[:, :, :],
                                         slot[:, :].rearrange("p (s e) -> p s e", e=1).broadcast_to([P, SLOTS, E - 1]),
                                         by_e(end[:, 0:E - 1], SLOTS), ALU.is_ge))
            link(nc.vector.tensor_reduce(expertf[:, :], ended[:, :, :], AX.X, ALU.add))
            link(nc.vector.tensor_copy(expert[:, :], expertf[:, :]))


def moe(nc, A, X, ident, ysort, zsort, pos, expert):
    E, DF = 8, 1024
    FC, HALF = DF // P, DF // 2
    with Stage(nc, "experts") as st:
        sb, ps, sem = st.sb, st.ps, st.sem
        w1, w2 = sb("w1", [P, E, DC, DF]), sb("w2", [P, E, FC, D])
        b1, b2 = sb("b1", [P, E, FC]), sb("b2", [P, E, D])
        b1_slot = sb("b1_slot", [P, 1, FC])
        g2, be2 = sb("g2", [P, D]), sb("be2", [P, D])
        y, yT = sb("y", [P, 2, D]), sb("yT", [P, D])
        h, hT = sb("h", [P, DF]), sb("hT", [P, DF])
        base, z = sb("base", [P, 2, D]), sb("z", [P, D])
        zout = sb("zout", [P, 2, D])
        gather = [sb(f"gather{k}", [P, D]) for k in range(4)]
        stats, mv = sb("stats", [P, 1, 6]), sb("mv", [P, 1, 2])
        veps, guess, tmp, rstd, pad = (sb(n, [P, 1]) for n in ("veps", "guess", "tmp", "rstd", "pad"))
        ps_h = [ps(f"h{k}", [P, HALF]) for k in range(2)]
        ps_hT = [ps(f"hT{k}", [P, HALF]) for k in range(2)]
        ps_y, ps_z = ps("y", [P, D]), ps("z", [P, D])

        loaded = sem("loaded")
        y_loaded = [sem(f"y_loaded{k}") for k in range(2)]
        y_turned, yT_ready, base_ready = sem("y_turned"), sem("yT_ready"), sem("base_ready")
        h_ps, h_ready, h_turned, hT_ready = sem("h_ps"), sem("h_ready"), sem("h_turned"), sem("hT_ready")
        z_ps, step = sem("z_ps"), sem("dve_step")
        normed, scaled, zout_ready = sem("normed"), sem("scaled"), sem("zout_ready")
        stored = [sem(f"stored{k}") for k in range(2)]
        x_done, z_taken = sem("x_done"), sem("z_taken")
        GB = 4
        gathered = [sem(f"gathered{k}") for k in range(GB)]
        loads = [(w1, "w1"), (w2, "w2"), (b1, "b1"), (b2, "b2"), (g2, "g2"), (be2, "be2")]
        NLOAD = 16 * len(loads)
        block = st.block()

        PAIRS = (SLOTS - 3) // 2

        def pairs(eng, body):
            with eng.Fori(0, PAIRS) as jj:
                for k in range(2):
                    body(jj * 2 + k + 2, k, jj + 2)

        @block.sync
        def _(sp):
            for dst, name in loads:
                sp.dma_start(whole(dst), A[f"moe_{name}"]).then_inc(loaded, 16)
            sp.wait_ge(loaded, NLOAD)
            fetch = lambda j, k: sp.dma_start(y[:, k, :], ysort[bass.ds(j * P, P), :]).then_inc(y_loaded[k], 16)
            fetch(0, 0)
            fetch(1, 1)

            def body(j, k, n, more=True):
                if more:
                    sp.wait_ge(y_turned, j + 1)
                    sp.wait_ge(base_ready, j + 1)
                    fetch(j + 2, k)
                sp.wait_ge(zout_ready, j + 1)
                sp.dma_start(zsort[bass.ds(j * P, P), :], zout[:, k, :]).then_inc(stored[k], 16)

            body(0, 0, 1)
            with sp.Fori(0, PAIRS) as jj:
                for k in range(2):
                    body(jj * 2 + k + 1, (k + 1) % 2, 0)
            body(SLOTS - 2, 1, 0, False)
            body(SLOTS - 1, 0, 0, False)
            for k in range(2):
                sp.wait_ge(stored[k], 16 * ((SLOTS + 1 - k) // 2))

        @block.gpsimd
        def _(pool):
            pool.wait_ge(loaded, NLOAD)

            def body(j, k, n):
                e = pool.value_load(expert[0:1, bass.ds(j, 1)], min_val=0, max_val=E - 1)
                pool.wait_ge(y_loaded[k], n * 16)
                nc.gpsimd.tensor_tensor(base[:, k, :].rearrange("p (a d) -> p a d", a=1),
                                        y[:, k, :].rearrange("p (a d) -> p a d", a=1),
                                        b2[:, bass.ds(e, 1), :], ALU.add).then_inc(base_ready, 1)
                pool.wait_ge(normed, j + 1)
                nc.gpsimd.tensor_tensor(z[:, :], z[:, :], g2[:, :], ALU.mult).then_inc(scaled, 1)
                pool.wait_ge(scaled, j + 1)
                if type(j) is not int:
                    pool.wait_ge(stored[k], (n - 1) * 16)
                elif j >= 2:
                    pool.wait_ge(stored[k], j // 2 * 16)
                nc.gpsimd.tensor_tensor(zout[:, k, :], z[:, :], be2[:, :], ALU.add).then_inc(zout_ready, 1)

            body(0, 0, 1)
            body(1, 1, 1)
            pairs(pool, body)
            body(SLOTS - 1, 0, SLOTS // 2 + 1)
            for k in range(2):
                pool.wait_ge(stored[k], 16 * ((SLOTS + 1 - k) // 2))
            for t in range(NT):
                if t >= GB:
                    pool.wait_ge(x_done, t - GB + 1)
                nc.gpsimd.indirect_dma_start(
                    gather[t % GB][:, :], None, zsort,
                    bass.IndirectOffsetOnAxis(ap=pos[:, t:t + 1], axis=0)).then_inc(gathered[t % GB], 16)

        @block.scalar
        def _(act):
            def turn(j):
                act.wait_ge(y_turned, j + 1)
                nc.scalar.activation(yT[:, :], ps_y[:, :], ACT.Identity).then_inc(yT_ready, 1)

            def relu(j):
                for k in range(2):
                    act.wait_ge(h_turned, j * 2 + k + 1)
                    for c in range(k * FC // 2, (k + 1) * FC // 2):
                        ins = nc.scalar.activation(hT[:, c * P:(c + 1) * P], ps_hT[k][:, c * P - k * HALF:(c + 1) * P - k * HALF],
                                                   ACT.Relu, bias=b1_slot[:, 0, c:c + 1])
                    ins.then_inc(hT_ready, 1)

            turn(0)
            turn(1)
            relu(0)
            with act.Fori(1, SLOTS - 1) as j:
                turn(j + 1)
                relu(j)
            relu(SLOTS - 1)

        @block.vector
        def _(dve):
            dve.wait_ge(loaded, NLOAD)

            def hidden(j):
                e = dve.value_load(expert[0:1, bass.ds(j, 1)], min_val=0, max_val=E - 1)
                if type(j) is not int or j:
                    dve.wait_ge(hT_ready, j * 2)
                nc.vector.tensor_scalar(b1_slot[:, :, :], b1[:, bass.ds(e, 1), :], 1.0, None, ALU.mult)
                for k in range(2):
                    dve.wait_ge(h_ps, j * 2 + k + 1)
                    nc.vector.tensor_copy(h[:, k * HALF:(k + 1) * HALF], ps_h[k][:, :]).then_inc(h_ready, 1)

            ch = Chain(dve, step, per=2 + ROOT_STEPS)

            def finish(j, k):
                ch.start(j)
                dve.wait_ge(z_ps, j + 1)
                dve.wait_ge(base_ready, j + 1)
                if type(j) is not int or j:
                    dve.wait_ge(zout_ready, j)
                nc.vector.tensor_tensor(z[:, :], ps_z[:, :], base[:, k, :], ALU.add).then_inc(z_taken, 1)
                dve.wait_ge(z_taken, j + 1)
                layer_norm_stats(nc, ch, z[:, :].rearrange("p (a d) -> p a d", a=1), 1, stats, mv, pad)
                inverse_root(nc, ch.link, mv, 1, veps, guess, tmp, rstd)
                nc.vector.tensor_scalar(z[:, :], z[:, :], mv[:, 0, 0:1], rstd[:, 0:1],
                                        ALU.subtract, ALU.mult).then_inc(normed, 1)
                ch.stop()

            hidden(0)
            for j in range(2):
                hidden(j + 1)
                finish(j, j)
            pairs(dve, lambda j, k, n: (hidden(j + 1), finish(j, k)))
            finish(SLOTS - 1, 0)
            for t in range(NT):
                dve.wait_ge(gathered[t % GB], 16 * (t // GB + 1))
                nc.vector.tensor_tensor(X[:, t, :], X[:, t, :], gather[t % GB][:, :], ALU.add).then_inc(x_done, 1)
            dve.wait_ge(x_done, NT)

        @block.tensor
        def _(pe):
            pe.wait_ge(loaded, NLOAD)

            def turn_y(j, k, n):
                pe.wait_ge(y_loaded[k], n * 16)
                if type(j) is not int or j:
                    pe.wait_ge(yT_ready, j)
                for c in range(DC):
                    mm = nc.tensor.transpose(ps_y[:, c * P:(c + 1) * P], y[:, k, c * P:(c + 1) * P], ident[:, :])
                mm.then_inc(y_turned, 1)

            def up(j):
                e = pe.value_load(expert[0:1, bass.ds(j, 1)], min_val=0, max_val=E - 1)
                pe.wait_ge(yT_ready, j + 1)
                for k in range(2):
                    if type(j) is not int or j:
                        pe.wait_ge(h_ready, j * 2 - 1 + k)
                    for c in range(DC):
                        mm = nc.tensor.matmul(ps_h[k][:, :], yT[:, c * P:(c + 1) * P],
                                              w1[:, bass.ds(e, 1), c, k * HALF:(k + 1) * HALF].rearrange("p a d -> p (a d)"),
                                              start=(c == 0), stop=(c == DC - 1))
                    mm.then_inc(h_ps, 1)

            def turn_h(j):
                for k in range(2):
                    pe.wait_ge(h_ready, j * 2 + k + 1)
                    if type(j) is not int or j:
                        pe.wait_ge(hT_ready, j * 2 - 1 + k)
                    for c in range(4):
                        mm = nc.tensor.transpose(ps_hT[k][:, c * P:(c + 1) * P],
                                                 h[:, k * HALF + c * P:k * HALF + (c + 1) * P], ident[:, :])
                    mm.then_inc(h_turned, 1)

            def down(j):
                e = pe.value_load(expert[0:1, bass.ds(j, 1)], min_val=0, max_val=E - 1)
                for k in range(2):
                    pe.wait_ge(hT_ready, j * 2 + k + 1)
                if type(j) is not int or j:
                    pe.wait_ge(z_taken, j)
                for c in range(FC):
                    mm = nc.tensor.matmul(ps_z[:, :], hT[:, c * P:(c + 1) * P],
                                          w2[:, bass.ds(e, 1), c, :].rearrange("p a d -> p (a d)"),
                                          start=(c == 0), stop=(c == FC - 1))
                mm.then_inc(z_ps, 1)

            def body(j, k, n):
                up(j)
                down(j - 1)
                turn_y(j + 1, (k + 1) % 2, n + k)
                turn_h(j)

            turn_y(0, 0, 1)
            up(0)
            turn_y(1, 1, 1)
            turn_h(0)
            body(1, 1, 1)
            pairs(pe, body)
            up(SLOTS - 1)
            down(SLOTS - 2)
            turn_h(SLOTS - 1)
            down(SLOTS - 1)


def store(nc, X, out, dealt):
    with Stage(nc, "store") as st:
        stored = st.sem("stored")
        block = st.block()

        @block.sync
        def _(sp):
            if dealt:
                for b in range(B):
                    sp.dma_start(out[b * S:(b + 1) * S, :].rearrange("(t q) d -> q t d", q=8),
                                 X[8 * b:8 * b + 8, :, :]).then_inc(stored, 16)
                sp.wait_ge(stored, 16 * B)
            else:
                sp.dma_start(out.rearrange("(n p) d -> p n d", p=P), X[:, :, :]).then_inc(stored, 16)
                sp.wait_ge(stored, 16)


STAGES = ("mamba", "cross0", "bitffn", "self1", "cross1", "moe")


def program(nc, A, out, stages=STAGES):
    with ExitStack() as ctx:
        X = ctx.enter_context(nc.sbuf_tensor("X", [P, NT, D], F32))
        ident = ctx.enter_context(nc.sbuf_tensor("ident", [P, P], F32))
        identb = ctx.enter_context(nc.sbuf_tensor("identb", [P, P], BF16))
        Stage.used.clear()
        setup(nc, A, X, ident, identb)
        for kind in stages:
            if len(Stage.used) > 60:
                clear_semaphores(nc)
            if kind == "mamba":
                mamba(nc, A, X, ident, identb)
            elif kind == "bitffn":
                bitffn(nc, A, X, identb)
            elif kind == "moe":
                scratch = nc.dram_tensor("scratch", (B * S, D), F32).ap()
                ysort = nc.dram_tensor("ysort", (SLOTS * P, D), F32).ap()
                zsort = nc.dram_tensor("zsort", (SLOTS * P, D), F32).ap()
                to_positions(nc, X, scratch)
                clear_semaphores(nc)
                pos = ctx.enter_context(nc.sbuf_tensor("pos", [P, NT], I32))
                expert = ctx.enter_context(nc.sbuf_tensor("expert", [P, SLOTS], I32))
                with nc.sbuf_tensor("Y", [P, NT, D], F32) as Y:
                    attention(nc, A, X, ident, "batch", Y)
                    route(nc, A, ident, Y, ysort, pos, expert)
                clear_semaphores(nc)
                moe(nc, A, X, ident, ysort, zsort, pos, expert)
            else:
                attention(nc, A, X, ident, kind)
        store(nc, X, out, "moe" in stages)


def layout(inputs):
    import numpy as np

    a = {k: np.asarray(v) for k, v in inputs.items()}

    def rows(w):
        return np.ascontiguousarray(w.reshape(-1, P, w.shape[-1]).transpose(1, 0, 2))

    def cols(v):
        return np.ascontiguousarray(v.reshape(-1, P).T)

    def spread(v):
        return np.ascontiguousarray(np.broadcast_to(v.reshape(1, -1), (P, v.size)))

    def heads_last(w):
        return w.transpose(1, 0, 2).reshape(D, -1)

    o = {"x": a["x"].reshape(B * S, D)}
    w = {k[8:]: v for k, v in a.items() if k.startswith("L0_attn_")}
    xp = w["xp_w"].T
    o |= {
        "mb_in_w": rows(w["in_w"].T), "mb_out_w": rows(w["out_w"].T), "mb_xp_dt": rows(xp[:, :64]),
        "mb_xp_bc": rows(np.concatenate([xp[:, 64:]] * 3, axis=1)), "mb_dtp_w": np.ascontiguousarray(w["dtp_w"].T),
        "mb_ln_w": cols(w["ln_w"]), "mb_ln_b": cols(w["ln_b"]), "mb_in_b": cols(w["in_b"]),
        "mb_conv_w": rows(w["conv_w"][:, 0, :]), "mb_conv_b": cols(w["conv_b"]), "mb_dtp_b": cols(w["dtp_b"]),
        "mb_D": cols(w["D"]), "mb_A_log": rows(w["A_log"]), "mb_out_b": spread(w["out_b"]),
    }
    o["ctxT"] = rows(a["ctx_1024"].reshape(-1, D).T)
    o["c0_mask"] = np.ascontiguousarray(
        a["mask_Bx1xSxS2_bk0"].reshape(NT, P, -1).transpose(1, 0, 2))
    for pre, name, fix in (("c0", "L0_xattn", lambda m: m), ("c1", "L1_xattn", heads_last)):
        for k in "qkv":
            o[f"{pre}_w{k}" + ("" if k == "q" else "0")] = rows(fix(a[f"{name}_{'w' if pre == 'c0' else 'W'}{k}"]))
            v = a[f"{name}_b{k}"].reshape(-1)
            o[f"{pre}_b{k}"] = spread(v) if k == "v" else cols(v)
        o[f"{pre}_wo"] = rows(a[f"{name}_{'w' if pre == 'c0' else 'W'}o"])
        o[f"{pre}_bo"] = spread(a[f"{name}_bo"])
    o |= {"sa_wq": rows(a["L1_attn_Wq"]), "sa_wo": rows(a["L1_attn_Wo"])}
    for s, name in enumerate(("L1_attn_Wkv_short", "L1_attn_Wkv_long")):
        o |= {f"sa_wk{s}": rows(a[name][:, :D]), f"sa_wv{s}": rows(a[name][:, D:])}
    o["sa_mix"] = spread(np.stack([a["L1_attn_mix_weight"], a["L1_attn_decay_factor"]]))
    f = {k[7:]: v for k, v in a.items() if k.startswith("L0_ffn_")}
    o |= {"ff_w1": rows(f["w1"].T), "ff_w2": rows(f["w2"].T)}
    o |= {f"ff_{k}": spread(f[k]) for k in ("b1", "b2", "ln1_w", "ln1_b", "ln2_w", "ln2_b")}
    wqkv = a["L1_ffn_Wqkv"].T
    for k, name in enumerate(("wq", "wk0", "wv0")):
        o[f"ba_{name}"] = rows(wqkv[:, k * D:(k + 1) * D])
    bqkv = a["L1_ffn_bqkv"]
    o |= {"ba_bq": cols(bqkv[:D]), "ba_bk": cols(bqkv[D:2 * D]), "ba_bv": spread(bqkv[2 * D:]),
          "ba_wo": rows(a["L1_ffn_Wo"].T), "ba_bo": spread(a["L1_ffn_bo"]),
          "ba_g1": spread(a["L1_ffn_g1"]), "ba_be1": spread(a["L1_ffn_be1"]),
          "ba_mod8": (np.arange(P) % 8).astype(np.float32).reshape(P, 1)}
    m = {k[7:]: v for k, v in a.items() if k.startswith("L1_ffn_")}
    E = m["Wg"].shape[0]

    def per_expert(w):
        return np.ascontiguousarray(w.reshape(E, -1, P, w.shape[-1]).transpose(2, 0, 1, 3))

    def spread_all(v):
        return np.ascontiguousarray(np.broadcast_to(v[None], (P,) + v.shape))

    o |= {"moe_wg": rows(m["Wg"].T), "moe_w1": per_expert(m["W1"]), "moe_w2": per_expert(m["W2"]),
          "moe_b1": np.ascontiguousarray(m["b1"].reshape(E, -1, P).transpose(2, 0, 1)), "moe_b2": spread_all(m["b2"]),
          "moe_g2": spread(m["g2"]), "moe_be2": spread(m["be2"])}
    return o


def kernel(**inputs):
    import concourse.bacc as _bacc
    from concourse.bass_utils import run_bass_kernel_spmd as _run

    nc = _bacc.Bacc("TRN2", target_bir_lowering=False, num_devices=1)
    arrays, A = {}, {}
    for name, v in layout(inputs).items():
        arrays[f"in_{name}_dram"] = v
        A[name] = nc.dram_tensor(f"in_{name}_dram", v.shape, mybir.dt.from_np(v.dtype), kind="ExternalInput").ap()
    out = nc.dram_tensor("out_0_dram", (B * S, D), F32, kind="ExternalOutput").ap()
    program(nc, A, out)
    r = _run(nc, [arrays], core_ids=[0])
    return r.results[0]["out_0_dram"].reshape(B, S, D)
```

```python
from contextlib import ExitStack

import concourse.bass as bass
from concourse import mybir

F32 = mybir.dt.float32
BF16 = mybir.dt.bfloat16
I32 = mybir.dt.int32
U8 = mybir.dt.uint8
ALU = mybir.AluOpType
ACT = mybir.ActivationFunctionType
AX = mybir.AxisListType

P = 128
D = 256
DC = D // P
B, S = 16, 256
NT = B * S // P
EPS = 1e-5
SLOTS = NT + 7


class Stage:

    used = []

    def __init__(self, nc, name):
        self.nc, self.name, self.ctx = nc, name, ExitStack()

    def __enter__(self):
        self.ctx.__enter__()
        return self

    def __exit__(self, *a):
        return self.ctx.__exit__(*a)

    def sb(self, name, shape, dt=F32):
        return self.ctx.enter_context(self.nc.sbuf_tensor(f"{self.name}_{name}", shape, dt))

    def ps(self, name, shape, dt=F32):
        return self.ctx.enter_context(self.nc.psum_tensor(f"{self.name}_ps_{name}", shape, dt))

    def sem(self, name):
        s = self.ctx.enter_context(self.nc.semaphore(f"{self.name}_{name}"))
        self.used.append(s.num)
        return s

    def block(self):
        return self.ctx.enter_context(self.nc.Block())


def clear_semaphores(nc):
    nums = sorted(Stage.used)
    for lo in (n for n in nums if n - 1 not in nums):
        hi = lo
        while hi in nums:
            hi += 1
        nc.all_engine_barrier(sems_to_clear=range(lo, hi))
    Stage.used.clear()


class Chain:

    def __init__(self, eng, sem, per=0, base=0):
        self.eng, self.sem, self.per, self.n, self.i, self.base = eng, sem, per, 0, None, base

    def start(self, i):
        self.i, self.n = i, 0

    def mark(self, ins):
        self.n += 1
        ins.then_inc(self.sem, 1)

    def link(self, ins):
        self.mark(ins)
        at = self.n + self.base
        self.eng.wait_ge(self.sem, at if self.i is None else self.i * self.per + at)

    def stop(self):
        assert self.i is None or self.n == self.per, (self.n, self.per)


def layer_norm_stats(nc, ch, src, tiles, stats, mv, pad):
    for t in range(tiles):
        (ch.mark if t < tiles - 1 else ch.link)(nc.vector.bn_stats(stats[:, t, :], src[:, t, :]))
    nc.vector.memset(pad[:, :], 0.0)
    for t in range(tiles):
        (ch.mark if t < tiles - 1 else ch.link)(nc.vector.bn_aggr(mv[:, t, :], stats[:, t, :]))


ROOT_STEPS = 12


def inverse_root(nc, link, mv, tiles, veps, guess, tmp, rstd, parts=(0, 1, 2, 3)):
    bits = lambda v: v[:, 0:tiles].bitcast(I32)
    for k in parts:
        if k == 0:
            link(nc.vector.tensor_scalar(veps[:, 0:tiles], mv[:, 0:tiles, 1], EPS, None, ALU.add))
            link(nc.vector.tensor_scalar(bits(tmp), bits(veps), 1, None, ALU.arith_shift_right))
            link(nc.vector.tensor_scalar(bits(guess), bits(tmp), -1.0, float(0x5F3759DF), ALU.mult, ALU.add))
        else:
            link(nc.vector.tensor_tensor(tmp[:, 0:tiles], guess[:, 0:tiles], guess[:, 0:tiles], ALU.mult))
            link(nc.vector.scalar_tensor_tensor(out=tmp[:, 0:tiles], in0=tmp[:, 0:tiles], scalar=-0.5,
                                                in1=veps[:, 0:tiles], op0=ALU.mult, op1=ALU.mult))
            link(nc.vector.scalar_tensor_tensor(out=(rstd if k == 3 else guess)[:, 0:tiles], in0=tmp[:, 0:tiles],
                                                scalar=1.5, in1=guess[:, 0:tiles], op0=ALU.add, op1=ALU.mult))


def normalize(nc, link, src, dst, tiles, mv, rstd):
    for t in range(tiles):
        link(nc.vector.tensor_scalar(dst[:, t, :], src[:, t, :], mv[:, t, 0:1], rstd[:, t:t + 1],
                                     ALU.subtract, ALU.mult))


def whole(t):
    return t[tuple(slice(None) for _ in t.shape)]


def setup(nc, A, X, ident, identb):
    with Stage(nc, "setup") as st:
        x_loaded, zeroed, made = st.sem("x_loaded"), st.sem("zeroed"), st.sem("made")
        block = st.block()

        @block.sync
        def _(sp):
            sp.dma_start(X[:, :, :], A["x"].rearrange("(n p) d -> p n d", p=P)).then_inc(x_loaded, 16)
            sp.wait_ge(x_loaded, 16)

        @block.gpsimd
        def _(pool):
            nc.gpsimd.memset(ident[:, :], 0.0).then_inc(zeroed, 1)
            nc.gpsimd.memset(identb[:, :], 0.0).then_inc(zeroed, 1)
            pool.wait_ge(zeroed, 2)
            for m in (ident, identb):
                nc.gpsimd.affine_select(out=m[:, :], in_=m[:, :], compare_op=ALU.not_equal, fill=1.0,
                                        base=0, pattern=[[-1, P]], channel_multiplier=1).then_inc(made, 1)
            pool.wait_ge(made, 2)


def after(eng, sem, value):
    if type(value) is not int or value > 0:
        eng.wait_ge(sem, value)


def pipeline(eng, front, group, tail, iters, groups, buffers, depths, ahead=1, front_first=False):
    depth = max(depths)
    first = -(-depth // buffers) * buffers
    loops = (iters - ahead - first) // buffers

    def body(j, jk, here):
        for g in range(groups):
            if here < iters and not front_first:
                group(j, jk, g)
            if here < iters - ahead:
                front(j + ahead, (jk + ahead) % buffers, g)
            if here < iters and front_first:
                group(j, jk, g)
            for d in depths:
                if 0 <= here - d < iters:
                    tail(j - d, (jk - d) % buffers, d * groups + g)

    for i in range(ahead):
        for g in range(groups):
            front(i, i, g)
    for j in range(first):
        body(j, j % buffers, j)
    with eng.Fori(0, loops) as jj:
        for k in range(buffers):
            body(jj * buffers + first + k, k, first + k)
    for j in range(first + loops * buffers, iters + depth):
        body(j, j % buffers, j)


def mamba(nc, A, X, ident, identb):
    TT = S // P
    N = S
    ITER = B
    R, NS = 64, 16
    INNER = 512
    MC = INNER // P
    K = 4
    Q = 4
    QG = NS // Q
    G = MC * QG
    ND, NU = 4, 4
    FILLS = NS
    F_STATS, F_GUESS, F_ROOT, F_NORM = (0, 3), (0, 3), (0, 3), (1, 5)
    F_TURN, F_TURNED, F_IN, F_TAPS, F_CONV, F_GATE, F_SILU = 6, 6, 6, 6, (7, 8), 7, 9
    F_PARAMS, F_SPLIT, F_DT, F_SOFT, F_LOG, F_SUM, F_RESET = 10, 10, 10, 11, 11, 12, 13
    F_FILL = (11, 11, 12, 12, 13, 13, 14, 14, 15, 15, 16, 16, 17, 17, 17, 17)
    LEAD = 2
    T_OUT, T_ADD = G + 2, G + 4
    RESET = 1.0e20
    FRONT_STEPS = 1 + 2 * (2 * TT + ROOT_STEPS) + 2 * (K - 1) + 4

    with Stage(nc, "mamba") as st:
        sb, ps, sem = st.sb, st.ps, st.sem
        in_w = sb("in_w", [P, DC, 2 * INNER])
        out_w = sb("out_w", [P, MC, D])
        xp_dt = sb("xp_dt", [P, MC, R])
        xp_bc = sb("xp_bc", [P, MC, 96])
        dtp_w = sb("dtp_w", [R, INNER])
        ln_w, ln_b = sb("ln_w", [P, DC]), sb("ln_b", [P, DC])
        in_b = sb("in_b", [P, 2 * MC])
        conv_w, conv_b = sb("conv_w", [P, MC, K]), sb("conv_b", [P, MC])
        dtp_b, Dw = sb("dtp_b", [P, MC]), sb("Dw", [P, MC])
        a_log, neg_a, a = sb("a_log", [P, MC, NS]), sb("neg_a", [P, MC, NS]), sb("a", [P, MC, NS])
        out_b = sb("out_b", [P, D])
        sel = sb("sel", [96, 32, P], BF16)
        pad, pool_pad = sb("pad", [P, 1]), sb("pool_pad", [P, 1])
        xt, hid, hn = sb("xt", [P, TT, D]), sb("hid", [P, TT, D]), sb("hn", [P, TT, D])
        stats, mv = sb("stats", [P, TT, 6]), sb("mv", [P, TT, 2])
        veps, guess, tmp, rstd, shift = (sb(n, [P, TT]) for n in ("veps", "guess", "tmp", "rstd", "shift"))
        hnT = sb("hnT", [P, DC, N])
        xpad = sb("xpad", [P, MC, K - 1 + N])
        dtraw = sb("dtraw", [R, N])
        spa = sb("spa", [P, MC, N])
        parts, split2, resid = sb("parts", [96, N], BF16), sb("split2", [96, N], BF16), sb("resid", [96, N])
        gate, xc, dt, dtx = ([sb(f"{n}{k}", [P, MC, N]) for k in range(2)] for n in ("gate", "xc", "dt", "dtx"))
        bc = [sb(f"bc{k}", [P, 2 * NS, N]) for k in range(2)]
        decay, u = sb("decay", [P, ND, Q, N]), sb("u", [P, NU, Q, N])
        ps_f = [ps(f"f{k}", [P, 2, N]) for k in range(3)]
        ps_b = [ps(f"b{k}", [P, 2, N]) for k in range(2)]
        ps_y = [ps(f"y{k}", [P, N]) for k in range(2)]
        ps_out = ps("out", [P, TT, D])

        loaded = sem("loaded")
        sel_ready, a_exp, consts = sem("sel_ready"), sem("a_exp"), sem("consts")
        fstep, ystep, astep, pstep = sem("dve_front_step"), sem("dve_y_step"), sem("act_step"), sem("pool_step")
        root_ready, hid_ready, hn_ready = sem("root_ready"), sem("hid_ready"), sem("hn_ready")
        turned, hnT_ready = sem("turned"), sem("hnT_ready")
        proj_ready, proj_taken = sem("proj_ready"), sem("proj_taken")
        conv_ready, xc_ready = sem("conv_ready"), sem("xc_ready")
        bc_ps, parts_ready = sem("bc_ps"), sem("parts_ready")
        dtraw_ps, dtraw_ready = sem("dtraw_ps"), sem("dtraw_ready")
        spread, spread_taken = sem("spread"), sem("spread_taken")
        dt_ps, dt_taken, dt_log, dt_sum = sem("dt_ps"), sem("dt_taken"), sem("dt_log"), sem("dt_sum")
        dtx_ready, dt_reset = sem("dtx_ready"), sem("dt_reset")
        decay_ready, u_ready, h_ready, hc_ready = sem("decay_ready"), sem("u_ready"), sem("h_ready"), sem("hc_ready")
        hc_summed = sem("hc_summed")
        yg_ready, out_ready = sem("yg_ready"), sem("out_ready")
        base_ready, x_done = sem("base_ready"), sem("x_done")
        loads = [(in_w, "in_w"), (out_w, "out_w"), (xp_dt, "xp_dt"), (xp_bc, "xp_bc"), (dtp_w, "dtp_w"),
                 (ln_w, "ln_w"), (ln_b, "ln_b"), (in_b, "in_b"), (conv_w, "conv_w"), (conv_b, "conv_b"),
                 (dtp_b, "dtp_b"), (Dw, "D"), (a_log, "A_log"), (out_b, "out_b")]
        NLOAD = 16 * len(loads)
        block = st.block()

        def run(eng, front, group, tail):
            pipeline(eng, front, group, tail, ITER, G, 2, (0, 1))

        def nothing(i, k, g):
            pass

        def fill_row(f):
            q, j = f // 4, f % 4
            return (0 if j < 2 else NS) + Q * q + 2 * (j % 2)

        @block.sync
        def _(sp):
            for dst, name in loads:
                sp.dma_start(whole(dst), A[f"mb_{name}"]).then_inc(loaded, 16)
            sp.wait_ge(loaded, NLOAD)

        @block.gpsimd
        def _(pool):
            nc.gpsimd.memset(sel[:, :, :], 0.0).then_inc(sel_ready, 1)
            for j in range(3):
                pool.wait_ge(sel_ready, j + 1)
                nc.gpsimd.affine_select(out=sel[:, :, :], in_=sel[:, :, :], compare_op=ALU.not_equal, fill=1.0,
                                        base=-32 * j, pattern=[[-1, 32], [0, P]],
                                        channel_multiplier=1).then_inc(sel_ready, 1)
            pool.wait_ge(loaded, NLOAD)

            def front(i, k, g):
                if g == F_STATS[1]:
                    there = X[:, bass.ds(i * TT, TT), :]
                    pool.wait_ge(hid_ready, i + 1)
                    nc.gpsimd.tensor_tensor(pool_pad[:, :], Dw[:, 0:1], Dw[:, 0:1], ALU.add)
                    nc.gpsimd.tensor_tensor(there, there, hid[:, :, :], ALU.add).then_inc(pstep, 1)
                    pool.wait_ge(pstep, i + 1)
                    nc.gpsimd.tensor_tensor(pool_pad[:, :], Dw[:, 0:1], Dw[:, 0:1], ALU.add)
                    nc.gpsimd.tensor_tensor(there, there,
                                            out_b[:, :].rearrange("p (a d) -> p a d", a=1).broadcast_to([P, TT, D]),
                                            ALU.add).then_inc(base_ready, 1)
                if g in (F_SUM, F_SUM + 1):
                    if g == F_SUM:
                        pool.wait_ge(xc_ready, (i + 1) * MC)
                        after(pool, u_ready, (i - 1) * G)
                    for m in range((g - F_SUM) * MC // 2, (g - F_SUM + 1) * MC // 2):
                        pool.wait_ge(dt_sum, i * MC + m + 1)
                        nc.gpsimd.tensor_tensor(dtx[k][:, m, :], dt[k][:, m, :], xc[k][:, m, :],
                                                ALU.mult).then_inc(dtx_ready, 1)

            def group(i, k, g):
                m, q = g // QG, g % QG
                if g == 0:
                    pool.wait_ge(dtx_ready, (i + 1) * MC)
                if m == 0:
                    pool.wait_ge(spread_taken, i * FILLS + 4 * q + 2)
                after(pool, hc_summed, i * G + g - NU + 1)
                nc.gpsimd.tensor_tensor(u[:, g % NU, :, :], dtx[k][:, m:m + 1, :].broadcast_to([P, Q, N]),
                                        bc[k][:, Q * q:Q * (q + 1), :], ALU.mult).then_inc(u_ready, 1)

            run(pool, front, group, nothing)

        @block.scalar
        def _(act):
            act.wait_ge(loaded, NLOAD)
            nc.scalar.activation(neg_a[:, :, :], a_log[:, :, :], ACT.Exp).then_inc(a_exp, 1)
            act.wait_ge(consts, 1)

            def front(i, k, g):
                if g >= G - LEAD:
                    decays(i, k, g - (G - LEAD))
                for r, (dst, src, ready) in enumerate(((hid, xt, hid_ready), (hn, hid, hn_ready))):
                    if g == F_NORM[r]:
                        act.wait_ge(root_ready, 2 * i + r + 1)
                        after(act, turned if r else base_ready, i)
                        for t in range(TT):
                            ins = nc.scalar.activation(dst[:, t, :], src[:, t, :], ACT.Identity,
                                                       bias=shift[:, t:t + 1], scale=rstd[:, t:t + 1])
                        ins.then_inc(ready, 1)
                if g == F_TURNED:
                    act.wait_ge(turned, i + 1)
                    after(act, proj_ready, i * 2 * MC)
                    for c in range(DC):
                        nc.scalar.activation(hnT[:, c, :], ps_f[2][:, c, :], ACT.Identity,
                                             bias=ln_b[:, c:c + 1], scale=ln_w[:, c:c + 1]).then_inc(hnT_ready, 1)
                if g == F_TAPS:
                    after(act, conv_ready, i * MC)
                    for m in range(MC):
                        act.wait_ge(proj_ready, i * 2 * MC + m // 2 * 2 + 2)
                        nc.scalar.activation(xpad[:, m, K - 1:], ps_f[m // 2][:, m % 2, :],
                                             ACT.Identity, bias=in_b[:, m:m + 1]).then_inc(proj_taken, 1)
                if g == F_SILU:
                    after(act, out_ready, i - 1)
                    after(act, yg_ready, (i - 1) * MC)
                    for m in range(MC):
                        act.wait_ge(proj_ready, i * 2 * MC + MC + m // 2 * 2 + 2)
                        nc.scalar.activation(gate[k][:, m, :], ps_f[(2, 0)[m // 2]][:, m % 2, :], ACT.Silu,
                                             bias=in_b[:, MC + m:MC + m + 1]).then_inc(proj_taken, 1)
                    for m in range(MC):
                        act.wait_ge(conv_ready, i * MC + m + 1)
                        nc.scalar.activation(xc[k][:, m, :], dt[k][:, m, :], ACT.Silu).then_inc(xc_ready, 1)
                if g == F_SPLIT:
                    act.wait_ge(dtraw_ps, i + 1)
                    after(act, dt_ps, i * MC)
                    nc.scalar.activation(dtraw[:, :], ps_f[1][0:R, 0, :], ACT.Identity).then_inc(dtraw_ready, 1)
                if g == F_SOFT:
                    act.wait_ge(xc_ready, (i + 1) * MC)
                    after(act, dt_sum, i * MC)
                    for m in range(MC):
                        act.wait_ge(dt_ps, i * MC + m // 2 * 2 + 2)
                        z = ps_f[m // 2][:, m % 2, :]
                        nc.scalar.activation(spa[:, m, :], z, ACT.Abs, bias=dtp_b[:, m:m + 1]).then_inc(astep, 1)
                        nc.scalar.activation(dt[k][:, m, :], z, ACT.Relu, bias=dtp_b[:, m:m + 1]).then_inc(dt_taken, 1)
                    act.wait_ge(astep, i * 2 * MC + MC)
                    for m in range(MC):
                        nc.scalar.activation(spa[:, m, :], spa[:, m, :], ACT.Exp, scale=-1.0).then_inc(astep, 1)
                if g == F_LOG:
                    act.wait_ge(astep, (i + 1) * 2 * MC)
                    for m in range(MC):
                        nc.scalar.activation(spa[:, m, :], spa[:, m, :], ACT.Ln, bias=1.0).then_inc(dt_log, 1)
                for f in range(FILLS):
                    if g == F_FILL[f]:
                        take_fill(i, k, f)

            def take_fill(i, k, f):
                if f == 0:
                    after(act, u_ready, (i - 1) * G)
                    after(act, hc_ready, (i - 1) * G)
                act.wait_ge(spread, i * FILLS + f + 1)
                row = fill_row(f)
                nc.scalar.activation(bc[k][:, row:row + 2, :], ps_b[f % 2][:, :, :],
                                     ACT.Identity).then_inc(spread_taken, 1)

            def group(i, k, g):
                if g + LEAD < G:
                    decays(i, k, g + LEAD)

            def decays(i, k, g):
                m, q = g // QG, g % QG
                if g == 0:
                    act.wait_ge(dt_reset, i + 1)
                after(act, h_ready, i * G + g - ND + 1)
                for s in range(Q):
                    ins = nc.scalar.activation(decay[:, g % ND, s, :], dt[k][:, m, :], ACT.Exp,
                                               scale=a[:, m, Q * q + s:Q * q + s + 1])
                ins.then_inc(decay_ready, 1)

            def tail(i, k, t):
                for f in range(FILLS):
                    if t + G == F_FILL[f]:
                        take_fill(i, k, f)

            run(act, front, group, tail)

        @block.vector
        def _(dve):
            nc.vector.memset(xpad[:, :, 0:K - 1], 0.0)
            dve.wait_ge(a_exp, 1)
            nc.vector.tensor_scalar(a[:, :, :], neg_a[:, :, :], -1.0, None, ALU.mult).then_inc(consts, 1)
            dve.wait_ge(loaded, NLOAD)
            fch = Chain(dve, fstep, per=FRONT_STEPS)
            ych = Chain(dve, ystep, per=MC)

            def front(i, k, g):
                if g == 0:
                    fch.start(i)
                    after(dve, hid_ready, i)
                    fch.link(nc.vector.tensor_scalar(xt[:, :, :], X[:, bass.ds(i * TT, TT), :], 1.0, None, ALU.mult))
                for r, src in enumerate((xt, hid)):
                    if g == F_STATS[r]:
                        if r:
                            dve.wait_ge(hid_ready, i + 1)
                        layer_norm_stats(nc, fch, src, TT, stats, mv, pad)
                    if g == F_GUESS[r]:
                        inverse_root(nc, fch.link, mv, TT, veps, guess, tmp, rstd, (0, 1))
                    if g == F_ROOT[r]:
                        if r == 0:
                            after(dve, hn_ready, i)
                        inverse_root(nc, fch.link, mv, TT, veps, guess, tmp, rstd, (2, 3))
                        nc.vector.scalar_tensor_tensor(out=shift[:, :], in0=mv[:, :, 0], scalar=-1.0, in1=rstd[:, :],
                                                       op0=ALU.mult, op1=ALU.mult).then_inc(root_ready, 1)
                if g in F_CONV:
                    if g == F_CONV[0]:
                        after(dve, decay_ready, (i - 1) * G)
                    half = F_CONV.index(g)
                    chunks = range(half * MC // 2, (half + 1) * MC // 2)
                    dve.wait_ge(proj_taken, i * 2 * MC + chunks[-1] + 1)
                    for j in range(K):
                        for m in chunks:
                            z = dt[k][:, m, :]
                            if j == 0:
                                ins = nc.vector.tensor_scalar(z, xpad[:, m, 0:N], conv_w[:, m, 0:1], conv_b[:, m:m + 1],
                                                              ALU.mult, ALU.add)
                            else:
                                ins = nc.vector.scalar_tensor_tensor(out=z, in0=xpad[:, m, j:j + N],
                                                                     scalar=conv_w[:, m, j:j + 1], in1=z,
                                                                     op0=ALU.mult, op1=ALU.add)
                            if j == K - 1:
                                ins.then_inc(conv_ready, 1)
                        if j < K - 1:
                            fch.link(ins)
                if g == F_SPLIT:
                    dve.wait_ge(bc_ps, i + 1)
                    after(dve, spread, i * FILLS)
                    q = ps_f[2][0:96, 0, :]
                    fch.link(nc.vector.tensor_copy(parts[:, :], q))
                    fch.link(nc.vector.tensor_tensor(resid[:, :], q, parts[:, :], ALU.subtract))
                    fch.link(nc.vector.tensor_copy(split2[:, :], resid[:, :]))
                    fch.link(nc.vector.tensor_copy(parts[32:64, :], split2[32:64, :]))
                    nc.vector.tensor_tensor(parts[64:96, :], resid[64:96, :], split2[64:96, :],
                                            ALU.subtract).then_inc(parts_ready, 1)
                if g == F_SUM:
                    for m in range(MC):
                        dve.wait_ge(dt_log, i * MC + m + 1)
                        nc.vector.tensor_tensor(dt[k][:, m, :], dt[k][:, m, :], spa[:, m, :], ALU.add).then_inc(dt_sum, 1)
                if g == F_RESET:
                    dve.wait_ge(dtx_ready, (i + 1) * MC)
                    nc.vector.memset(dt[k][:, :, 0:1], RESET).then_inc(dt_reset, 1)
                if g == G - 1:
                    fch.stop()

            def group(i, k, g):
                m, q = g // QG, g % QG
                n = i * G + g
                dve.wait_ge(decay_ready, n + 1)
                dve.wait_ge(u_ready, n + 1)
                flat = lambda x: x.rearrange("p a b -> p (a b)")
                nc.vector.tensor_tensor_scan(flat(u[:, g % NU, :, :]), flat(decay[:, g % ND, :, :]),
                                             flat(u[:, g % NU, :, :]), 0.0, ALU.mult, ALU.add).then_inc(h_ready, 1)
                dve.wait_ge(h_ready, n + 1)
                if m == 0:
                    dve.wait_ge(spread_taken, i * FILLS + 4 * q + 4)
                nc.vector.tensor_tensor(u[:, g % NU, :, :], u[:, g % NU, :, :],
                                        bc[k][:, NS + Q * q:NS + Q * (q + 1), :], ALU.mult).then_inc(hc_ready, 1)

            def tail(i, k, t):
                for m in range(MC):
                    if t == (m + 1) * QG + 1:
                        ych.start(i)
                        ych.n = m
                        dve.wait_ge(hc_summed, i * G + (m + 1) * QG)
                        ych.link(nc.vector.scalar_tensor_tensor(out=xc[k][:, m, :], in0=xc[k][:, m, :],
                                                                scalar=Dw[:, m:m + 1], in1=ps_y[m % 2][:, :],
                                                                op0=ALU.mult, op1=ALU.add))
                        nc.vector.tensor_tensor(xc[k][:, m, :], xc[k][:, m, :], gate[k][:, m, :],
                                                ALU.mult).then_inc(yg_ready, 1)
                if t == T_ADD:
                    dve.wait_ge(out_ready, i + 1)
                    dve.wait_ge(base_ready, i + 1)
                    there = X[:, bass.ds(i * TT, TT), :]
                    nc.vector.tensor_tensor(there, there, ps_out[:, :, :], ALU.add).then_inc(x_done, 1)

            run(dve, front, group, tail)
            dve.wait_ge(x_done, ITER)

        @block.tensor
        def _(pe):
            pe.wait_ge(loaded, NLOAD)
            pe.wait_ge(sel_ready, 4)

            def project(i, m, bank):
                for c in range(DC):
                    mm = nc.tensor.matmul(ps_f[bank][:, m % 2, :], in_w[:, c, m * P:(m + 1) * P], hnT[:, c, :],
                                          start=(c == 0), stop=(c == DC - 1))
                mm.then_inc(proj_ready, 1)

            def front(i, k, g):
                if g == F_TURN:
                    pe.wait_ge(hn_ready, i + 1)
                    after(pe, parts_ready, i)
                    for c in range(DC):
                        for t in range(TT):
                            mm = nc.tensor.transpose(ps_f[2][:, c, t * P:(t + 1) * P], hn[:, t, c * P:(c + 1) * P],
                                                     ident[:, :])
                    mm.then_inc(turned, 1)
                if g == F_IN:
                    pe.wait_ge(hnT_ready, (i + 1) * DC)
                    after(pe, dt_taken, i * MC)
                    for m in range(MC):
                        project(i, m, m // 2)
                if g == F_GATE:
                    project(i, MC, 2)
                    project(i, MC + 1, 2)
                    pe.wait_ge(proj_taken, i * 2 * MC + 2)
                    project(i, MC + 2, 0)
                    project(i, MC + 3, 0)
                if g == F_PARAMS:
                    pe.wait_ge(xc_ready, (i + 1) * MC)
                    pe.wait_ge(proj_taken, (i + 1) * 2 * MC)
                    for m in range(MC):
                        mm = nc.tensor.matmul(ps_f[1][0:R, 0, :], xp_dt[:, m, :], xc[k][:, m, :],
                                              start=(m == 0), stop=(m == MC - 1))
                    mm.then_inc(dtraw_ps, 1)
                    for m in range(MC):
                        mm = nc.tensor.matmul(ps_f[2][0:96, 0, :], xp_bc[:, m, :], xc[k][:, m, :],
                                              start=(m == 0), stop=(m == MC - 1))
                    mm.then_inc(bc_ps, 1)
                if g == F_DT:
                    pe.wait_ge(dtraw_ready, i + 1)
                    for m in range(MC):
                        nc.tensor.matmul(ps_f[m // 2][:, m % 2, :], dtp_w[:, m * P:(m + 1) * P], dtraw[:, :],
                                         start=True, stop=True).then_inc(dt_ps, 1)
                for f in range(FILLS):
                    if g == F_FILL[f]:
                        fill(i, f)

            def fill(i, f):
                if f == 0:
                    pe.wait_ge(parts_ready, i + 1)
                after(pe, spread_taken, i * FILLS + f - 1)
                for j in range(2):
                    mm = nc.tensor.matmul(ps_b[f % 2][:, j, :], sel[:, fill_row(f) + j, :], parts[:, :],
                                          start=True, stop=True)
                mm.then_inc(spread, 1)

            def tail(i, k, t):
                for f in range(FILLS):
                    if t + G == F_FILL[f]:
                        fill(i, f)
                g = t - 1
                if 0 <= g < G:
                    m, q = g // QG, g % QG
                    pe.wait_ge(hc_ready, i * G + g + 1)
                    if q == 0:
                        after(pe, yg_ready, i * MC + m - 1)
                    for j in range(Q):
                        mm = nc.tensor.matmul(ps_y[m % 2][:, :], ident[:, :], u[:, g % NU, j, :],
                                              start=(q == 0 and j == 0), stop=(q == QG - 1 and j == Q - 1))
                    mm.then_inc(hc_summed, 1)
                if t == T_OUT:
                    pe.wait_ge(yg_ready, (i + 1) * MC)
                    after(pe, x_done, i)
                    for r in range(TT):
                        for m in range(MC):
                            mm = nc.tensor.matmul(ps_out[:, r, :], xc[k][:, m, r * P:(r + 1) * P], out_w[:, m, :],
                                                  start=(m == 0), stop=(m == MC - 1))
                    mm.then_inc(out_ready, 1)

            run(pe, front, nothing, tail)


def attention(nc, A, X, ident, kind, Y=None):
    LT = 2
    ITER = NT // LT
    HD = 64 if kind == "batch" else 16
    NH = D // HD
    HC = P // HD
    NK = {"self1": 256, "batch": P}.get(kind, 120)
    SETS = 2 if kind in ("self1", "batch") else 1
    UNITS = {"self1": [(0, 0), (0, 1), (1, 0), (1, 1)], "batch": [(0, 0), (1, 1)]}.get(kind, [(0, 0), (1, 0)])
    KC = -(-NK // P)
    KP = min(NK, P)
    GH = 4 // KC
    GU = NH // GH
    U = len(UNITS)
    G = U * GU
    SCALE = HD ** -0.5
    cross = kind.startswith("cross")
    has_bias = kind in ("cross0", "self1", "batch")
    pre = {"cross0": "c0", "cross1": "c1", "self1": "sa", "batch": "ba"}[kind]
    MASKED = 1.0e30
    LAGT, LAGW = {"batch": (2, 3), "self1": (2, 4)}.get(kind, (3, 4))
    NP = 4
    NB = 4 if kind == "batch" else 2

    with Stage(nc, kind) as st:
        sb, ps, sem = st.sb, st.ps, st.sem
        wq, wo = sb("wq", [P, DC, D]), sb("wo", [P, DC, D])
        wk = [sb(f"wk{s}", [P, DC, D]) for s in range(SETS if kind == "self1" else 1)]
        wv = [sb(f"wv{s}", [P, DC, D]) for s in range(SETS if kind == "self1" else 1)]
        loads = [(wq, "wq"), (wo, "wo")] + [(w, f"wk{s}") for s, w in enumerate(wk)] + [(w, f"wv{s}") for s, w in enumerate(wv)]
        if kind != "self1":
            bq, bk, bv, bo = sb("bq", [P, DC]), sb("bk", [P, DC]), sb("bv", [P, D]), sb("bo", [P, D])
            loads += [(bq, "bq"), (bk, "bk"), (bv, "bv"), (bo, "bo")]
        else:
            mix = sb("mix", [P, 2])
            share = sb("share", [P, 2])
            neg_rate = sb("neg_rate", [P, 1])
            small = sb("small", [P, 2])
            loads += [(mix, "mix")]
        if kind == "batch":
            mod8 = sb("mod8", [P, 1])
            loads += [(mod8, "mod8")]
        xt, xn = sb("xt", [P, LT, D]), sb("xn", [P, LT, D])
        stats, mv = sb("stats", [P, LT, 6]), sb("mv", [P, LT, 2])
        veps, guess, tmp, rstd = (sb(n, [P, LT]) for n in ("veps", "guess", "tmp", "rstd"))
        xnT, qT = sb("xnT", [P, DC, LT * P]), [sb(f"qT{k}", [P, DC, LT * P]) for k in range(NB)]
        kT = [sb(f"kT{s}", [P, DC, NK]) for s in range(SETS)]
        kz = [[sb(f"kz{s}{k}", [P, DC, HC, NK]) for k in range(NB)] for s in range(SETS)]
        V = [[sb(f"V{s}{k}", [P, KC, NH, HD + 1]) for k in range(NB)] for s in range(SETS)]
        if cross:
            ctxT = sb("ctxT", [P, 2, DC, NK])
        if kind == "cross0":
            mask8 = sb("mask8", [P, 2, LT, NK], U8)
        if has_bias:
            biases = [sb(f"bias{k}", [P, LT, NK]) for k in range(2 if kind == "cross0" else 1)]
            bias = biases[0]
            biased = sb("biased", [P, 3, GH, NK])
        top, ntop = sb("top", [P, G * GH]), sb("ntop", [P, G * GH])
        prob = sb("prob", [P, NP, GH, NK])
        pT = sb("pT", [P, 2, 4, P])
        inv = sb("inv", [P, 2, NH])
        ao, aob, aoT = sb("ao", [P, LT, D]), sb("aob", [P, D]), sb("aoT", [P, DC, P])
        ps_s = [ps(f"s{k}", [P, 512]) for k in range(2)]
        ps_t = [ps(f"t{k}", [P, 512]) for k in range(2)]
        ps_o = [ps(f"o{k}", [P, 512]) for k in range(2)]
        ps_w = ps("w", [P, 512])
        ps_f = ps("f", [P, 512])

        loaded, ready0, kzeroed = sem("loaded"), sem("ready0"), sem("kzeroed")
        ctx_loaded = [sem(f"ctx_loaded{k}") for k in range(2)]
        made = sem("made")
        step, fstep, ustep = sem("dve_step"), sem("dve_front_step"), sem("dve_unit_step")
        xn_ready, turned, xnT_ready = sem("xn_ready"), sem("turned"), sem("xnT_ready")
        q_ps, q_ready = sem("q_ps"), sem("q_ready")
        k_ps, kT_ready, kz_ready = sem("k_ps"), sem("kT_ready"), sem("kz_ready")
        v_ps, v_ready = sem("v_ps"), sem("v_ready")
        scored, top_ready, prob_ready = sem("scored"), sem("top_ready"), sem("prob_ready")
        prob_turned = sem("prob_turned")
        pT_even, pT_odd = sem("pT_even"), sem("pT_odd")
        bias_ready = sem("bias_ready")
        sums_read = sem("sums_read")
        weighed, ao_ready = sem("weighed"), sem("ao_ready")
        ao_turned, aoT_ready, out_ps = sem("ao_turned"), sem("aoT_ready"), sem("out_ps")
        base_ready, x_done = sem("base_ready"), sem("x_done")
        NLOAD = 16 * len(loads)
        NDMA = HC * SETS
        pad = sb("pad", [P, 1])
        block = st.block()

        def tile_ends(u):
            return u == U - 1 or UNITS[u + 1][0] != UNITS[u][0]

        ENDS = [u for u in range(U) if tile_ends(u)]
        FRONT_STEPS = 1 + 2 * LT + ROOT_STEPS + LT - 1
        SCORE_STEPS = {"cross0": G, "cross1": 0, "self1": G // 2, "batch": G}[kind]
        UNIT_STEPS = 2 if kind == "self1" else 1
        at = lambda x: int(x * G)
        F_NORM = [at(x) for x in (0.0, 0.0625, 0.125, 0.1875)]
        F_TURN = at(0.25)
        F_KEYS = [at(0.0 if cross else 0.35 + 0.1 * s) for s in range(SETS)]
        F_QUERIES = at(0.6)
        F_VALUES = [at(0.75 + 0.1 * s) for s in range(SETS)]
        F_NORM_NEXT = 0
        E_UNIT = [(u + 1) * GU - 1 + LAGW for u in range(U)]
        E_TILE = [(u + 1) * GU - 1 + LAGW for u in ENDS]
        LATE = max(E_TILE) + 4
        DEPTH = LATE // G
        DEPTHS = range(DEPTH, -1, -1) if kind == "batch" else range(DEPTH + 1)
        E_ADD = 2 if kind == "batch" else 3

        def context_count(i, k):
            per = 32 if kind == "cross0" else 16
            if type(i) is int:
                return (i // 2 + 1) * per
            return (i - k) * (per // 2) + per

        def run(eng, front, group, tail, front_first=False):
            pipeline(eng, front, group, tail, ITER, G, NB, DEPTHS, 2 if kind == "batch" else 1,
                     front_first)

        @block.sync
        def _(sp):
            for dst, name in loads:
                sp.dma_start(whole(dst), A[f"{pre}_{name}"]).then_inc(loaded, 16)
            sp.wait_ge(kzeroed, NB * SETS + 1)

            def fetch(b, k):
                sp.dma_start(ctxT[:, k, :, :], A["ctxT"][:, :, bass.ds(b * NK, NK)]).then_inc(ctx_loaded[k], 16)
                if kind == "cross0":
                    sp.dma_start(mask8[:, k, :, :],
                                 A["c0_mask"][:, bass.ds(b * LT, LT), :]).then_inc(ctx_loaded[k], 16)

            def body(i, k, first=False, more=True):
                sp.wait_ge(kT_ready, (i + 1) * SETS * DC)
                if not first:
                    sp.wait_ge(scored, (i - NB + 1) * G)
                for s in range(SETS):
                    for h in range(HC):
                        rows = slice(HD * h, HD * h + HD)
                        sp.dma_start(kz[s][k][rows, :, h, :], kT[s][rows, :, :]).then_inc(kz_ready, 16)
                if cross and more:
                    sp.wait_ge(v_ps, (i + 1) * SETS * KC)
                    sp.wait_ge(k_ps, (i + 1) * SETS * DC)
                    if kind == "cross0":
                        sp.wait_ge(bias_ready, i + 1)
                    fetch(i + 2, k)

            if cross:
                fetch(0, 0)
                fetch(1, 1)
            for i in range(NB):
                body(i, i, first=True)
            with sp.Fori(0, ITER // NB - 2) as ii:
                for k in range(NB):
                    body(ii * NB + NB + k, k)
            for k in range(NB):
                body(ITER - NB + k, k, more=False)
            sp.wait_ge(loaded, NLOAD)
            sp.wait_ge(kz_ready, 16 * NDMA * ITER)

        @block.gpsimd
        def _(pool):
            for s in range(SETS):
                for k in range(NB):
                    nc.gpsimd.memset(whole(kz[s][k]), 0.0).then_inc(kzeroed, 1)
            if kind == "self1":
                nc.gpsimd.iota(bias[:, :, :], [[-P, LT], [1, NK]], base=0, channel_multiplier=-1,
                               allow_small_or_imprecise_dtypes=True).then_inc(kzeroed, 1)
            elif kind == "batch":
                ids = biased[:, 0:1, 0, :].rearrange("p a k -> p (a k)")
                nc.gpsimd.iota(ids.rearrange("p (b q) -> p b q", q=8), [[0, 16], [1, 8]], base=0,
                               channel_multiplier=0, allow_small_or_imprecise_dtypes=True).then_inc(kzeroed, 1)
            else:
                nc.gpsimd.memset(ao[:, 0, 0:1], 0.0).then_inc(kzeroed, 1)
            pool.wait_ge(loaded, NLOAD)
            if kind != "self1":
                with pool.Fori(0, ITER) as i:
                    pool.wait_ge(xn_ready, i + 1)
                    there = (Y if kind == "batch" else X)[:, bass.ds(i * LT, LT), :]
                    nc.gpsimd.tensor_tensor(there, xn[:, :, :] if kind == "batch" else there,
                                            bo[:, :].rearrange("p (a d) -> p a d", a=1).broadcast_to([P, LT, D]),
                                            ALU.add).then_inc(base_ready, 1)

        @block.scalar
        def _(act):
            act.wait_ge(loaded, NLOAD)
            if kind == "self1":
                nc.scalar.activation(small[:, 0:1], mix[:, 0:1], ACT.Exp, scale=-1.0).then_inc(ready0, 1)

            def front(i, k, g):
                if g == F_TURN:
                    act.wait_ge(turned, i + 1)
                    after(act, v_ps, i * SETS * KC)
                    nc.scalar.activation(xnT[:, :, :], ps_f[:, :].rearrange("p (c n) -> p c n", c=DC),
                                         ACT.Identity).then_inc(xnT_ready, 1)
                for s in range(SETS):
                    if g == F_KEYS[s]:
                        act.wait_ge(k_ps, i * SETS * DC + DC * (s + 1))
                        after(act, kz_ready, i * NDMA * 16)
                        for m in range(DC):
                            kw = {} if kind == "self1" else {"bias": bk[:, m:m + 1]}
                            nc.scalar.activation(kT[s][:, m, :], ps_f[:, m * 256:m * 256 + NK], ACT.Identity,
                                                 **kw).then_inc(kT_ready, 1)

            def group(i, k, g):
                act.wait_ge(top_ready, i * G + g + 1)
                after(act, prob_turned, i * G + g - NP + 1)
                for h in range(GH):
                    src = (biased[:, g % 2, h, :] if has_bias and (kind != "self1" or UNITS[g // GU][1] == 0)
                           else ps_s[g % 2][:, h * NK:(h + 1) * NK])
                    ins = nc.scalar.activation(prob[:, (k * G + g) % NP, h, :], src, ACT.Exp,
                                               bias=ntop[:, g * GH + h:g * GH + h + 1])
                ins.then_inc(prob_ready, 1)

            def tail(i, k, t):
                e = t - LAGT
                if 0 <= e < G and e % 2:
                    act.wait_ge(prob_turned, i * G + e + 1)
                    after(act, weighed, i * G + e - 1)
                    nc.scalar.activation(pT[0:KP, e % 2, :, :],
                                         ps_t[e % 2][0:KP, :].rearrange("p (j n) -> p j n", j=4),
                                         ACT.Identity).then_inc(pT_odd, 1)
                for n, at_end in enumerate(E_TILE):
                    if t == at_end + 1:
                        act.wait_ge(ao_turned, i * LT + n + 1)
                        nc.scalar.activation(aoT[:, :, :], ps_w[:, 0:D].rearrange("p (c n) -> p c n", c=DC),
                                             ACT.Identity).then_inc(aoT_ready, 1)

            run(act, front, group, tail, front_first=True)

        @block.vector
        def _(dve):
            for s in range(SETS):
                for k in range(NB):
                    nc.vector.memset(V[s][k][:, :, :, HD:HD + 1], 1.0).then_inc(made, 1)
            nc.vector.memset(top[:, :], 0.0)
            dve.wait_ge(loaded, NLOAD)
            ch0 = Chain(dve, step)
            if kind == "self1":
                dve.wait_ge(ready0, 1)
                ch0.link(nc.vector.tensor_scalar(small[:, 1:2], small[:, 0:1], 1.0, None, ALU.add))
                ch0.link(nc.vector.reciprocal(share[:, 0:1], small[:, 1:2]))
                ch0.link(nc.vector.tensor_scalar(share[:, 1:2], share[:, 0:1], -1.0, 1.0, ALU.mult, ALU.add))
                ch0.link(nc.vector.tensor_scalar(small[:, 0:1], mix[:, 1:2], -1.0, 1.0, ALU.mult, ALU.add))
                ch0.link(nc.vector.tensor_scalar(neg_rate[:, :], small[:, 0:1], -1.0, None, ALU.mult))
                dve.wait_ge(kzeroed, NB * SETS + 1)
                dist = biased[:, 0:2, 0, :]
                ch0.link(nc.vector.scalar_tensor_tensor(out=dist, in0=bias[:, :, :], scalar=-1.0, in1=bias[:, :, :],
                                                        op0=ALU.mult, op1=ALU.max))
                ch0.link(nc.vector.tensor_scalar(bias[:, :, :], dist, neg_rate[:, 0:1], None, ALU.mult))
            elif kind == "batch":
                dve.wait_ge(kzeroed, NB * SETS + 1)
                ch0.link(nc.vector.tensor_scalar(bias[:, 0, :], biased[:, 0, 0, :], mod8[:, 0:1], None, ALU.is_equal))
                ch0.link(nc.vector.tensor_scalar(bias[:, 0, :], bias[:, 0, :], MASKED, -MASKED, ALU.mult, ALU.add))
                ch0.link(nc.vector.tensor_copy(bias[:, 1, :], bias[:, 0, :]))
            fch = Chain(dve, fstep, per=FRONT_STEPS)
            sch = Chain(dve, step, per=SCORE_STEPS, base=ch0.n)
            uch = Chain(dve, ustep, per=U * UNIT_STEPS)

            def norm(i, parts):
                if 0 in parts:
                    fch.start(i)
                    after(dve, xn_ready, i)
                    fch.link(nc.vector.tensor_scalar(xt[:, :, :], X[:, bass.ds(i * LT, LT), :], 1.0, None, ALU.mult))
                    layer_norm_stats(nc, fch, xt, LT, stats, mv, pad)
                if 1 in parts:
                    inverse_root(nc, fch.link, mv, LT, veps, guess, tmp, rstd, (0, 1))
                if 2 in parts:
                    inverse_root(nc, fch.link, mv, LT, veps, guess, tmp, rstd, (2, 3))
                if 3 in parts:
                    after(dve, turned, i)
                    if kind != "self1":
                        after(dve, base_ready, i)
                    for t in range(LT):
                        ins = nc.vector.tensor_scalar(xn[:, t, :], xt[:, t, :], mv[:, t, 0:1], rstd[:, t:t + 1],
                                                      ALU.subtract, ALU.mult)
                        if t < LT - 1:
                            fch.link(ins)
                        else:
                            ins.then_inc(xn_ready, 1)
                    fch.stop()

            def front(i, k, g):
                if kind != "batch":
                    norm(i, [n for n in range(4) if g == F_NORM[n]])
                else:
                    if type(i) is int and i == 0 and g == 0:
                        norm(0, range(4))
                    if g == F_NORM_NEXT and not (type(i) is int and i == ITER - 1):
                        norm(i + 1, range(4))
                if g == F_TURN and kind == "cross0":
                    dve.wait_ge(ctx_loaded[k], context_count(i, k))
                    nc.vector.tensor_scalar(biases[k][:, :, :], mask8[:, k, :, :], MASKED, -MASKED,
                                            ALU.mult, ALU.add).then_inc(bias_ready, 1)
                if g == F_QUERIES:
                    dve.wait_ge(q_ps, (i + 1) * DC)
                    for m in range(DC):
                        src = ps_f[:, m * LT * P:(m + 1) * LT * P]
                        if kind == "self1":
                            nc.vector.tensor_scalar(qT[k][:, m, :], src, SCALE, None, ALU.mult).then_inc(q_ready, 1)
                        else:
                            nc.vector.tensor_scalar(qT[k][:, m, :], src, bq[:, m:m + 1], SCALE, ALU.add,
                                                    ALU.mult).then_inc(q_ready, 1)
                for s in range(SETS):
                    if g == F_VALUES[s]:
                        dve.wait_ge(v_ps, i * SETS * KC + (s + 1) * KC)
                        after(dve, weighed, (i - NB + 1) * G)
                        for c in range(KC):
                            src = ps_f[0:KP, c * D:(c + 1) * D].rearrange("p (h e) -> p h e", h=NH)
                            dst = V[s][k][0:KP, c, :, 0:HD]
                            if kind == "self1":
                                nc.vector.tensor_copy(dst, src).then_inc(v_ready, 1)
                            else:
                                nc.vector.tensor_tensor(dst, src, bv[0:KP, :].rearrange("p (h e) -> p h e", h=NH),
                                                        ALU.add).then_inc(v_ready, 1)

            def group(i, k, g):
                if g == 0:
                    sch.start(i)
                t, s = UNITS[g // GU]
                dve.wait_ge(scored, i * G + g + 1)
                if has_bias and (kind != "self1" or s == 0):
                    after(dve, prob_ready, i * G + g - 1)
                    if g == 0 and kind == "cross0":
                        dve.wait_ge(bias_ready, i + 1)
                    nc.vector.memset(pad[:, :], 0.0)
                    for h in range(GH):
                        ins = nc.vector.tensor_tensor_reduce(
                            out=biased[:, g % 2, h, :], in0=ps_s[g % 2][:, h * NK:(h + 1) * NK],
                            in1=biases[k if kind == "cross0" else 0][:, t, :], scale=1.0, scalar=-3.0e38,
                            op0=ALU.add, op1=ALU.max, accum_out=top[:, g * GH + h:g * GH + h + 1])
                    sch.link(ins)
                    nc.vector.tensor_scalar(ntop[:, g * GH:(g + 1) * GH], top[:, g * GH:(g + 1) * GH],
                                            -1.0, None, ALU.mult).then_inc(top_ready, 1)
                else:
                    nc.vector.tensor_reduce(ntop[:, g * GH:(g + 1) * GH],
                                            ps_s[g % 2][:, 0:GH * NK].rearrange("p (h k) -> p h k", h=GH),
                                            AX.X, ALU.max, negate=True).then_inc(top_ready, 1)
                if g == G - 1:
                    sch.stop()

            def tail(i, k, t):
                e = t - LAGT
                if 0 <= e < G and e % 2 == 0:
                    dve.wait_ge(prob_turned, i * G + e + 1)
                    after(dve, weighed, i * G + e - 1)
                    nc.vector.tensor_copy(pT[0:KP, e % 2, :, :],
                                          ps_t[e % 2][0:KP, :].rearrange("p (j n) -> p j n", j=4)).then_inc(pT_even, 1)
                for n, at_end in enumerate(E_TILE):
                    if t == at_end + E_ADD:
                        dve.wait_ge(out_ps, i * LT + n + 1)
                        if n == 0 and kind != "self1":
                            dve.wait_ge(base_ready, i + 1)
                        R = (Y if kind == "batch" else X)[:, bass.ds(i * LT + n, 1), :]
                        o = ps_w[:, D:2 * D].rearrange("p (a d) -> p a d", a=1)
                        nc.vector.tensor_tensor(R, R, o, ALU.add).then_inc(x_done, 1)
                for u in range(U):
                    if t == E_UNIT[u]:
                        normalize_unit(i, u)

            def normalize_unit(i, u):
                t, s = UNITS[u]
                o = ps_o[u % 2][:, 0:NH * (HD + 1)].rearrange("p (h e) -> p h e", h=NH)
                dve.wait_ge(weighed, i * G + (u + 1) * GU)
                uch.start(i)
                uch.n = u * UNIT_STEPS
                uch.link(nc.vector.reciprocal(inv[:, u % 2, :].rearrange("p (h e) -> p h e", e=1), o[:, :, HD:HD + 1]))
                if kind == "self1":
                    uch.link(nc.vector.tensor_scalar(inv[:, u % 2, :], inv[:, u % 2, :], share[:, s:s + 1], None, ALU.mult))
                second = kind == "self1" and s == 1
                dst = aob[:, :] if second else ao[:, t, :]
                nc.vector.tensor_tensor(dst.rearrange("p (h e) -> p h e", h=NH), o[:, :, 0:HD],
                                        inv[:, u % 2, :].rearrange("p (h e) -> p h e", e=1).broadcast_to([P, NH, HD]),
                                        ALU.mult).then_inc(sums_read, 1)
                if second:
                    dve.wait_ge(sums_read, i * U + u + 1)
                    nc.vector.tensor_tensor(ao[:, t, :], ao[:, t, :], aob[:, :], ALU.add).then_inc(ao_ready, 1)

            run(dve, front, group, tail)
            dve.wait_ge(x_done, ITER * LT)

        @block.tensor
        def _(pe):
            pe.wait_ge(loaded, NLOAD)
            pe.wait_ge(made, NB * SETS)

            def front(i, k, g):
                values_read = lambda: after(pe, v_ready, i * SETS * KC)
                for s in range(SETS):
                    if g == F_KEYS[s] and cross:
                        values_read()
                        pe.wait_ge(ctx_loaded[k], context_count(i, k))
                        keys(k, s)
                if g == F_TURN:
                    pe.wait_ge(xn_ready, i + 1)
                    if cross:
                        pe.wait_ge(kT_ready, (i + 1) * SETS * DC)
                    else:
                        values_read()
                    for c in range(DC):
                        for t in range(LT):
                            mm = nc.tensor.transpose(ps_f[:, (c * LT + t) * P:(c * LT + t + 1) * P],
                                                     xn[:, t, c * P:(c + 1) * P], ident[:, :])
                    mm.then_inc(turned, 1)
                for s in range(SETS):
                    if g == F_KEYS[s] and not cross:
                        if s == 0:
                            pe.wait_ge(xnT_ready, i + 1)
                        else:
                            pe.wait_ge(kT_ready, i * SETS * DC + s * DC)
                        keys(k, s)
                if g == F_QUERIES:
                    if cross:
                        pe.wait_ge(xnT_ready, i + 1)
                    else:
                        pe.wait_ge(kT_ready, (i + 1) * SETS * DC)
                    for m in range(DC):
                        for c in range(DC):
                            mm = nc.tensor.matmul(ps_f[:, m * LT * P:(m + 1) * LT * P], wq[:, c, m * P:(m + 1) * P],
                                                  xnT[:, c, :], start=(c == 0), stop=(c == DC - 1))
                        mm.then_inc(q_ps, 1)
                for s in range(SETS):
                    if g == F_VALUES[s]:
                        if s == 0:
                            pe.wait_ge(q_ready, (i + 1) * DC)
                        else:
                            pe.wait_ge(v_ready, i * SETS * KC + s * KC)
                        src = ctxT[:, k, :, :] if cross else xnT
                        off = s * P if kind == "batch" else 0
                        for n in range(KC):
                            for c in range(DC):
                                mm = nc.tensor.matmul(ps_f[0:KP, n * D:(n + 1) * D],
                                                      src[:, c, off + n * P:off + n * P + KP],
                                                      wv[s if kind == "self1" else 0][:, c, :],
                                                      start=(c == 0), stop=(c == DC - 1))
                            mm.then_inc(v_ps, 1)

            def keys(k, s):
                src = ctxT[:, k, :, :] if cross else xnT[:, :, :] if kind == "self1" else xnT[:, :, s * P:(s + 1) * P]
                for m in range(DC):
                    for c in range(DC):
                        mm = nc.tensor.matmul(ps_f[:, m * 256:m * 256 + NK],
                                              wk[s if kind == "self1" else 0][:, c, m * P:(m + 1) * P], src[:, c, :],
                                              start=(c == 0), stop=(c == DC - 1))
                    mm.then_inc(k_ps, 1)

            def group(i, k, g):
                if g == 0:
                    pe.wait_ge(kz_ready, (i + 1) * NDMA * 16)
                    pe.wait_ge(q_ready, (i + 1) * DC)
                    pe.wait_ge(v_ready, (i + 1) * SETS * KC)
                t, s = UNITS[g // GU]
                by_vector = has_bias and (kind != "self1" or UNITS[(g - 2) % G // GU][1] == 0)
                after(pe, top_ready if by_vector else prob_ready, i * G + g - 1)
                h0 = (g % GU) * GH
                q = lambda c: qT[k][:, c, t * P:(t + 1) * P]
                if HC >= GH:
                    c, hh = h0 // HC, h0 % HC
                    mm = nc.tensor.matmul(ps_s[g % 2][:, 0:GH * NK], q(c),
                                          kz[s][k][:, c, hh:hh + GH, :].rearrange("p h k -> p (h k)"),
                                          start=True, stop=True)
                else:
                    for c in range(DC):
                        mm = nc.tensor.matmul(ps_s[g % 2][:, c * HC * NK:(c + 1) * HC * NK], q(c),
                                              kz[s][k][:, c, :, :].rearrange("p h k -> p (h k)"),
                                              start=True, stop=True)
                mm.then_inc(scored, 1)

            def tail(i, k, t):
                e = t - LAGT
                if 0 <= e < G:
                    pe.wait_ge(prob_ready, i * G + e + 1)
                    after(pe, pT_odd if e % 2 else pT_even, i * (G // 2) + e // 2)
                    for j in range(4):
                        h, c = j // KC, j % KC
                        mm = nc.tensor.transpose(ps_t[e % 2][0:KP, j * P:(j + 1) * P],
                                                 prob[:, (k * G + e) % NP, h, c * P:c * P + KP], ident[:, :])
                    mm.then_inc(prob_turned, 1)
                e = t - LAGW
                if 0 <= e < G:
                    pe.wait_ge(pT_odd if e % 2 else pT_even, i * (G // 2) + e // 2 + 1)
                    u = e // GU
                    _, s = UNITS[u]
                    if e % GU == 0:
                        after(pe, sums_read, i * U + u - 1)
                    for j in range(4):
                        h, c = (e % GU) * GH + j // KC, j % KC
                        mm = nc.tensor.matmul(ps_o[u % 2][:, h * (HD + 1):(h + 1) * (HD + 1)],
                                              pT[0:KP, e % 2, j, :], V[s][k][0:KP, c, h, :],
                                              start=(c == 0), stop=(c == KC - 1))
                    mm.then_inc(weighed, 1)
                for n, at_end in enumerate(E_TILE):
                    if t == at_end + 1:
                        if kind == "self1":
                            pe.wait_ge(ao_ready, i * LT + n + 1)
                        else:
                            pe.wait_ge(sums_read, i * U + ENDS[n] + 1)
                        after(pe, x_done, i * LT + n)
                        for c in range(DC):
                            mm = nc.tensor.transpose(ps_w[:, c * P:(c + 1) * P],
                                                     ao[:, UNITS[ENDS[n]][0], c * P:(c + 1) * P], ident[:, :])
                        mm.then_inc(ao_turned, 1)
                    if t == at_end + 2:
                        pe.wait_ge(aoT_ready, i * LT + n + 1)
                        for c in range(DC):
                            mm = nc.tensor.matmul(ps_w[:, D:2 * D], aoT[:, c, :], wo[:, c, :],
                                                  start=(c == 0), stop=(c == DC - 1))
                        mm.then_inc(out_ps, 1)

            run(pe, front, group, tail)


def bitffn(nc, A, X, identb):
    LT = 2
    ITER = NT // LT
    HID = 1024
    HCH = HID // P
    ROUND = 12582912.0
    with Stage(nc, "bitffn") as st:
        sb, ps, sem = st.sb, st.ps, st.sem
        w1, w2 = sb("w1", [P, DC, HID]), sb("w2", [P, HCH, D])
        w1q, w2q = sb("w1q", [P, DC, HID], BF16), sb("w2q", [P, HCH, D], BF16)
        b1, b2 = sb("b1", [P, HID]), sb("b2", [P, D])
        ln1_w, ln1_b = sb("ln1_w", [P, D]), sb("ln1_b", [P, D])
        ln2_w, ln2_b = sb("ln2_w", [P, HID]), sb("ln2_b", [P, HID])
        loads = [(w1, "w1"), (w2, "w2"), (b1, "b1"), (b2, "b2"), (ln1_w, "ln1_w"), (ln1_b, "ln1_b"),
                 (ln2_w, "ln2_w"), (ln2_b, "ln2_b")]
        ones = sb("ones", [P, P])
        minus_round = sb("minus_round", [P, 1])
        absum, w_mean, w_scale, w_back = (sb(n, [P, 2]) for n in ("absum", "w_mean", "w_scale", "w_back"))
        pad = sb("pad", [P, 1])
        xt, h = sb("xt", [P, LT, D]), sb("h", [P, LT, D])
        stats, stats2, mv = sb("stats", [P, LT, 6]), sb("stats2", [P, LT, 2, 6]), sb("mv", [P, 2 * LT, 2])
        veps, guess, tmp, rstd = (sb(n, [P, 2 * LT]) for n in ("veps", "guess", "tmp", "rstd"))
        amax, a_scale, f1, f2 = (sb(n, [P, LT]) for n in ("amax", "a_scale", "f1", "f2"))
        q1, q1T = sb("q1", [P, LT, D], BF16), sb("q1T", [P, DC, LT * P], BF16)
        g1 = sb("g1", [P, LT, HID])
        gn = sb("gn", [P, LT, HID])
        q2, q2T = sb("q2", [P, LT, HID], BF16), sb("q2T", [P, LT, HCH, P], BF16)
        ps_h = [ps(f"h{k}", [P, 512]) for k in range(4)]
        ps_q = ps("q", [P, DC, LT * P], BF16)
        ps_q2 = [ps(f"q2{k}", [P, HCH, P], BF16) for k in range(LT)]
        ps_o = ps("o", [P, LT, D])

        loaded, step, const_ready, summed, w_ready = sem("loaded"), sem("dve_step"), sem("const_ready"), sem("summed"), sem("w_ready")
        base_ready = sem("base_ready")
        rstep = sem("dve_root_step")
        xt_ready, fstep, weighted = sem("xt_ready"), sem("dve_front_step"), sem("weighted")
        pool_pad = sb("pool_pad", [P, 1])
        q1_sum, q1_ready, q1_turned, q1T_ready = sem("q1_sum"), sem("q1_ready"), sem("q1_turned"), sem("q1T_ready")
        h_ps, h_ready, g_ready = sem("h_ps"), sem("h_ready"), sem("g_ready")
        gn_ready, scaled, q2_sum, q2_ready = sem("gn_ready"), sem("scaled"), sem("q2_sum"), sem("q2_ready")
        q2_turned, q2T_ready, o_ps, x_done = sem("q2_turned"), sem("q2T_ready"), sem("o_ps"), sem("x_done")
        NLOAD = 16 * len(loads)
        block = st.block()

        @block.sync
        def _(sp):
            for dst, name in loads:
                sp.dma_start(whole(dst), A[f"ff_{name}"]).then_inc(loaded, 16)
            sp.wait_ge(loaded, NLOAD)

        G = 4
        FRONT_STEPS = 2 * 3 * LT + ROOT_STEPS + 2 + 5 + LT
        GROUP_STEPS = LT + 2 + 5 + LT
        over = lambda v: v[:, :].rearrange("p (a d) -> p a d", a=1).broadcast_to([P, LT, v.shape[-1]])

        def run(eng, front, group, tail):
            pipeline(eng, front, group, tail, ITER, G, 2, (0, 1))

        def nothing(i, k, g):
            pass

        @block.gpsimd
        def _(pool):
            nc.gpsimd.memset(ones[:, :], 1.0).then_inc(const_ready, 1)
            nc.gpsimd.memset(minus_round[:, :], -ROUND).then_inc(const_ready, 1)
            pool.wait_ge(loaded, NLOAD)

            def front(i, k, g):
                if g == 1:
                    there = X[:, bass.ds(i * LT, LT), :]
                    pool.wait_ge(xt_ready, i + 1)
                    nc.gpsimd.tensor_tensor(pool_pad[:, :], b2[:, 0:1], b2[:, 0:1], ALU.add)
                    nc.gpsimd.tensor_tensor(there, there, over(b2), ALU.add).then_inc(base_ready, 1)

            def group(i, k, g):
                if g == 1:
                    for t in range(LT):
                        pool.wait_ge(gn_ready, i * LT + t + 1)
                        nc.gpsimd.tensor_tensor(gn[:, t, :], gn[:, t, :], ln2_w[:, :], ALU.mult).then_inc(weighted, 1)
                        if t < LT - 1:
                            pool.wait_ge(weighted, i * LT + t + 1)
                            nc.gpsimd.tensor_tensor(gn[:, t, :], gn[:, t, :], ln2_b[:, :], ALU.add).then_inc(scaled, 1)

            run(pool, front, group, nothing)

        @block.scalar
        def _(act):
            act.wait_ge(const_ready, 2)

            def front(i, k, g):
                if g == 2:
                    act.wait_ge(q1_sum, i + 1)
                    after(act, q1_turned, i)
                    nc.scalar.activation(q1[:, :, :], h[:, :, :], ACT.Identity, bias=minus_round[:, 0:1]).then_inc(q1_ready, 1)
                    act.wait_ge(q1_turned, i + 1)
                    after(act, h_ps, i * LT)
                    nc.scalar.activation(q1T[:, :, :], ps_q[:, :, :], ACT.Identity).then_inc(q1T_ready, 1)

            def group(i, k, g):
                if g == 0:
                    for t in range(LT):
                        act.wait_ge(h_ready, i * LT + t + 1)
                        nc.scalar.activation(g1[:, t, :], g1[:, t, :], ACT.Gelu).then_inc(g_ready, 1)
                if g == 3:
                    for t in range(LT):
                        act.wait_ge(q2_sum, i * LT + t + 1)
                        after(act, q2_turned, (i - 1) * LT + t + 1)
                        nc.scalar.activation(q2[:, t, :], gn[:, t, :], ACT.Identity, bias=minus_round[:, 0:1]).then_inc(q2_ready, 1)
                    for t in range(LT):
                        act.wait_ge(q2_turned, i * LT + t + 1)
                        after(act, o_ps, (i - 1) * LT + t + 1)
                        nc.scalar.activation(q2T[:, t, :, :], ps_q2[t][:, :, :], ACT.Identity).then_inc(q2T_ready, 1)

            run(act, front, group, nothing)

        @block.vector
        def _(dve):
            dve.wait_ge(loaded, NLOAD)
            dve.wait_ge(const_ready, 2)
            ch0 = Chain(dve, step)
            for k, w in enumerate((w1, w2)):
                ch0.link(nc.vector.tensor_reduce(absum[:, k:k + 1], w[:, :, :], AX.XY, ALU.add, apply_absolute_value=True))
            nc.vector.memset(pad[:, :], 0.0).then_inc(summed, 1)
            dve.wait_ge(summed, 2)
            ch0.link(nc.vector.tensor_scalar(w_mean[:, :], ps_o[:, 0, 0:2], 1.0 / (D * HID), EPS, ALU.mult, ALU.max))
            ch0.link(nc.vector.reciprocal(w_scale[:, :], w_mean[:, :]))
            ch0.link(nc.vector.reciprocal(w_back[:, :], w_scale[:, :]))
            for k, (w, q) in enumerate(((w1, w1q), (w2, w2q))):
                ch0.link(nc.vector.tensor_scalar(w[:, :, :], w[:, :, :], w_scale[:, k:k + 1], ROUND, ALU.mult, ALU.add))
                ch0.link(nc.vector.tensor_scalar(w[:, :, :], w[:, :, :], ROUND, -1.0, ALU.subtract, ALU.max))
                nc.vector.tensor_scalar(q[:, :, :], w[:, :, :], 1.0, None, ALU.min).then_inc(w_ready, 1)
            fch = Chain(dve, fstep, per=FRONT_STEPS)
            gch = Chain(dve, step, per=GROUP_STEPS, base=ch0.n)
            rch = Chain(dve, rstep, per=ROOT_STEPS)
            nc.vector.memset(mv[:, 0:LT, :], 1.0)

            def quant_scale(link, src, f, w):
                link(nc.vector.tensor_reduce(amax[:, :], src[:, :, :], AX.X, ALU.max, apply_absolute_value=True))
                link(nc.vector.tensor_scalar(amax[:, :], amax[:, :], EPS, None, ALU.max))
                link(nc.vector.reciprocal(a_scale[:, :], amax[:, :]))
                link(nc.vector.tensor_scalar(a_scale[:, :], a_scale[:, :], 127.0, None, ALU.mult))
                link(nc.vector.tensor_scalar(f[:, :], amax[:, :], w_back[:, w:w + 1], 1.0 / 127.0, ALU.mult, ALU.mult))

            def front(i, k, g):
                if g == 0:
                    fch.start(i)
                    ins = nc.vector.tensor_scalar(xt[:, :, :], X[:, bass.ds(i * LT, LT), :], 1.0, None, ALU.mult)
                    ins.then_inc(xt_ready, 1)
                    dve.wait_ge(xt_ready, i + 1)
                    after(dve, q1_ready, i)
                if g < 2:
                    layer_norm_stats(nc, fch, xt if g == 0 else h, LT, stats, late(mv), pad)
                if g == 0:
                    inverse_root(nc, fch.link, late(mv), LT, late(veps), late(guess), late(tmp), late(rstd))
                    normalize(nc, fch.link, xt, h, LT, late(mv), late(rstd))
                if g == 1 and type(i) is int and i == 0:
                    roots(i)
                    round_input(i)

            def late(v):
                return v[:, LT:2 * LT]

            def roots(i):
                rch.start(i)
                inverse_root(nc, rch.link, mv, 2 * LT, veps, guess, tmp, rstd)

            def round_input(i):
                normalize(nc, fch.link, h, h, LT, late(mv), late(rstd))
                for v, op in ((ln1_w, ALU.mult), (ln1_b, ALU.add)):
                    fch.link(nc.vector.tensor_tensor(h[:, :, :], h[:, :, :], over(v), op))
                quant_scale(fch.link, h, f1, 0)
                for t in range(LT):
                    fch.link(nc.vector.tensor_scalar(h[:, t, :], h[:, t, :], a_scale[:, t:t + 1], 127.0, ALU.mult, ALU.min))
                nc.vector.tensor_scalar(h[:, :, :], h[:, :, :], -128.0, ROUND, ALU.max, ALU.add).then_inc(q1_sum, 1)
                fch.stop()

            def group(i, k, g):
                if g == 0:
                    gch.start(i)
                    after(dve, gn_ready, i * LT)
                    for t in range(LT):
                        dve.wait_ge(h_ps, i * LT + t + 1)
                        for n in range(2):
                            ins = nc.vector.scalar_tensor_tensor(out=g1[:, t, n * 512:(n + 1) * 512],
                                                                 in0=ps_h[2 * t + n][:, :], scalar=f1[:, t:t + 1],
                                                                 in1=b1[:, n * 512:(n + 1) * 512],
                                                                 op0=ALU.mult, op1=ALU.add)
                        ins.then_inc(h_ready, 1)
                if g == 1:
                    for t in range(LT):
                        dve.wait_ge(g_ready, i * LT + t + 1)
                        for n in range(2):
                            ins = nc.vector.bn_stats(stats2[:, t, n, :], g1[:, t, n * 512:(n + 1) * 512])
                        gch.link(ins)
                    nc.vector.memset(pad[:, :], 0.0)
                    for t in range(LT):
                        ins = nc.vector.bn_aggr(mv[:, t, :], stats2[:, t, :, :])
                    gch.link(ins)
                if g == 2:
                    dve.wait_ge(weighted, (i + 1) * LT)
                    gch.link(nc.vector.tensor_tensor(gn[:, LT - 1, :], gn[:, LT - 1, :], ln2_b[:, :], ALU.add))
                    dve.wait_ge(scaled, (i + 1) * (LT - 1))
                    quant_scale(gch.link, gn, f2, 1)
                    for t in range(LT):
                        gch.link(nc.vector.tensor_scalar(gn[:, t, :], gn[:, t, :], a_scale[:, t:t + 1], 127.0, ALU.mult, ALU.min))
                        nc.vector.tensor_scalar(gn[:, t, :], gn[:, t, :], -128.0, ROUND, ALU.max, ALU.add).then_inc(q2_sum, 1)
                    gch.stop()

            def tail(i, k, t):
                if t == 1:
                    roots(i + 1)
                    after(dve, q2_ready, i * LT)
                    for n in range(LT):
                        nc.vector.tensor_scalar(gn[:, n, :], g1[:, n, :], mv[:, n, 0:1], rstd[:, n:n + 1],
                                                ALU.subtract, ALU.mult).then_inc(gn_ready, 1)
                    if not (type(i) is int and i == ITER - 1):
                        round_input(i + 1)
                if t == G + 1:
                    dve.wait_ge(base_ready, i + 1)
                    dve.wait_ge(o_ps, (i + 1) * LT)
                    for n in range(LT):
                        there = X[:, bass.ds(i * LT + n, 1), :]
                        nc.vector.scalar_tensor_tensor(out=there, in0=ps_o[:, n:n + 1, :], scalar=f2[:, n:n + 1],
                                                       in1=there, op0=ALU.mult, op1=ALU.add).then_inc(x_done, 1)

            run(dve, front, group, tail)
            dve.wait_ge(x_done, ITER * LT)

        @block.tensor
        def _(pe):
            pe.wait_ge(summed, 1)
            nc.tensor.matmul(ps_o[:, 0, 0:2], ones[:, :], absum[:, :], start=True, stop=True).then_inc(summed, 1)
            pe.wait_ge(w_ready, 2)

            def front(i, k, g):
                if g == 2:
                    pe.wait_ge(q1_ready, i + 1)
                    after(pe, q1T_ready, i)
                    for c in range(DC):
                        for t in range(LT):
                            mm = nc.tensor.transpose(ps_q[:, c, t * P:(t + 1) * P], q1[:, t, c * P:(c + 1) * P], identb[:, :])
                    mm.then_inc(q1_turned, 1)
                    pe.wait_ge(q1T_ready, i + 1)
                    after(pe, h_ready, i * LT)
                    for t in range(LT):
                        for n in range(2):
                            for c in range(DC):
                                mm = nc.tensor.matmul(ps_h[2 * t + n][:, :], q1T[:, c, t * P:(t + 1) * P],
                                                      w1q[:, c, n * 512:(n + 1) * 512], start=(c == 0), stop=(c == DC - 1))
                        mm.then_inc(h_ps, 1)

            def group(i, k, g):
                if g == 3:
                    for t in range(LT):
                        pe.wait_ge(q2_ready, i * LT + t + 1)
                        after(pe, q2T_ready, (i - 1) * LT + t + 1)
                        for c in range(HCH):
                            mm = nc.tensor.transpose(ps_q2[t][:, c, :], q2[:, t, c * P:(c + 1) * P], identb[:, :])
                        mm.then_inc(q2_turned, 1)

            def tail(i, k, t):
                if t == G:
                    after(pe, x_done, i * LT)
                    for n in range(LT):
                        pe.wait_ge(q2T_ready, i * LT + n + 1)
                        for c in range(HCH):
                            mm = nc.tensor.matmul(ps_o[:, n, :], q2T[:, n, c, :], w2q[:, c, :],
                                                  start=(c == 0), stop=(c == HCH - 1))
                        mm.then_inc(o_ps, 1)

            run(pe, front, group, tail)


def to_positions(nc, X, scratch):
    with Stage(nc, "deal") as st:
        written, read = st.sem("written"), st.sem("read")
        block = st.block()

        @block.sync
        def _(sp):
            sp.dma_start(scratch.rearrange("(n p) d -> p n d", p=P), X[:, :, :]).then_inc(written, 16)
            sp.wait_ge(written, 16)
            for b in range(B):
                sp.dma_start(X[8 * b:8 * b + 8, :, :],
                             scratch[b * S:(b + 1) * S, :].rearrange("(t q) d -> q t d", q=8)).then_inc(read, 16)
            sp.wait_ge(read, 16 * B)


def route(nc, A, ident, Y, ysort, pos, expert, w1):
    LT, E = 4, 8
    ITER = NT // LT
    ROUND = 12582912.0
    with Stage(nc, "route") as st:
        sb, ps, sem = st.sb, st.ps, st.sem
        wg = sb("wg", [P, DC, E])
        g1, be1 = sb("g1", [P, D]), sb("be1", [P, D])
        stats, mv, pad = sb("stats", [P, LT, 6]), sb("mv", [P, LT, 2]), sb("pad", [P, 1])
        veps, guess, tmp, rstd = (sb(n, [P, LT]) for n in ("veps", "guess", "tmp", "rstd"))
        yi = sb("yi", [P, LT, D])
        yb, yT = sb("yb", [P, LT, D]), sb("yT", [P, DC, LT * P])
        logits = sb("logits", [P, NT, E])
        best = sb("best", [P, NT])
        chosen, rank = sb("chosen", [P, NT, E]), sb("rank", [P, NT, E])
        zeros = sb("zeros", [P, SLOTS // 3, D])
        before, ones = sb("before", [P, P]), sb("ones", [P, P])
        descend = sb("descend", [P, E])
        keep = sb("keep", [P, E, NT])
        slot = sb("slot", [P, SLOTS])
        count, upto = sb("count", [P, E, NT]), sb("upto", [P, E, NT])
        tiles, end, base = sb("tiles", [P, E]), sb("end", [P, E]), sb("base", [P, E])
        ended = sb("ended", [P, SLOTS, E - 1])
        posf, expertf = sb("posf", [P, NT]), sb("expertf", [P, SLOTS])
        ps_t = [ps(f"t{k}", [P, LT * P]) for k in range(DC)]
        ps_l = ps("l", [P, LT, E])
        ps_rank, ps_count = ps("rank", [P, NT, E]), ps("count", [P, NT, E])

        loaded, zeroed, cleared, const_ready = sem("loaded"), sem("zeroed"), sem("cleared"), sem("const_ready")
        w1_loaded = sem("w1_loaded")
        yb_ready, turned, yT_ready = sem("yb_ready"), sem("turned"), sem("yT_ready")
        nstep, y_done = sem("norm_step"), sem("y_done")
        logits_ps, logits_ready = sem("logits_ps"), sem("logits_ready")
        step, chosen_ready, counted, pos_ready, scattered = (
            sem("dve_step"), sem("chosen_ready"), sem("counted"), sem("pos_ready"), sem("scattered"))
        block = st.block()

        @block.sync
        def _(sp):
            for dst, name in ((wg, "moe_wg"), (g1, "ba_g1"), (be1, "ba_be1")):
                sp.dma_start(whole(dst), A[name]).then_inc(loaded, 16)
            sp.wait_ge(zeroed, 1)
            for k in range(3):
                sp.dma_start(ysort.rearrange("(s p) d -> p s d", p=P)[:, k * (SLOTS // 3):(k + 1) * (SLOTS // 3), :],
                             zeros[:, :, :]).then_inc(cleared, 16)
            sp.dma_start(whole(w1), A["moe_w1"]).then_inc(w1_loaded, 16)
            sp.wait_ge(loaded, 48)
            sp.wait_ge(cleared, 48)
            sp.wait_ge(w1_loaded, 16)

        @block.gpsimd
        def _(pool):
            nc.gpsimd.memset(zeros[:, :, :], 0.0).then_inc(zeroed, 1)
            nc.gpsimd.memset(before[:, :], 1.0).then_inc(zeroed, 1)
            nc.gpsimd.memset(ones[:, :], 1.0).then_inc(zeroed, 1)
            nc.gpsimd.memset(keep[:, :, :], 1.0).then_inc(zeroed, 1)
            pool.wait_ge(zeroed, 4)
            nc.gpsimd.affine_select(out=before[:, :], in_=before[:, :], compare_op=ALU.is_ge, fill=0.0,
                                    base=-1, pattern=[[1, P]], channel_multiplier=-1).then_inc(const_ready, 1)
            nc.gpsimd.affine_select(out=keep[:, :, :], in_=keep[:, :, :], compare_op=ALU.is_ge, fill=0.0,
                                    base=-1, pattern=[[0, E], [1, NT]], channel_multiplier=0).then_inc(const_ready, 1)
            nc.gpsimd.iota(slot[:, :], [[1, SLOTS]], base=0, channel_multiplier=0,
                           allow_small_or_imprecise_dtypes=True).then_inc(const_ready, 1)
            nc.gpsimd.iota(descend[:, :], [[-1, E]], base=E, channel_multiplier=0,
                           allow_small_or_imprecise_dtypes=True).then_inc(const_ready, 1)
            pool.wait_ge(cleared, 48)
            pool.wait_ge(pos_ready, 1)
            for t in range(NT):
                nc.gpsimd.indirect_dma_start(
                    ysort, bass.IndirectOffsetOnAxis(ap=pos[:, t:t + 1], axis=0), Y[:, t, :], None).then_inc(scattered, 16)
            pool.wait_ge(scattered, 16 * NT)

        @block.scalar
        def _(act):
            with act.Fori(0, ITER) as i:
                for c in range(DC):
                    act.wait_ge(turned, i * DC + c + 1)
                    nc.scalar.activation(yT[:, c, :], ps_t[c][:, :], ACT.Identity).then_inc(yT_ready, 1)

        @block.tensor
        def _(pe):
            pe.wait_ge(loaded, 48)
            with pe.Fori(0, ITER) as i:
                pe.wait_ge(yb_ready, i + 1)
                for c in range(DC):
                    for t in range(LT):
                        mm = nc.tensor.transpose(ps_t[c][:, t * P:(t + 1) * P], yb[:, t, c * P:(c + 1) * P], ident[:, :])
                    mm.then_inc(turned, 1)
                pe.wait_ge(yT_ready, (i + 1) * DC)
                for t in range(LT):
                    for c in range(DC):
                        mm = nc.tensor.matmul(ps_l[:, t, :], yT[:, c, t * P:(t + 1) * P], wg[:, c, :],
                                              start=(c == 0), stop=(c == DC - 1))
                mm.then_inc(logits_ps, 1)
            pe.wait_ge(chosen_ready, 1)
            pe.wait_ge(const_ready, 4)
            flat = lambda v: v[:, :, :].rearrange("p t e -> p (t e)")
            nc.tensor.matmul(flat(ps_rank), before[:, :], flat(chosen), start=True, stop=True).then_inc(counted, 1)
            nc.tensor.matmul(flat(ps_count), ones[:, :], flat(chosen), start=True, stop=True).then_inc(counted, 1)

        @block.vector
        def _(dve):
            dve.wait_ge(loaded, 48)
            ch = Chain(dve, nstep, per=1 + 3 * LT + ROOT_STEPS + 1)
            over = lambda v: v[:, :].rearrange("p (a d) -> p a d", a=1).broadcast_to([P, LT, D])
            with dve.Fori(0, ITER) as i:
                ch.start(i)
                ch.link(nc.vector.tensor_scalar(yi[:, :, :], Y[:, bass.ds(i * LT, LT), :], 1.0, None, ALU.mult))
                layer_norm_stats(nc, ch, yi, LT, stats, mv, pad)
                inverse_root(nc, ch.link, mv, LT, veps, guess, tmp, rstd)
                for t in range(LT):
                    (ch.mark if t < LT - 1 else ch.link)(nc.vector.tensor_scalar(
                        yi[:, t, :], yi[:, t, :], mv[:, t, 0:1], rstd[:, t:t + 1], ALU.subtract, ALU.mult))
                ch.link(nc.vector.tensor_tensor(yi[:, :, :], yi[:, :, :], over(g1), ALU.mult))
                ch.stop()
                nc.vector.tensor_tensor(yb[:, :, :], yi[:, :, :], over(be1), ALU.add).then_inc(yb_ready, 1)
                dve.wait_ge(yb_ready, i + 1)
                nc.vector.tensor_scalar(Y[:, bass.ds(i * LT, LT), :], yb[:, :, :], 1.0, None, ALU.mult).then_inc(y_done, 1)
                dve.wait_ge(y_done, i + 1)
                dve.wait_ge(logits_ps, i + 1)
                nc.vector.tensor_scalar(logits[:, bass.ds(i * LT, LT), :], ps_l[:, :, :], 1.0, None,
                                        ALU.mult).then_inc(logits_ready, 1)
                dve.wait_ge(logits_ready, i + 1)
            dve.wait_ge(const_ready, 4)
            link = Chain(dve, step).link
            over_e = lambda v: v[:, :].rearrange("p (t e) -> p t e", e=1).broadcast_to([P, NT, E])
            by_e = lambda v, n: v.rearrange("p (a e) -> p a e", a=1).broadcast_to([P, n, v.shape[-1]])
            tile_major = lambda v: v[:, :, :].rearrange("p e t -> p t e")
            link(nc.vector.tensor_reduce(best[:, :], logits[:, :, :], AX.X, ALU.max))
            link(nc.vector.tensor_tensor(chosen[:, :, :], logits[:, :, :], over_e(best), ALU.is_equal))
            link(nc.vector.tensor_tensor(rank[:, :, :], chosen[:, :, :], by_e(descend[:, :], NT), ALU.mult))
            link(nc.vector.tensor_reduce(best[:, :], rank[:, :, :], AX.X, ALU.max))
            nc.vector.tensor_tensor(chosen[:, :, :], rank[:, :, :], over_e(best), ALU.is_equal).then_inc(chosen_ready, 1)
            dve.wait_ge(counted, 2)
            link(nc.vector.tensor_copy(tile_major(count), ps_count[:, :, :]))
            link(nc.vector.tensor_tensor_scan(upto[:, :, :].rearrange("p e t -> p (e t)"),
                                              keep[:, :, :].rearrange("p e t -> p (e t)"),
                                              count[:, :, :].rearrange("p e t -> p (e t)"), 0.0, ALU.mult, ALU.add))
            link(nc.vector.tensor_scalar(tiles[:, :], upto[:, :, NT - 1], 1.0 / P, (P - 1) / (2.0 * P), ALU.mult, ALU.add))
            link(nc.vector.tensor_scalar(tiles[:, :], tiles[:, :], ROUND, None, ALU.add))
            link(nc.vector.tensor_scalar(tiles[:, :], tiles[:, :], ROUND, None, ALU.subtract))
            link(nc.vector.tensor_tensor_scan(end[:, :], ones[:, 0:E], tiles[:, :], 0.0, ALU.mult, ALU.add))
            link(nc.vector.tensor_tensor(base[:, :], end[:, :], tiles[:, :], ALU.subtract))
            link(nc.vector.tensor_scalar(base[:, :], base[:, :], float(P), None, ALU.mult))
            link(nc.vector.tensor_tensor(upto[:, :, :], upto[:, :, :], count[:, :, :], ALU.subtract))
            link(nc.vector.tensor_tensor(rank[:, :, :], ps_rank[:, :, :], tile_major(upto), ALU.add))
            link(nc.vector.tensor_tensor(rank[:, :, :], rank[:, :, :], by_e(base[:, :], NT), ALU.add))
            link(nc.vector.tensor_tensor(rank[:, :, :], rank[:, :, :], chosen[:, :, :], ALU.mult))
            link(nc.vector.tensor_reduce(posf[:, :], rank[:, :, :], AX.X, ALU.add))
            nc.vector.tensor_copy(pos[:, :], posf[:, :]).then_inc(pos_ready, 1)
            link(nc.vector.tensor_tensor(ended[:, :, :],
                                         slot[:, :].rearrange("p (s e) -> p s e", e=1).broadcast_to([P, SLOTS, E - 1]),
                                         by_e(end[:, 0:E - 1], SLOTS), ALU.is_ge))
            link(nc.vector.tensor_reduce(expertf[:, :], ended[:, :, :], AX.X, ALU.add))
            link(nc.vector.tensor_copy(expert[:, :], expertf[:, :]))


def moe(nc, A, X, ident, ysort, zsort, pos, expert, w1):
    E, DF = 8, 1024
    FC, HALF = DF // P, DF // 2
    with Stage(nc, "experts") as st:
        sb, ps, sem = st.sb, st.ps, st.sem
        w2 = sb("w2", [P, E, FC, D])
        b1, b2 = sb("b1", [P, E, FC]), sb("b2", [P, E, D])
        b1_slot = sb("b1_slot", [P, 1, FC])
        g2, be2 = sb("g2", [P, D]), sb("be2", [P, D])
        y, yT = sb("y", [P, 2, D]), sb("yT", [P, D])
        h, hT = sb("h", [P, DF]), sb("hT", [P, DF])
        base, z = sb("base", [P, 2, D]), sb("z", [P, D])
        zout = sb("zout", [P, 2, D])
        gather = [sb(f"gather{k}", [P, D]) for k in range(4)]
        stats, mv = sb("stats", [P, 1, 6]), sb("mv", [P, 1, 2])
        veps, guess, tmp, rstd, pad = (sb(n, [P, 1]) for n in ("veps", "guess", "tmp", "rstd", "pad"))
        ps_h = [ps(f"h{k}", [P, HALF]) for k in range(2)]
        ps_hT = [ps(f"hT{k}", [P, HALF]) for k in range(2)]
        ps_y, ps_z = ps("y", [P, D]), ps("z", [P, D])

        loaded, w2_loaded = sem("loaded"), sem("w2_loaded")
        y_loaded = [sem(f"y_loaded{k}") for k in range(2)]
        y_turned, yT_ready, base_ready = sem("y_turned"), sem("yT_ready"), sem("base_ready")
        h_ps, h_ready, h_turned, hT_ready = sem("h_ps"), sem("h_ready"), sem("h_turned"), sem("hT_ready")
        z_ps, step = sem("z_ps"), sem("dve_step")
        normed, scaled, zout_ready = sem("normed"), sem("scaled"), sem("zout_ready")
        stored = [sem(f"stored{k}") for k in range(2)]
        x_done, z_taken = sem("x_done"), sem("z_taken")
        GB = 4
        gathered = [sem(f"gathered{k}") for k in range(GB)]
        loads = [(b1, "b1"), (b2, "b2"), (g2, "g2"), (be2, "be2")]
        NLOAD = 16 * len(loads)
        block = st.block()

        PAIRS = (SLOTS - 3) // 2

        def pairs(eng, body):
            with eng.Fori(0, PAIRS) as jj:
                for k in range(2):
                    body(jj * 2 + k + 2, k, jj + 2)

        @block.sync
        def _(sp):
            for dst, name in loads:
                sp.dma_start(whole(dst), A[f"moe_{name}"]).then_inc(loaded, 16)
            fetch = lambda j, k: sp.dma_start(y[:, k, :], ysort[bass.ds(j * P, P), :]).then_inc(y_loaded[k], 16)
            fetch(0, 0)
            fetch(1, 1)
            sp.dma_start(whole(w2), A["moe_w2"]).then_inc(w2_loaded, 16)
            sp.wait_ge(loaded, NLOAD)

            def refetch(j, k):
                sp.wait_ge(y_turned, j + 1)
                sp.wait_ge(base_ready, j + 1)
                fetch(j + 2, k)

            def keep(j, k):
                sp.wait_ge(zout_ready, j + 1)
                sp.dma_start(zsort[bass.ds(j * P, P), :], zout[:, k, :]).then_inc(stored[k], 16)

            refetch(0, 0)
            with sp.Fori(0, PAIRS) as jj:
                for k in range(2):
                    refetch(jj * 2 + k + 1, 1 - k)
                    keep(jj * 2 + k, k)
            for j in range(SLOTS - 3, SLOTS):
                keep(j, j % 2)
            for k in range(2):
                sp.wait_ge(stored[k], 16 * ((SLOTS + 1 - k) // 2))

        @block.gpsimd
        def _(pool):
            pool.wait_ge(loaded, NLOAD)

            def start(j, k, n):
                e = pool.value_load(expert[0:1, bass.ds(j, 1)], min_val=0, max_val=E - 1)
                pool.wait_ge(y_loaded[k], n * 16)
                nc.gpsimd.tensor_tensor(base[:, k, :].rearrange("p (a d) -> p a d", a=1),
                                        y[:, k, :].rearrange("p (a d) -> p a d", a=1),
                                        b2[:, bass.ds(e, 1), :], ALU.add).then_inc(base_ready, 1)

            def weigh(j, k, n):
                pool.wait_ge(normed, j + 1)
                nc.gpsimd.tensor_tensor(z[:, :], z[:, :], g2[:, :], ALU.mult).then_inc(scaled, 1)
                pool.wait_ge(scaled, j + 1)
                if type(j) is not int:
                    pool.wait_ge(stored[k], (n - 1) * 16)
                elif j >= 2:
                    pool.wait_ge(stored[k], j // 2 * 16)
                nc.gpsimd.tensor_tensor(zout[:, k, :], z[:, :], be2[:, :], ALU.add).then_inc(zout_ready, 1)

            def body(j, k, n):
                start(j + 1, 1 - k, n + k)
                weigh(j, k, n)

            start(0, 0, 1)
            body(0, 0, 1)
            body(1, 1, 1)
            pairs(pool, body)
            weigh(SLOTS - 1, 0, SLOTS // 2 + 1)
            for k in range(2):
                pool.wait_ge(stored[k], 16 * ((SLOTS + 1 - k) // 2))
            for t in range(NT):
                if t >= GB:
                    pool.wait_ge(x_done, t - GB + 1)
                nc.gpsimd.indirect_dma_start(
                    gather[t % GB][:, :], None, zsort,
                    bass.IndirectOffsetOnAxis(ap=pos[:, t:t + 1], axis=0)).then_inc(gathered[t % GB], 16)

        @block.scalar
        def _(act):
            def turn(j):
                act.wait_ge(y_turned, j + 1)
                nc.scalar.activation(yT[:, :], ps_y[:, :], ACT.Identity).then_inc(yT_ready, 1)

            def relu(j):
                for k in range(2):
                    act.wait_ge(h_turned, j * 2 + k + 1)
                    for c in range(k * FC // 2, (k + 1) * FC // 2):
                        ins = nc.scalar.activation(hT[:, c * P:(c + 1) * P], ps_hT[k][:, c * P - k * HALF:(c + 1) * P - k * HALF],
                                                   ACT.Relu, bias=b1_slot[:, 0, c:c + 1])
                    ins.then_inc(hT_ready, 1)

            turn(0)
            turn(1)
            relu(0)
            with act.Fori(1, SLOTS - 1) as j:
                turn(j + 1)
                relu(j)
            relu(SLOTS - 1)

        @block.vector
        def _(dve):
            dve.wait_ge(loaded, NLOAD)

            def hidden(j):
                e = dve.value_load(expert[0:1, bass.ds(j, 1)], min_val=0, max_val=E - 1)
                if type(j) is not int or j:
                    dve.wait_ge(hT_ready, j * 2)
                nc.vector.tensor_scalar(b1_slot[:, :, :], b1[:, bass.ds(e, 1), :], 1.0, None, ALU.mult)
                for k in range(2):
                    dve.wait_ge(h_ps, j * 2 + k + 1)
                    nc.vector.tensor_copy(h[:, k * HALF:(k + 1) * HALF], ps_h[k][:, :]).then_inc(h_ready, 1)

            ch = Chain(dve, step, per=2 + ROOT_STEPS)

            def finish(j, k):
                ch.start(j)
                dve.wait_ge(z_ps, j + 1)
                dve.wait_ge(base_ready, j + 1)
                if type(j) is not int or j:
                    dve.wait_ge(zout_ready, j)
                nc.vector.tensor_tensor(z[:, :], ps_z[:, :], base[:, k, :], ALU.add).then_inc(z_taken, 1)
                dve.wait_ge(z_taken, j + 1)
                layer_norm_stats(nc, ch, z[:, :].rearrange("p (a d) -> p a d", a=1), 1, stats, mv, pad)
                inverse_root(nc, ch.link, mv, 1, veps, guess, tmp, rstd)
                nc.vector.tensor_scalar(z[:, :], z[:, :], mv[:, 0, 0:1], rstd[:, 0:1],
                                        ALU.subtract, ALU.mult).then_inc(normed, 1)
                ch.stop()

            hidden(0)
            for j in range(2):
                hidden(j + 1)
                finish(j, j)
            pairs(dve, lambda j, k, n: (hidden(j + 1), finish(j, k)))
            finish(SLOTS - 1, 0)
            for t in range(NT):
                dve.wait_ge(gathered[t % GB], 16 * (t // GB + 1))
                nc.vector.tensor_tensor(X[:, t, :], X[:, t, :], gather[t % GB][:, :], ALU.add).then_inc(x_done, 1)
            dve.wait_ge(x_done, NT)

        @block.tensor
        def _(pe):

            def turn_y(j, k, n):
                pe.wait_ge(y_loaded[k], n * 16)
                if type(j) is not int or j:
                    pe.wait_ge(yT_ready, j)
                for c in range(DC):
                    mm = nc.tensor.transpose(ps_y[:, c * P:(c + 1) * P], y[:, k, c * P:(c + 1) * P], ident[:, :])
                mm.then_inc(y_turned, 1)

            def up(j):
                e = pe.value_load(expert[0:1, bass.ds(j, 1)], min_val=0, max_val=E - 1)
                pe.wait_ge(yT_ready, j + 1)
                for k in range(2):
                    if type(j) is not int or j:
                        pe.wait_ge(h_ready, j * 2 - 1 + k)
                    for c in range(DC):
                        mm = nc.tensor.matmul(ps_h[k][:, :], yT[:, c * P:(c + 1) * P],
                                              w1[:, bass.ds(e, 1), c, k * HALF:(k + 1) * HALF].rearrange("p a d -> p (a d)"),
                                              start=(c == 0), stop=(c == DC - 1))
                    mm.then_inc(h_ps, 1)

            def turn_h(j):
                for k in range(2):
                    pe.wait_ge(h_ready, j * 2 + k + 1)
                    if type(j) is not int or j:
                        pe.wait_ge(hT_ready, j * 2 - 1 + k)
                    for c in range(4):
                        mm = nc.tensor.transpose(ps_hT[k][:, c * P:(c + 1) * P],
                                                 h[:, k * HALF + c * P:k * HALF + (c + 1) * P], ident[:, :])
                    mm.then_inc(h_turned, 1)

            def down(j):
                e = pe.value_load(expert[0:1, bass.ds(j, 1)], min_val=0, max_val=E - 1)
                for k in range(2):
                    pe.wait_ge(hT_ready, j * 2 + k + 1)
                if type(j) is not int or j:
                    pe.wait_ge(z_taken, j)
                for c in range(FC):
                    mm = nc.tensor.matmul(ps_z[:, :], hT[:, c * P:(c + 1) * P],
                                          w2[:, bass.ds(e, 1), c, :].rearrange("p a d -> p (a d)"),
                                          start=(c == 0), stop=(c == FC - 1))
                mm.then_inc(z_ps, 1)

            def body(j, k, n):
                up(j)
                turn_y(j + 1, (k + 1) % 2, n + k)
                down(j - 1)
                turn_h(j)

            turn_y(0, 0, 1)
            up(0)
            turn_y(1, 1, 1)
            turn_h(0)
            pe.wait_ge(w2_loaded, 16)
            body(1, 1, 1)
            pairs(pe, body)
            up(SLOTS - 1)
            down(SLOTS - 2)
            turn_h(SLOTS - 1)
            down(SLOTS - 1)


def store(nc, X, out, dealt):
    with Stage(nc, "store") as st:
        stored = st.sem("stored")
        block = st.block()

        @block.sync
        def _(sp):
            if dealt:
                for b in range(B):
                    sp.dma_start(out[b * S:(b + 1) * S, :].rearrange("(t q) d -> q t d", q=8),
                                 X[8 * b:8 * b + 8, :, :]).then_inc(stored, 16)
                sp.wait_ge(stored, 16 * B)
            else:
                sp.dma_start(out.rearrange("(n p) d -> p n d", p=P), X[:, :, :]).then_inc(stored, 16)
                sp.wait_ge(stored, 16)


STAGES = ("mamba", "cross0", "bitffn", "self1", "cross1", "moe")


def program(nc, A, out, stages=STAGES):
    with ExitStack() as ctx:
        X = ctx.enter_context(nc.sbuf_tensor("X", [P, NT, D], F32))
        ident = ctx.enter_context(nc.sbuf_tensor("ident", [P, P], F32))
        identb = ctx.enter_context(nc.sbuf_tensor("identb", [P, P], BF16))
        Stage.used.clear()
        setup(nc, A, X, ident, identb)
        for kind in stages:
            if len(Stage.used) > 60:
                clear_semaphores(nc)
            if kind == "mamba":
                mamba(nc, A, X, ident, identb)
            elif kind == "bitffn":
                bitffn(nc, A, X, identb)
            elif kind == "moe":
                scratch = nc.dram_tensor("scratch", (B * S, D), F32).ap()
                ysort = nc.dram_tensor("ysort", (SLOTS * P, D), F32).ap()
                zsort = nc.dram_tensor("zsort", (SLOTS * P, D), F32).ap()
                to_positions(nc, X, scratch)
                clear_semaphores(nc)
                pos = ctx.enter_context(nc.sbuf_tensor("pos", [P, NT], I32))
                expert = ctx.enter_context(nc.sbuf_tensor("expert", [P, SLOTS], I32))
                w1 = ctx.enter_context(nc.sbuf_tensor("w1", [P, 8, DC, 1024], F32))
                with nc.sbuf_tensor("Y", [P, NT, D], F32) as Y:
                    attention(nc, A, X, ident, "batch", Y)
                    route(nc, A, ident, Y, ysort, pos, expert, w1)
                clear_semaphores(nc)
                moe(nc, A, X, ident, ysort, zsort, pos, expert, w1)
            else:
                attention(nc, A, X, ident, kind)
        store(nc, X, out, "moe" in stages)


def layout(inputs):
    import numpy as np

    a = {k: np.asarray(v) for k, v in inputs.items()}

    def rows(w):
        return np.ascontiguousarray(w.reshape(-1, P, w.shape[-1]).transpose(1, 0, 2))

    def cols(v):
        return np.ascontiguousarray(v.reshape(-1, P).T)

    def spread(v):
        return np.ascontiguousarray(np.broadcast_to(v.reshape(1, -1), (P, v.size)))

    def heads_last(w):
        return w.transpose(1, 0, 2).reshape(D, -1)

    o = {"x": a["x"].reshape(B * S, D)}
    w = {k[8:]: v for k, v in a.items() if k.startswith("L0_attn_")}
    xp = w["xp_w"].T
    o |= {
        "mb_in_w": rows(w["in_w"].T), "mb_out_w": rows(w["out_w"].T), "mb_xp_dt": rows(xp[:, :64]),
        "mb_xp_bc": rows(np.concatenate([xp[:, 64:]] * 3, axis=1)), "mb_dtp_w": np.ascontiguousarray(w["dtp_w"].T),
        "mb_ln_w": cols(w["ln_w"]), "mb_ln_b": cols(w["ln_b"]), "mb_in_b": cols(w["in_b"]),
        "mb_conv_w": rows(w["conv_w"][:, 0, :]), "mb_conv_b": cols(w["conv_b"]), "mb_dtp_b": cols(w["dtp_b"]),
        "mb_D": cols(w["D"]), "mb_A_log": rows(w["A_log"]), "mb_out_b": spread(w["out_b"]),
    }
    o["ctxT"] = rows(a["ctx_1024"].reshape(-1, D).T)
    o["c0_mask"] = np.ascontiguousarray(
        a["mask_Bx1xSxS2_bk0"].reshape(NT, P, -1).transpose(1, 0, 2))
    for pre, name, fix in (("c0", "L0_xattn", lambda m: m), ("c1", "L1_xattn", heads_last)):
        for k in "qkv":
            o[f"{pre}_w{k}" + ("" if k == "q" else "0")] = rows(fix(a[f"{name}_{'w' if pre == 'c0' else 'W'}{k}"]))
            v = a[f"{name}_b{k}"].reshape(-1)
            o[f"{pre}_b{k}"] = spread(v) if k == "v" else cols(v)
        o[f"{pre}_wo"] = rows(a[f"{name}_{'w' if pre == 'c0' else 'W'}o"])
        o[f"{pre}_bo"] = spread(a[f"{name}_bo"])
    o |= {"sa_wq": rows(a["L1_attn_Wq"]), "sa_wo": rows(a["L1_attn_Wo"])}
    for s, name in enumerate(("L1_attn_Wkv_short", "L1_attn_Wkv_long")):
        o |= {f"sa_wk{s}": rows(a[name][:, :D]), f"sa_wv{s}": rows(a[name][:, D:])}
    o["sa_mix"] = spread(np.stack([a["L1_attn_mix_weight"], a["L1_attn_decay_factor"]]))
    f = {k[7:]: v for k, v in a.items() if k.startswith("L0_ffn_")}
    o |= {"ff_w1": rows(f["w1"].T), "ff_w2": rows(f["w2"].T)}
    o |= {f"ff_{k}": spread(f[k]) for k in ("b1", "b2", "ln1_w", "ln1_b", "ln2_w", "ln2_b")}
    wqkv = a["L1_ffn_Wqkv"].T
    for k, name in enumerate(("wq", "wk0", "wv0")):
        o[f"ba_{name}"] = rows(wqkv[:, k * D:(k + 1) * D])
    bqkv = a["L1_ffn_bqkv"]
    o |= {"ba_bq": cols(bqkv[:D]), "ba_bk": cols(bqkv[D:2 * D]), "ba_bv": spread(bqkv[2 * D:]),
          "ba_wo": rows(a["L1_ffn_Wo"].T), "ba_bo": spread(a["L1_ffn_bo"]),
          "ba_g1": spread(a["L1_ffn_g1"]), "ba_be1": spread(a["L1_ffn_be1"]),
          "ba_mod8": (np.arange(P) % 8).astype(np.float32).reshape(P, 1)}
    m = {k[7:]: v for k, v in a.items() if k.startswith("L1_ffn_")}
    E = m["Wg"].shape[0]

    def per_expert(w):
        return np.ascontiguousarray(w.reshape(E, -1, P, w.shape[-1]).transpose(2, 0, 1, 3))

    def spread_all(v):
        return np.ascontiguousarray(np.broadcast_to(v[None], (P,) + v.shape))

    o |= {"moe_wg": rows(m["Wg"].T), "moe_w1": per_expert(m["W1"]), "moe_w2": per_expert(m["W2"]),
          "moe_b1": np.ascontiguousarray(m["b1"].reshape(E, -1, P).transpose(2, 0, 1)), "moe_b2": spread_all(m["b2"]),
          "moe_g2": spread(m["g2"]), "moe_be2": spread(m["be2"])}
    return o


def kernel(**inputs):
    import concourse.bacc as _bacc
    from concourse.bass_utils import run_bass_kernel_spmd as _run

    nc = _bacc.Bacc("TRN2", target_bir_lowering=False, num_devices=1)
    arrays, A = {}, {}
    for name, v in layout(inputs).items():
        arrays[f"in_{name}_dram"] = v
        A[name] = nc.dram_tensor(f"in_{name}_dram", v.shape, mybir.dt.from_np(v.dtype), kind="ExternalInput").ap()
    out = nc.dram_tensor("out_0_dram", (B * S, D), F32, kind="ExternalOutput").ap()
    program(nc, A, out)
    r = _run(nc, [arrays], core_ids=[0])
    return r.results[0]["out_0_dram"].reshape(B, S, D)
```
